# Optimizing a Trainium2 kernel written in Bass

```python
import numpy as np
import jax
import jax.numpy as jnp

def _softmax(x, axis=-1):
    return jax.nn.softmax(x, axis=axis)

def _gelu(x):
    return jax.nn.gelu(x, approximate=True)

def _silu(x):
    return jax.nn.silu(x)

def _sigmoid(x):
    return jax.nn.sigmoid(x)

def _layernorm(x, axis=-1, eps=1e-05):
    m = jnp.mean(x, axis=axis, keepdims=True)
    v = jnp.var(x, axis=axis, keepdims=True)
    return (x - m) / jnp.sqrt(v + eps)

def _scatter_add(tgt, idx, src, axis=0):
    return tgt.at[idx].add(src)

def _segment_sum(src, seg, n):
    return jax.ops.segment_sum(src, seg, n)
kernel_name = 'mk_xattn_ffn_d2_seqx_r4_bf054f'

def setup_inputs(seed: int=0):
    np.random.seed(seed)
    _w = jnp.asarray

    def _rec_inputs():
        import jax
        import jax.numpy as jnp
        _rk = jax.random.key(seed)
        x = 7.22e-05 + 1 * jax.random.normal(jax.random.fold_in(_rk, 1), (8, 512, 256), jnp.float32)
        _lenS = 512 - jax.random.randint(jax.random.fold_in(_rk, 7), (8,), 0, max(1, 512 // 4) + 1, jnp.int32)
        _lenS2 = 512 - jax.random.randint(jax.random.fold_in(_rk, 8), (8,), 0, max(1, 512 // 4) + 1, jnp.int32)
        _ctx_1024P = jax.random.normal(jax.random.fold_in(_rk, 11), (8, 16, 256), jnp.float32)
        _ctx_1024c = jax.random.dirichlet(jax.random.fold_in(_rk, 511), 0.3 * jnp.ones((16,), jnp.float32), (8, 512))
        _ctx_1024t = jnp.einsum('bsk,bkd->bsd', _ctx_1024c, _ctx_1024P)
        _ctx_1024t = _ctx_1024t * jax.lax.rsqrt(jnp.mean(jnp.square(_ctx_1024t)) + 1e-12) * 0.953939
        ctx_1024 = 4.13588e-05 + 0.999923 * (_ctx_1024t + 0.3 * jax.random.normal(jax.random.fold_in(_rk, 611), (8, 512, 256), jnp.float32))
        _validS = jnp.arange(512)[None, :] < _lenS[:, None]
        _validS2 = jnp.arange(512)[None, :] < _lenS2[:, None]
        _causal = jnp.tril(jnp.ones((512, 512), dtype=bool))
        mask_SxS2_bk0 = jnp.logical_not(jnp.broadcast_to(_validS2[0:1, :], (512, 512)))
        return (x, ctx_1024, mask_SxS2_bk0)
    x, ctx_1024, mask_SxS2_bk0 = _rec_inputs()

    def _L0_xattn_setup():
        import jax, jax.numpy as jnp
        import numpy as np
        B, T, D_MODEL, D_HIDDEN, MAX_SEQLEN = (4, 512, 256, 256, 512)
        key = jax.random.key(seed)
        ks = jax.random.split(key, 8)
        scale = 0.02
        return {'q': jax.random.normal(ks[0], (B, T, D_MODEL), dtype=jnp.float32), 'k': jax.random.normal(ks[1], (B, T, D_MODEL), dtype=jnp.float32), 'v': jax.random.normal(ks[2], (B, T, D_MODEL), dtype=jnp.float32), 'Wq': jax.random.normal(ks[3], (D_HIDDEN, D_MODEL), dtype=jnp.float32) * scale, 'Wk': jax.random.normal(ks[4], (D_HIDDEN, D_MODEL), dtype=jnp.float32) * scale, 'Wv': jax.random.normal(ks[5], (D_HIDDEN, D_MODEL), dtype=jnp.float32) * scale, 'Wo': jax.random.normal(ks[6], (D_MODEL, D_HIDDEN), dtype=jnp.float32) * scale, 'W_bias': jax.random.normal(ks[7], (MAX_SEQLEN, MAX_SEQLEN), dtype=jnp.float32) * scale}
    _L0_xattn_all = _L0_xattn_setup()
    _L0_xattn_in = {k: v for k, v in _L0_xattn_all.items() if k in ('Wq', 'Wk', 'Wv', 'Wo', 'W_bias')}
    del _L0_xattn_all

    def _L0_ffn_setup():
        import jax, jax.numpy as jnp
        import numpy as np
        CAPACITY_FACTOR = 1.0
        key = jax.random.key(seed)
        ks = jax.random.split(key, 5)
        B, S, D, E, F = (2, 512, 256, 8, 1024)
        x = jax.random.normal(ks[0], (B, S, D), dtype=jnp.float32)
        Ws = jax.random.normal(ks[1], (D, E), dtype=jnp.float32) * (1.0 / np.sqrt(D))
        bs = jnp.zeros((E,), dtype=jnp.float32)
        W1 = jax.random.normal(ks[2], (E, D, F), dtype=jnp.float32) * (1.0 / np.sqrt(D))
        b1 = jnp.zeros((E, F), dtype=jnp.float32)
        W2 = jax.random.normal(ks[3], (E, F, D), dtype=jnp.float32) * (1.0 / np.sqrt(F))
        b2 = jnp.zeros((E, D), dtype=jnp.float32)
        return {'x': x, 'Ws': Ws, 'bs': bs, 'W1': W1, 'b1': b1, 'W2': W2, 'b2': b2}
    _L0_ffn_all = _L0_ffn_setup()
    _L0_ffn_in = {k: v for k, v in _L0_ffn_all.items() if k in ('Ws', 'bs', 'W1', 'b1', 'W2', 'b2')}
    del _L0_ffn_all

    def _L1_xattn_setup():
        import jax, jax.numpy as jnp
        import numpy as np
        B, S, DIM, H = (4, 512, 256, 16)
        HD = DIM // H
        SCALE = HD ** (-0.5)

        def _heads(x):
            b, s, _ = x.shape
            return x.reshape(b, s, H, HD).transpose(0, 2, 1, 3)
        key = jax.random.key(seed)
        ks = jax.random.split(key, 7)
        init = 0.02
        return {'query': jax.random.normal(ks[0], (B, S, DIM), dtype=jnp.float32), 'key': jax.random.normal(ks[1], (B, S, DIM), dtype=jnp.float32), 'value': jax.random.normal(ks[2], (B, S, DIM), dtype=jnp.float32), 'attn_mask': jnp.tril(jnp.ones((S, S), dtype=bool)), 'Wq': jax.random.normal(ks[3], (DIM, DIM), dtype=jnp.float32) * init, 'Wk': jax.random.normal(ks[4], (DIM, DIM), dtype=jnp.float32) * init, 'Wv': jax.random.normal(ks[5], (DIM, DIM), dtype=jnp.float32) * init, 'Wo': jax.random.normal(ks[6], (DIM, DIM), dtype=jnp.float32) * init}
    _L1_xattn_all = _L1_xattn_setup()
    _L1_xattn_in = {k: v for k, v in _L1_xattn_all.items() if k in ('Wq', 'Wk', 'Wv', 'Wo')}
    del _L1_xattn_all

    def _L1_ffn_setup():
        import jax, jax.numpy as jnp
        import numpy as np
        import math
        B, S, D = (4, 512, 256)
        H = 16
        E = 8
        K = 2
        F = 1024

        def _layernorm(x, g, b, eps=1e-05):
            mu = jnp.mean(x, axis=-1, keepdims=True)
            var = jnp.mean(jnp.square(x - mu), axis=-1, keepdims=True)
            return (x - mu) * jax.lax.rsqrt(var + eps) * g + b

        def _attention(x, Wq, bq, Wk, bk, Wv, bv, Wo, bo):
            b, s, d = x.shape
            dh = d // H
            q = (x @ Wq + bq).reshape(b, s, H, dh)
            k = (x @ Wk + bk).reshape(b, s, H, dh)
            v = (x @ Wv + bv).reshape(b, s, H, dh)
            scores = jnp.einsum('bqhd,bkhd->bhqk', q, k) / math.sqrt(dh)
            attn = jax.nn.softmax(scores, axis=-1)
            out = jnp.einsum('bhqk,bkhd->bqhd', attn, v).reshape(b, s, d)
            return out @ Wo + bo

        def _moe(x, gate_w, gate_b, W1, b1, W2, b2):
            b, s, d = x.shape
            xt = x.reshape(b * s, d)
            probs = jax.nn.softmax(xt @ gate_w + gate_b, axis=-1)
            top_v, top_i = jax.lax.top_k(probs, K)
            combine = jnp.sum(jax.nn.one_hot(top_i, E, dtype=xt.dtype) * top_v[..., None], axis=1)
            out = jnp.zeros_like(xt)
            for e in range(E):
                h = jax.nn.gelu(xt @ W1[e] + b1[e], approximate=False) @ W2[e] + b2[e]
                out = out + combine[:, e:e + 1] * h
            return out.reshape(b, s, d)
        key = jax.random.key(seed)
        ks = jax.random.split(key, 16)
        s_d = 1.0 / math.sqrt(D)
        s_f = 1.0 / math.sqrt(F)
        return {'x': jax.random.normal(ks[0], (B, S, D), jnp.float32), 'Wq': jax.random.normal(ks[1], (D, D), jnp.float32) * s_d, 'Wk': jax.random.normal(ks[2], (D, D), jnp.float32) * s_d, 'Wv': jax.random.normal(ks[3], (D, D), jnp.float32) * s_d, 'Wo': jax.random.normal(ks[4], (D, D), jnp.float32) * s_d, 'bq': jnp.zeros((D,), jnp.float32), 'bk': jnp.zeros((D,), jnp.float32), 'bv': jnp.zeros((D,), jnp.float32), 'bo': jnp.zeros((D,), jnp.float32), 'ln1_g': jnp.ones((D,), jnp.float32), 'ln1_b': jnp.zeros((D,), jnp.float32), 'ln2_g': jnp.ones((D,), jnp.float32), 'ln2_b': jnp.zeros((D,), jnp.float32), 'gate_w': jax.random.normal(ks[5], (D, E), jnp.float32) * s_d, 'gate_b': jnp.zeros((E,), jnp.float32), 'W1': jax.random.normal(ks[6], (E, D, F), jnp.float32) * s_d, 'b1': jnp.zeros((E, F), jnp.float32), 'W2': jax.random.normal(ks[7], (E, F, D), jnp.float32) * s_f, 'b2': jnp.zeros((E, D), jnp.float32)}
    _L1_ffn_all = _L1_ffn_setup()
    _L1_ffn_in = {k: v for k, v in _L1_ffn_all.items() if k in ('Wq', 'bq', 'Wk', 'bk', 'Wv', 'bv', 'Wo', 'bo', 'ln1_g', 'ln1_b', 'ln2_g', 'ln2_b', 'gate_w', 'gate_b', 'W1', 'b1', 'W2', 'b2')}
    del _L1_ffn_all
    return {'x': x, 'ctx_1024': ctx_1024, 'mask_SxS2_bk0': mask_SxS2_bk0, 'L0_xattn_Wq': _L0_xattn_in['Wq'], 'L0_xattn_Wk': _L0_xattn_in['Wk'], 'L0_xattn_Wv': _L0_xattn_in['Wv'], 'L0_xattn_Wo': _L0_xattn_in['Wo'], 'L0_xattn_W_bias': _L0_xattn_in['W_bias'], 'L0_ffn_Ws': _L0_ffn_in['Ws'], 'L0_ffn_bs': _L0_ffn_in['bs'], 'L0_ffn_W1': _L0_ffn_in['W1'], 'L0_ffn_b1': _L0_ffn_in['b1'], 'L0_ffn_W2': _L0_ffn_in['W2'], 'L0_ffn_b2': _L0_ffn_in['b2'], 'L1_xattn_Wq': _L1_xattn_in['Wq'], 'L1_xattn_Wk': _L1_xattn_in['Wk'], 'L1_xattn_Wv': _L1_xattn_in['Wv'], 'L1_xattn_Wo': _L1_xattn_in['Wo'], 'L1_ffn_Wq': _L1_ffn_in['Wq'], 'L1_ffn_bq': _L1_ffn_in['bq'], 'L1_ffn_Wk': _L1_ffn_in['Wk'], 'L1_ffn_bk': _L1_ffn_in['bk'], 'L1_ffn_Wv': _L1_ffn_in['Wv'], 'L1_ffn_bv': _L1_ffn_in['bv'], 'L1_ffn_Wo': _L1_ffn_in['Wo'], 'L1_ffn_bo': _L1_ffn_in['bo'], 'L1_ffn_ln1_g': _L1_ffn_in['ln1_g'], 'L1_ffn_ln1_b': _L1_ffn_in['ln1_b'], 'L1_ffn_ln2_g': _L1_ffn_in['ln2_g'], 'L1_ffn_ln2_b': _L1_ffn_in['ln2_b'], 'L1_ffn_gate_w': _L1_ffn_in['gate_w'], 'L1_ffn_gate_b': _L1_ffn_in['gate_b'], 'L1_ffn_W1': _L1_ffn_in['W1'], 'L1_ffn_b1': _L1_ffn_in['b1'], 'L1_ffn_W2': _L1_ffn_in['W2'], 'L1_ffn_b2': _L1_ffn_in['b2']}

def reference(x, ctx_1024, mask_SxS2_bk0, L0_xattn_Wq, L0_xattn_Wk, L0_xattn_Wv, L0_xattn_Wo, L0_xattn_W_bias, L0_ffn_Ws, L0_ffn_bs, L0_ffn_W1, L0_ffn_b1, L0_ffn_W2, L0_ffn_b2, L1_xattn_Wq, L1_xattn_Wk, L1_xattn_Wv, L1_xattn_Wo, L1_ffn_Wq, L1_ffn_bq, L1_ffn_Wk, L1_ffn_bk, L1_ffn_Wv, L1_ffn_bv, L1_ffn_Wo, L1_ffn_bo, L1_ffn_ln1_g, L1_ffn_ln1_b, L1_ffn_ln2_g, L1_ffn_ln2_b, L1_ffn_gate_w, L1_ffn_gate_b, L1_ffn_W1, L1_ffn_b1, L1_ffn_W2, L1_ffn_b2):
    import jax
    import jax.numpy as jnp

    def _L0_xattn_ref(q, k, v, Wq, Wk, Wv, Wo, W_bias):
        import jax, jax.numpy as jnp
        import numpy as np
        B, T, D_MODEL, D_HIDDEN, MAX_SEQLEN = (4, 512, 256, 256, 512)
        Ti = q.shape[1]
        Tj = k.shape[1]
        Q = jnp.einsum('btm,hm->bth', q, Wq)
        K = jnp.einsum('btm,hm->bth', k, Wk)
        V = jnp.einsum('btm,hm->bth', v, Wv)
        pos_bias = W_bias[:Ti, :Tj][None]
        max_key = jnp.max(K, axis=0, keepdims=True)
        max_pos_bias = jnp.max(pos_bias, axis=0, keepdims=True)
        exp_key = jnp.exp(K - max_key)
        exp_pos_bias = jnp.exp(pos_bias - max_pos_bias)
        num = jnp.einsum('bij,bjd->bid', exp_pos_bias, exp_key * V)
        den = jnp.einsum('bij,bjd->bid', exp_pos_bias, exp_key)
        Yt = jax.nn.sigmoid(Q) * num / den
        return jnp.einsum('bth,mh->btm', Yt, Wo)

    def _L0_ffn_ref(x, Ws, bs, W1, b1, W2, b2):
        import jax, jax.numpy as jnp
        import numpy as np
        CAPACITY_FACTOR = 1.0
        B, S, D = x.shape
        E = Ws.shape[1]
        N = B * S
        k = int(CAPACITY_FACTOR * N / E)
        xf = x.reshape(N, D)
        route_prob = jax.nn.softmax(xf @ Ws + bs, axis=-1).T
        route_vals, routes = jax.lax.top_k(route_prob, k)
        xin = xf[routes]
        h = jax.nn.gelu(jnp.einsum('ekd,edf->ekf', xin, W1) + b1[:, None, :])
        out = jnp.einsum('ekf,efd->ekd', h, W2) + b2[:, None, :]
        out = out * route_vals[..., None]
        final = jnp.zeros((N, D), dtype=x.dtype).at[routes.reshape(-1)].add(out.reshape(-1, D))
        return final.reshape(B, S, D)

    def _L1_xattn_ref(query, key, value, attn_mask, Wq, Wk, Wv, Wo):
        import jax, jax.numpy as jnp
        import numpy as np
        B, S, DIM, H = (4, 512, 256, 16)
        HD = DIM // H
        SCALE = HD ** (-0.5)

        def _heads(x):
            b, s, _ = x.shape
            return x.reshape(b, s, H, HD).transpose(0, 2, 1, 3)
        q = _heads(query @ Wq.T)
        k = _heads(key @ Wk.T)
        v = _heads(value @ Wv.T)
        logits = jnp.einsum('bhqd,bhkd->bhqk', q, k) * SCALE
        mask = attn_mask[None, None, :, :]
        masked = jnp.where(mask, logits, -1000000000.0)
        weights = jax.nn.softmax(masked, axis=-1)
        weights = weights * mask.astype(weights.dtype)
        denom = jnp.maximum(weights.sum(axis=-1, keepdims=True), 1e-09)
        weights = weights / denom
        out = jnp.einsum('bhqk,bhkd->bhqd', weights, v)
        out = out.transpose(0, 2, 1, 3).reshape(query.shape[0], query.shape[1], -1)
        return out @ Wo.T

    def _L1_ffn_ref(x, Wq, bq, Wk, bk, Wv, bv, Wo, bo, ln1_g, ln1_b, ln2_g, ln2_b, gate_w, gate_b, W1, b1, W2, b2):
        import jax, jax.numpy as jnp
        import numpy as np
        import math
        B, S, D = (4, 512, 256)
        H = 16
        E = 8
        K = 2
        F = 1024

        def _layernorm(x, g, b, eps=1e-05):
            mu = jnp.mean(x, axis=-1, keepdims=True)
            var = jnp.mean(jnp.square(x - mu), axis=-1, keepdims=True)
            return (x - mu) * jax.lax.rsqrt(var + eps) * g + b

        def _attention(x, Wq, bq, Wk, bk, Wv, bv, Wo, bo):
            b, s, d = x.shape
            dh = d // H
            q = (x @ Wq + bq).reshape(b, s, H, dh)
            k = (x @ Wk + bk).reshape(b, s, H, dh)
            v = (x @ Wv + bv).reshape(b, s, H, dh)
            scores = jnp.einsum('bqhd,bkhd->bhqk', q, k) / math.sqrt(dh)
            attn = jax.nn.softmax(scores, axis=-1)
            out = jnp.einsum('bhqk,bkhd->bqhd', attn, v).reshape(b, s, d)
            return out @ Wo + bo

        def _moe(x, gate_w, gate_b, W1, b1, W2, b2):
            b, s, d = x.shape
            xt = x.reshape(b * s, d)
            probs = jax.nn.softmax(xt @ gate_w + gate_b, axis=-1)
            top_v, top_i = jax.lax.top_k(probs, K)
            combine = jnp.sum(jax.nn.one_hot(top_i, E, dtype=xt.dtype) * top_v[..., None], axis=1)
            out = jnp.zeros_like(xt)
            for e in range(E):
                h = jax.nn.gelu(xt @ W1[e] + b1[e], approximate=False) @ W2[e] + b2[e]
                out = out + combine[:, e:e + 1] * h
            return out.reshape(b, s, d)
        x = x + _layernorm(_attention(x, Wq, bq, Wk, bk, Wv, bv, Wo, bo), ln1_g, ln1_b)
        x = x + _layernorm(_moe(x, gate_w, gate_b, W1, b1, W2, b2), ln2_g, ln2_b)
        return x
    x = x + _L0_xattn_ref(_layernorm(x, axis=-1), ctx_1024, ctx_1024, L0_xattn_Wq, L0_xattn_Wk, L0_xattn_Wv, L0_xattn_Wo, L0_xattn_W_bias)
    x = x + _L0_ffn_ref(_layernorm(x, axis=-1), L0_ffn_Ws, L0_ffn_bs, L0_ffn_W1, L0_ffn_b1, L0_ffn_W2, L0_ffn_b2)
    x = x + _L1_xattn_ref(_layernorm(x, axis=-1), ctx_1024, ctx_1024, mask_SxS2_bk0, L1_xattn_Wq, L1_xattn_Wk, L1_xattn_Wv, L1_xattn_Wo)
    x = x + _L1_ffn_ref(_layernorm(x, axis=-1), L1_ffn_Wq, L1_ffn_bq, L1_ffn_Wk, L1_ffn_bk, L1_ffn_Wv, L1_ffn_bv, L1_ffn_Wo, L1_ffn_bo, L1_ffn_ln1_g, L1_ffn_ln1_b, L1_ffn_ln2_g, L1_ffn_ln2_b, L1_ffn_gate_w, L1_ffn_gate_b, L1_ffn_W1, L1_ffn_b1, L1_ffn_W2, L1_ffn_b2)
    return x

_drawn_inputs = setup_inputs


def setup_inputs(seed=0):
    import zlib

    import numpy as np

    out = dict(_drawn_inputs(seed))
    spreads = {'L0_ffn_bs': (0.0, 0.1),
     'L0_ffn_b1': (0.0, 0.1),
     'L0_ffn_b2': (0.0, 0.1),
     'L1_ffn_bq': (0.0, 0.1),
     'L1_ffn_bk': (0.0, 0.8),
     'L1_ffn_bv': (0.0, 0.1),
     'L1_ffn_bo': (0.0, 0.1),
     'L1_ffn_ln1_g': (1.0, 0.2),
     'L1_ffn_ln1_b': (0.0, 0.1),
     'L1_ffn_ln2_g': (1.0, 0.2),
     'L1_ffn_ln2_b': (0.0, 0.1),
     'L1_ffn_gate_b': (0.0, 0.1),
     'L1_ffn_b1': (0.0, 0.1),
     'L1_ffn_b2': (0.0, 0.1)}
    factors = {'L1_xattn_Wq': 4.024, 'L1_xattn_Wk': 3.51}
    for name, (base, spread) in spreads.items():
        noise = np.random.default_rng([zlib.crc32(name.encode()), seed]).standard_normal(out[name].shape)
        drawn = base * np.exp(spread * noise) if base else spread * noise
        out[name] = jnp.asarray(drawn.astype(out[name].dtype))
    for name, factor in factors.items():
        out[name] = (out[name] * factor).astype(out[name].dtype)
    return out
```

```python
from contextlib import ExitStack

import concourse.bass as bass
from concourse import mybir

F32 = mybir.dt.float32
BF16 = mybir.dt.bfloat16
U32 = mybir.dt.uint32
U8 = mybir.dt.uint8
ALU = mybir.AluOpType
ACT = mybir.ActivationFunctionType
AX = mybir.AxisListType

P = 128
B, S, D = 8, 512, 256
N = B * S
NC = N // P
CB = S // P
DC = D // P
E, F = 8, 1024
FC = F // P
H, HD = 16, 16
HG = 4
NG = H // HG
HC = H // DC
CAP = N // E
TOPK = 2
TILE = 512
TC = TILE // P
TILES = {"L0": E * CAP // TILE, "L1": (N * TOPK + E * (TILE - 1)) // TILE}
COLS = (TILES["L1"] + 1) * TC
SLAB = 16
BITS = 30
EPS = 1e-5
SCALE = HD ** -0.5
BIG = 2.0 ** 30
Q_TERMS = (0, 0, 1, 1, 0, 2)
K_TERMS = (0, 1, 0, 1, 2, 0)
KR = 16 * len(Q_TERMS)


def past(n):
    return n + 1


class Stage:

    def __init__(self, nc, ctx, tag):
        self.nc, self.ctx, self.tag, self.sems = nc, ctx, tag, []

    def sb(self, name, shape, dt=F32):
        return self.ctx.enter_context(self.nc.sbuf_tensor(f"{self.tag}_{name}", shape, dt))

    def ps(self, name, shape, dt=F32):
        return self.ctx.enter_context(self.nc.psum_tensor(f"{self.tag}_{name}", shape, dt))

    def sem(self, name):
        self.sems.append(self.ctx.enter_context(self.nc.semaphore(f"{self.tag}_{name}")))
        return self.sems[-1]

    def pool_dma_sem(self, name):
        return self.ctx.enter_context(self.nc.semaphore(f"{self.tag}_{name}"))

    def set_semaphores(self, sp):
        for s in self.sems:
            sp.sem_inc(s, 1)


def alone(eng):
    eng.nop(nofuse=True)


class Chain:

    def __init__(self, eng, sem, base=0):
        self.eng, self.sem, self.base, self.n = eng, sem, base, 0

    def __call__(self, ins):
        ins.then_inc(self.sem, 1)
        self.n += 1
        self.eng.wait_ge(self.sem, past(self.base + self.n))
        if not isinstance(self.base, int):
            alone(self.eng)


def setup(nc, G, a):
    with ExitStack() as ctx:
        st = Stage(nc, ctx, "setup")
        loaded, cleared, built, mask_in = (st.sem(n) for n in ("loaded", "cleared", "built", "mask_in"))
        vec, zeroed, stored, counted = (st.sem(n) for n in ("vec", "zeroed", "stored", "counted"))
        zero = st.sb("zero", [P, D])
        lane_i, token_i, spare_i = (st.sb(n, [P, w], mybir.dt.int32) for n, w in (("lane", P), ("tok", NC), ("spare", 1)))
        raw = [st.sb(f"mask_raw{i}", [P, CB, S], U8) for i in range(2)]
        with nc.Block() as block:

            @block.sync
            def _(sp):
                st.set_semaphores(sp)
                sp.dma_start(G["x"][:], a["x"].rearrange("b (c p) d -> p (b c) d", p=P)).then_inc(loaded, 16)
                sp.dma_start(raw[0][:], a["mask"].rearrange("(c p) k -> p c k", p=P)).then_inc(mask_in, 16)
                sp.dma_start(raw[1][:], a["maskT"].rearrange("(c p) k -> p c k", p=P)).then_inc(mask_in, 16)
                sp.wait_ge(loaded, past(16))
                sp.wait_ge(zeroed, past(1))
                for dst, first in ((G["sum1"], 0), (G["rows0"], NC), (G["rows1"], NC), (G["sum0"], NC)):
                    sp.dma_start(dst.rearrange("(c p) d -> p c d", p=P)[:, first:, :],
                                 zero[:].unsqueeze(1).broadcast_to([P, NC + 1 - first, D])).then_inc(stored, 16)
                sp.wait_ge(stored, past(64))

            @block.gpsimd
            def _(pool):
                pool.memset(G["ident"][:], 0.0).then_inc(cleared, 1)
                pool.memset(G["identb"][:], 0.0).then_inc(cleared, 1)
                pool.memset(G["before"][:], 1.0).then_inc(cleared, 1)
                pool.memset(G["ones"][:], 1.0).then_inc(built, 1)
                pool.memset(G["mhalf"][:], -0.5).then_inc(built, 1)
                pool.memset(G["lower"][:], 1.0).then_inc(cleared, 1)
                pool.wait_ge(cleared, past(4))
                for t in (G["ident"], G["identb"]):
                    pool.affine_select(out=t[:], in_=t[:], compare_op=ALU.not_equal, fill=1.0, base=0,
                                       pattern=[[-1, P]], channel_multiplier=1).then_inc(built, 1)
                pool.affine_select(out=G["before"][:], in_=G["before"][:], compare_op=ALU.is_gt, fill=0.0,
                                   base=0, pattern=[[1, P]], channel_multiplier=-1).then_inc(built, 1)
                pool.affine_select(out=G["lower"][:], in_=G["lower"][:], compare_op=ALU.is_gt, fill=0.0,
                                   base=0, pattern=[[1, E], [-1, E]], channel_multiplier=0).then_inc(built, 1)
                pool.wait_ge(built, past(6))
                pool.iota(lane_i[:], pattern=[[1, P]], base=0, channel_multiplier=0).then_inc(counted, 1)
                pool.iota(token_i[:], pattern=[[P, NC]], base=1, channel_multiplier=1).then_inc(counted, 1)
                pool.iota(spare_i[:], pattern=[[1, 1]], base=N + 1, channel_multiplier=1).then_inc(counted, 1)

            @block.vector
            def _(dve):
                dve.memset(zero[:], 0.0).then_inc(zeroed, 1)
                dve.wait_ge(counted, past(3))
                for dst, src in ((G["lane"], lane_i), (G["token1"], token_i), (G["spare1"], spare_i)):
                    dve.tensor_copy(dst[:], src[:]).then_inc(vec, 1)
                dve.wait_ge(mask_in, past(32))
                for i in range(2):
                    dve.tensor_scalar(G["bias"][i][:], raw[i][:], BIG, -BIG, ALU.mult, ALU.add).then_inc(vec, 1)
                dve.wait_ge(vec, past(5))


def aft_keys(nc, G, a):
    with ExitStack() as ctx:
        st = Stage(nc, ctx, "aft")
        ctxT = st.sb("ctxT", [P, DC, N])
        wk, wv = st.sb("wk", [P, DC, D]), st.sb("wv", [P, DC, D])
        keys = st.sb("keys", [P, DC, B, S])
        top = st.sb("top", [P, DC, S])
        diff, ex = st.sb("diff", [P, DC, S]), st.sb("ex", [P, DC, S])
        den, num, rden = st.sb("den", [P, DC]), st.sb("num", [P, DC]), st.sb("rden", [P, DC])
        pk = [st.ps(f"pk{i}", [P, S]) for i in range(DC)]
        pv = [st.ps(f"pv{i}", [P, S]) for i in range(DC)]
        loaded, keys_ps, keys_saved, keys_top = (st.sem(n) for n in ("loaded", "keys_ps", "keys_saved", "keys_top"))
        diff_ready, ex_ready, vals_ps, summed, dvec = (
            st.sem(n) for n in ("diff_ready", "ex_ready", "vals_ps", "summed", "dvec"))
        cleared = st.sem("cleared")
        with nc.Block() as block:

            @block.sync
            def _(sp):
                st.set_semaphores(sp)
                sp.dma_start(ctxT[:], a["ctxT"].rearrange("(c p) n -> p c n", p=P)).then_inc(loaded, 16)
                sp.dma_start(wk[:], a["L0_WkT"].rearrange("(c p) n -> p c n", p=P)).then_inc(loaded, 16)
                sp.dma_start(wv[:], a["L0_WvT"].rearrange("(c p) n -> p c n", p=P)).then_inc(loaded, 16)

            @block.tensor
            def _(pe):
                pe.wait_ge(loaded, past(48))
                with pe.Fori(0, B) as b:
                    pe.wait_ge(keys_saved, past(b * DC))
                    for o in range(DC):
                        for m in range(DC):
                            mm = pe.matmul(pk[o][:], wk[:, m, o * P:(o + 1) * P], ctxT[:, m, bass.ds(b * S, S)],
                                           start=m == 0, stop=m == DC - 1)
                        mm.then_inc(keys_ps, 1)
                with pe.Fori(0, B) as b:
                    pe.wait_ge(summed, past(b * DC))
                    for o in range(DC):
                        for m in range(DC):
                            mm = pe.matmul(pv[o][:], wv[:, m, o * P:(o + 1) * P], ctxT[:, m, bass.ds(b * S, S)],
                                           start=m == 0, stop=m == DC - 1)
                        mm.then_inc(vals_ps, 1)

            @block.scalar
            def _(act):
                with act.Fori(0, B) as b:
                    for o in range(DC):
                        act.wait_ge(keys_ps, past(b * DC + o + 1))
                        act.copy(keys[:, o, b, :], pk[o][:]).then_inc(keys_saved, 1)
                with act.Fori(0, B) as b:
                    act.wait_ge(diff_ready, past(b + 1))
                    act.wait_ge(summed, past(b * DC))
                    for o in range(DC):
                        act.activation(ex[:, o, :], diff[:, o, :], ACT.Exp,
                                       accum_out=den[:, o:o + 1]).then_inc(ex_ready, 1)

            @block.vector
            def _(dve):
                dve.memset(top[:], -3.0e38).then_inc(cleared, 1)
                dve.wait_ge(cleared, past(1))
                with dve.Fori(0, B) as b:
                    dve.wait_ge(keys_top, past(b * DC))
                    for o in range(DC):
                        dve.wait_ge(keys_saved, past(b * DC + o + 1))
                        dve.tensor_tensor(top[:, o, :], top[:, o, :], keys[:, o, b, :], ALU.max).then_inc(keys_top, 1)
                dve.wait_ge(keys_top, past(B * DC))
                dve.wait_ge(keys_saved, past(B * DC))
                with dve.Fori(0, B) as b:
                    dve.wait_ge(ex_ready, past(b * DC))
                    dve.tensor_tensor(diff[:], keys[:, :, b, :], top[:], ALU.subtract).then_inc(diff_ready, 1)
                    dve.wait_ge(dvec, past(b * 2))
                    for o in range(DC):
                        dve.wait_ge(ex_ready, past(b * DC + o + 1))
                        dve.wait_ge(vals_ps, past(b * DC + o + 1))
                        dve.tensor_tensor_reduce(ex[:, o, :], ex[:, o, :], pv[o][:], 1.0, 0.0, ALU.mult, ALU.add,
                                                 num[:, o:o + 1]).then_inc(summed, 1)
                    dve.reciprocal(rden[:], den[:]).then_inc(dvec, 1)
                    dve.wait_ge(dvec, past(b * 2 + 1))
                    dve.wait_ge(summed, past(b * DC + DC))
                    dve.tensor_tensor(G["ratio"][:, :, b], num[:], rden[:], ALU.mult).then_inc(dvec, 1)
                dve.wait_ge(dvec, past(2 * B))


def norm_stats(dve, chain, stats, mv, src):
    for t in range(CB):
        ins = dve.bn_stats(stats[:, t, :], src(t))
    chain(ins)
    for t in range(CB):
        ins = dve.bn_aggr(mv[:, t, :], stats[:, t, :])
    return ins


def norm_rstd(pool, G, chain, mv, rstd):
    alone(pool)
    chain(pool.tensor_scalar(rstd[:], mv[:, :, 1], EPS, None, ALU.add))
    return pool.tensor_tensor(rstd[:], rstd[:], G["mhalf"][:, 0:CB], ALU.pow)


def norm_apply(dve, dst, src, mv, rstd):
    for t in range(CB):
        ins = dve.tensor_scalar(dst(t), src(t), mv[:, t, 0:1], rstd[:, t:t + 1], ALU.subtract, ALU.mult)
    return ins


def turn(pe, G, bank, src):
    for m in range(DC):
        for t in range(CB):
            ins = pe.transpose(bank(m)[:, t * P:(t + 1) * P], src(t, m), G["ident"][:])
    return ins


def router_dve(dve, chain, logits, small, wide, exp_ready, ex_wait, psum_ready_inc, out):
    top, tot, rec = small
    shifted, ex = wide
    chain(dve.tensor_reduce(top[:], logits, AX.X, ALU.max))
    dve.tensor_tensor(shifted[:], logits, top[:].unsqueeze(2).broadcast_to([P, CB, E]),
                      ALU.subtract).then_inc(psum_ready_inc, 1)
    dve.wait_ge(exp_ready, past(ex_wait))
    chain(dve.tensor_reduce(tot[:], ex[:], AX.X, ALU.add))
    chain(dve.reciprocal(rec[:], tot[:]))
    chain(dve.tensor_tensor(out, ex[:], rec[:].unsqueeze(2).broadcast_to([P, CB, E]), ALU.mult))


def aft_tokens(nc, G, a):
    with ExitStack() as ctx:
        st = Stage(nc, ctx, "tok")
        wq, wo, ws = st.sb("wq", [P, DC, D]), st.sb("wo", [P, DC, D]), st.sb("ws", [P, DC, E])
        bs = st.sb("bs", [1, E])
        stats, mv, rstd = st.sb("stats", [P, CB, 6]), st.sb("mv", [P, CB, 2]), st.sb("rstd", [P, CB])
        xn, xnT, yT = st.sb("xn", [P, CB, D]), st.sb("xnT", [P, DC, S]), st.sb("yT", [P, DC, S])
        fxT = st.sb("fxT", [P, DC, S])
        small = [st.sb(n, [P, CB]) for n in ("rtop", "rsum", "rrec")]
        wide = [st.sb(n, [P, CB, E]) for n in ("rshift", "rexp")]
        pt = [st.ps(f"pt{i}", [P, S]) for i in range(DC)]
        pq = [st.ps(f"pq{i}", [P, S]) for i in range(DC)]
        po = [st.ps(f"po{i}", [P, 2, D]) for i in range(2)]
        pl = st.ps("pl", [P, S])
        names = ("loaded", "stats_ready", "rstd_ready", "xn_ready", "turned", "xnT_ready", "q_ps", "sig_ready",
                 "yT_ready", "out_ps", "x1_ready", "logits_ps", "shift_ready", "rexp_ready", "vchain", "pchain",
                 "x1_stored", "rows_stored")
        (loaded, stats_ready, rstd_ready, xn_ready, turned, xnT_ready, q_ps, sig_ready, yT_ready, out_ps, x1_ready,
         logits_ps, shift_ready, rexp_ready, vchain, pchain, x1_stored, rows_stored) = (st.sem(n) for n in names)
        X = G["x"]
        VPER, PPER = 6, 2

        with nc.Block() as block:

            @block.sync
            def _(sp):
                st.set_semaphores(sp)
                for dst, src in ((wq, "L0_WqT"), (wo, "L0_WoT"), (ws, "L0_Ws")):
                    sp.dma_start(dst[:], a[src].rearrange("(c p) n -> p c n", p=P)).then_inc(loaded, 16)
                sp.dma_start(bs[:], a["L0_bs"]).then_inc(loaded, 16)
                with sp.Fori(0, B) as b:
                    here = bass.ds(b * CB, CB)
                    sp.wait_ge(x1_ready, past(b + 1))
                    sp.dma_start(G["sum0"].rearrange("(c p) d -> p c d", p=P)[:, here, :], X[:, here, :]
                                 ).then_inc(x1_stored, 16)
                    sp.wait_ge(xn_ready, past(b * 2 + 2))
                    sp.dma_start(G["rows0"].rearrange("(c p) d -> p c d", p=P)[:, here, :], xn[:]
                                 ).then_inc(rows_stored, 16)
                sp.wait_ge(x1_stored, past(16 * B))
                sp.wait_ge(rows_stored, past(16 * B))

            @block.tensor
            def _(pe):
                pe.wait_ge(loaded, past(64))
                with pe.Fori(0, B) as b:
                    pe.wait_ge(xn_ready, past(b * 2 + 1))
                    turn(pe, G, lambda m: pt[m], lambda t, m: xn[:, t, m * P:(m + 1) * P]).then_inc(turned, 1)
                    pe.wait_ge(xnT_ready, past(b * 2 + 1))
                    for o in range(DC):
                        for m in range(DC):
                            mm = pe.matmul(pq[o][:], wq[:, m, o * P:(o + 1) * P], xnT[:, m, :],
                                           start=m == 0, stop=m == DC - 1)
                    mm.then_inc(q_ps, 1)
                    pe.wait_ge(yT_ready, past(b + 1))
                    for t in range(CB):
                        for m in range(DC):
                            mm = pe.matmul(po[t // 2][:, t % 2, :], yT[:, m, t * P:(t + 1) * P], wo[:, m, :],
                                           start=m == 0, stop=m == DC - 1)
                    mm.then_inc(out_ps, 1)
                    pe.wait_ge(xn_ready, past(b * 2 + 2))
                    turn(pe, G, lambda m: pt[m], lambda t, m: xn[:, t, m * P:(m + 1) * P]).then_inc(turned, 1)
                    pe.wait_ge(xnT_ready, past(b * 2 + 2))
                    for t in range(CB):
                        pe.matmul(pl[:, t * E:(t + 1) * E], G["ones"][0:1, :], bs[:], start=True, stop=False)
                        for m in range(DC):
                            mm = pe.matmul(pl[:, t * E:(t + 1) * E], fxT[:, m, t * P:(t + 1) * P], ws[:, m, :],
                                           start=False, stop=m == DC - 1)
                    mm.then_inc(logits_ps, 1)

            @block.scalar
            def _(act):
                with act.Fori(0, B) as b:
                    act.wait_ge(turned, past(b * 2 + 1))
                    for m in range(DC):
                        ins = act.copy(xnT[:, m, :], pt[m][:])
                    ins.then_inc(xnT_ready, 1)
                    act.wait_ge(q_ps, past(b + 1))
                    act.wait_ge(out_ps, past(b))
                    for o in range(DC):
                        ins = act.activation(yT[:, o, :], pq[o][:], ACT.Sigmoid)
                    ins.then_inc(sig_ready, 1)
                    act.wait_ge(turned, past(b * 2 + 2))
                    act.wait_ge(logits_ps, past(b))
                    for m in range(DC):
                        ins = act.copy(fxT[:, m, :], pt[m][:])
                    ins.then_inc(xnT_ready, 1)
                    act.wait_ge(shift_ready, past(b + 1))
                    act.activation(wide[1][:], wide[0][:], ACT.Exp).then_inc(rexp_ready, 1)

            @block.gpsimd
            def _(pool):
                with pool.Fori(0, B) as b:
                    chain = Chain(pool, pchain, b * PPER)
                    for k in range(2):
                        pool.wait_ge(stats_ready, past(b * 2 + k + 1))
                        norm_rstd(pool, G, chain, mv, rstd).then_inc(rstd_ready, 1)
                    assert chain.n == PPER

            @block.vector
            def _(dve):
                with dve.Fori(0, B) as b:
                    chain = Chain(dve, vchain, b * VPER)

                    def rows(t):
                        return X[:, b * CB + t, :]

                    def norm(k):
                        alone(dve)
                        norm_stats(dve, chain, stats, mv, rows).then_inc(stats_ready, 1)
                        dve.wait_ge(rstd_ready, past(b * 2 + k + 1))
                        dve.wait_ge(stats_ready, past(b * 2 + k + 1))
                        dve.wait_ge(turned, past(b * 2 + k))
                        if k == 0:
                            dve.wait_ge(rows_stored, past(b * 16))
                        norm_apply(dve, lambda t: xn[:, t, :], rows, mv, rstd).then_inc(xn_ready, 1)

                    norm(0)
                    dve.wait_ge(sig_ready, past(b + 1))
                    for o in range(DC):
                        ins = dve.tensor_scalar(yT[:, o, :], yT[:, o, :], G["ratio"][:, o, bass.ds(b, 1)], None,
                                                ALU.mult)
                    ins.then_inc(yT_ready, 1)
                    dve.wait_ge(out_ps, past(b + 1))
                    for k in range(2):
                        rr = X[:, bass.ds(b * CB + 2 * k, 2), :]
                        ins = dve.tensor_tensor(rr, rr, po[k][:], ALU.add)
                    ins.then_inc(x1_ready, 1)
                    dve.wait_ge(x1_ready, past(b + 1))
                    norm(1)
                    dve.wait_ge(logits_ps, past(b + 1))
                    router_dve(dve, chain, pl[:, 0:CB * E].rearrange("p (t e) -> p t e", e=E), small, wide,
                               rexp_ready, b + 1, shift_ready, G["prob"][:, bass.ds(b * CB, CB), :])
                    assert chain.n == VPER


def in_front_pe(pe, G, pin, pall, flags):
    pe.matmul(pin[:, 0:E * NC], G["before"][:], flags, start=True, stop=True)
    return pe.matmul(pall[:, 0:E * NC], G["ones"][:], flags, start=True, stop=True)


def in_front_dve(dve, chain, rank, scan, keep, pin, pall):
    chain(dve.tensor_tensor_scan(scan[:], keep[:], pall[:, 0:E * NC], 0.0, ALU.mult, ALU.add))
    chain(dve.tensor_tensor(rank[:], scan[:], pall[:, 0:E * NC], ALU.subtract))
    chain(dve.tensor_tensor(rank[:], rank[:], pin[:, 0:E * NC], ALU.add))


def expert_choice(nc, G):
    with ExitStack() as ctx:
        st = Stage(nc, ctx, "pick")
        low, cand, took = (st.sb(n, [P, E], U32) for n in ("low", "cand", "took"))
        bit = st.sb("bit", [P, 1], U32)
        cmp_, more, equal = (st.sb(n, [P, E, NC]) for n in ("cmp", "more", "equal"))
        cnt, need = st.sb("cnt", [P, E]), st.sb("need", [P, E])
        keep, rank, scan = (st.sb(n, [P, E * NC]) for n in ("keep", "rank", "scan"))
        ptot, pin, pall = st.ps("ptot", [P, S]), st.ps("pin", [P, S]), st.ps("pall", [P, S])
        vchain, counted, totalled = (st.sem(n) for n in ("vchain", "counted", "totalled"))
        prob = G["prob"][:].rearrange("p c e -> p e c")

        def wide(t):
            return t.unsqueeze(2).broadcast_to([P, E, NC])

        VPER, INIT = 6, 4
        with nc.Block() as block:

            @block.sync
            def _(sp):
                st.set_semaphores(sp)

            @block.vector
            def _(dve):
                chain = Chain(dve, vchain)
                chain(dve.memset(low[:], 0))
                chain(dve.memset(bit[:], 1 << (BITS - 1)))
                chain(dve.memset(keep[:], 1.0))
                chain(dve.memset(keep[:].rearrange("p (e c) -> p e c", c=NC)[:, :, 0:1], 0.0))
                assert chain.n == INIT
                with dve.Fori(0, BITS) as i:
                    c = Chain(dve, vchain, i * VPER + INIT)
                    c(dve.tensor_tensor(cand[:], low[:], bit[:].broadcast_to([P, E]), ALU.bitwise_or))
                    c(dve.tensor_tensor(cmp_[:], prob, wide(cand[:].bitcast(F32)), ALU.is_ge))
                    dve.tensor_reduce(cnt[:], cmp_[:], AX.X, ALU.add).then_inc(counted, 1)
                    dve.wait_ge(totalled, past(i + 1))
                    c(dve.scalar_tensor_tensor(out=took[:], in0=ptot[:, 0:E], scalar=float(CAP),
                                               in1=bit[:].broadcast_to([P, E]), op0=ALU.is_ge, op1=ALU.mult))
                    c(dve.tensor_tensor(low[:], low[:], took[:], ALU.bitwise_or))
                    c(dve.tensor_scalar(bit[:], bit[:], 1, None, ALU.logical_shift_right))
                    c(dve.nop())
                    assert c.n == VPER
                chain = Chain(dve, vchain, BITS * VPER + INIT)
                edge = wide(low[:].bitcast(F32))
                chain(dve.tensor_tensor(more[:], prob, edge, ALU.is_gt))
                chain(dve.tensor_tensor(equal[:], prob, edge, ALU.is_equal))
                dve.tensor_reduce(cnt[:], more[:], AX.X, ALU.add).then_inc(counted, 1)
                dve.wait_ge(totalled, past(BITS + 1))
                chain(dve.tensor_scalar(need[:], ptot[:, 0:E], -1.0, float(CAP), ALU.mult, ALU.add))
                in_front_dve(dve, chain, rank, scan, keep, pin, pall)
                rv = rank[:].rearrange("p (e c) -> p e c", c=NC)
                chain(dve.tensor_tensor(rv, rv, wide(need[:]), ALU.is_lt))
                chain(dve.tensor_tensor(rv, rv, equal[:], ALU.mult))
                dve.tensor_tensor(more[:], rv, more[:], ALU.add).then_inc(counted, 1)
                dve.wait_ge(counted, past(BITS + 2))
                dve.wait_ge(totalled, past(BITS + 2))
                in_front_dve(dve, chain, rank, scan, keep, pin, pall)
                chain(dve.scalar_tensor_tensor(out=rv, in0=rv, scalar=1.0, in1=more[:], op0=ALU.add, op1=ALU.mult))
                chain(dve.tensor_scalar(G["place"][:], rank[:], -1.0, None, ALU.add))
                chain(dve.tensor_copy(G["weight"][:].rearrange("p (e c) -> p e c", c=NC), prob))

            @block.tensor
            def _(pe):
                with pe.Fori(0, BITS) as i:
                    pe.wait_ge(counted, past(i + 1))
                    pe.matmul(ptot[:, 0:E], G["ones"][:], cnt[:], start=True, stop=True).then_inc(totalled, 1)
                pe.wait_ge(counted, past(BITS + 1))
                eq = equal[:].rearrange("p e c -> p (e c)")
                in_front_pe(pe, G, pin, pall, eq)
                pe.matmul(ptot[:, 0:E], G["ones"][:], cnt[:], start=True, stop=True).then_inc(totalled, 1)
                pe.wait_ge(counted, past(BITS + 2))
                in_front_pe(pe, G, pin, pall, more[:].rearrange("p e c -> p (e c)")).then_inc(totalled, 1)


def lists(nc, G, tag, sets, per, cols):
    with ExitStack() as ctx:
        st = Stage(nc, ctx, "li" + tag)
        n_all, I32 = sets * per, mybir.dt.int32
        whole, high, low = (st.sb(n, [P, n_all], I32) for n in ("whole", "high", "low"))
        highf, lowf = st.sb("highf", [P, n_all]), st.sb("lowf", [P, n_all])
        hot_low = [st.sb(f"hot_low{i}", [P, SLAB, P]) for i in range(2)]
        hot_high = st.sb("hot_high", [P, SLAB, cols])
        scaled = [st.sb(f"scaled{i}", [P, SLAB, 2, cols]) for i in range(2)]
        spare = st.sb("spare", [P, sets, cols])
        pt = st.ps("pt", [P, S])
        slabs = per // SLAB
        vchain, built, summed = (st.sem(n) for n in ("vchain", "built", "summed"))
        INIT, VPER = 7, 2 * slabs
        lane = G["lane"]
        with nc.Block() as block:

            @block.sync
            def _(sp):
                st.set_semaphores(sp)

            @block.vector
            def _(dve):
                chain = Chain(dve, vchain)
                chain(dve.tensor_copy(whole[:], G["place"][:, 0:n_all]))
                chain(dve.tensor_scalar(high[:], whole[:], 7, None, ALU.logical_shift_right))
                chain(dve.tensor_scalar(low[:], whole[:], P - 1, None, ALU.bitwise_and))
                chain(dve.tensor_copy(highf[:], high[:]))
                chain(dve.tensor_copy(lowf[:], low[:]))
                chain(dve.tensor_scalar(G["row"][:], G["spare1"][:].broadcast_to([P, COLS]), -1.0, None, ALU.add))
                chain(dve.memset(G["roww"][:], 0.0))
                assert chain.n == INIT
                with dve.Fori(0, sets) as r:
                    c = Chain(dve, vchain, r * VPER + INIT)
                    for s in range(slabs):
                        here, buf = bass.ds(r * per + s * SLAB, SLAB), s % 2
                        dve.wait_ge(summed, past(r * slabs + max(s - 1, 0)))

                        def chunks(t, width):
                            return t.unsqueeze(2).broadcast_to([P, SLAB, width])

                        c(dve.tensor_tensor(hot_low[buf][:], lane[:].unsqueeze(1).broadcast_to([P, SLAB, P]),
                                            chunks(lowf[:, here], P), ALU.is_equal))
                        c(dve.tensor_tensor(hot_high[:], lane[:, 0:cols].unsqueeze(1).broadcast_to([P, SLAB, cols]),
                                            chunks(highf[:, here], cols), ALU.is_equal))
                        first = s * SLAB % NC
                        dve.tensor_tensor(scaled[buf][:, :, 0, :], hot_high[:],
                                          chunks(G["token1"][:, first:first + SLAB], cols), ALU.mult
                                          ).then_inc(built, 1)
                        dve.tensor_tensor(scaled[buf][:, :, 1, :], hot_high[:],
                                          chunks(G["weight"][:, here], cols), ALU.mult).then_inc(built, 1)
                        dve.wait_ge(built, past(r * slabs * 2 + s * 2 + 2))
                        alone(dve)
                    assert c.n == VPER
                dve.wait_ge(summed, past(sets * slabs))
                chain = Chain(dve, vchain, sets * VPER + INIT)
                view = pt[:, 0:sets * 2 * cols].rearrange("p (r k c) -> p r k c", k=2, c=cols)
                chain(dve.tensor_scalar(spare[:], view[:, :, 0, :], 0.0, G["spare1"][:, 0:1], ALU.is_equal, ALU.mult))
                chain(dve.scalar_tensor_tensor(
                    out=G["row"][:, 0:sets * cols].rearrange("p (r c) -> p r c", c=cols), in0=view[:, :, 0, :],
                    scalar=-1.0, in1=spare[:], op0=ALU.add, op1=ALU.add))
                chain(dve.tensor_copy(G["roww"][:, 0:sets * cols].rearrange("p (r c) -> p r c", c=cols),
                                      view[:, :, 1, :]))

            @block.tensor
            def _(pe):
                with pe.Fori(0, sets) as r:
                    for s in range(slabs):
                        pe.wait_ge(built, past(r * slabs * 2 + s * 2 + 2))
                        alone(pe)
                        for i in range(SLAB):
                            mm = pe.matmul(pt[:, bass.ds(r * 2 * cols, 2 * cols)], hot_low[s % 2][:, i, :],
                                           scaled[s % 2][:, i, :, :].rearrange("p k c -> p (k c)"),
                                           start=s == 0 and i == 0, stop=s == slabs - 1 and i == SLAB - 1)
                        mm.then_inc(summed, 1)


def experts(nc, G, a, tag, gelu):
    rows, sums, tiles = G["rows" + tag[1]], G["sum" + tag[1]], TILES[tag]
    with ExitStack() as ctx:
        st = Stage(nc, ctx, "ex" + tag)
        w1, w2 = st.sb("w1", [P, DC, F]), st.sb("w2", [P, FC, D])
        b1, b2 = st.sb("b1", [P, FC]), st.sb("b2", [1, D])
        get, put = st.sb("get", [P, TC], U32), st.sb("put", [P, TC], U32)
        xg, xgT = st.sb("xg", [P, TC, D]), st.sb("xgT", [P, DC, TILE])
        hid, ys = st.sb("hid", [P, FC, TILE]), st.sb("ys", [P, TC, D])
        pt = [st.ps(f"pt{i}", [P, TILE]) for i in range(DC)]
        ph = [st.ps(f"ph{i}", [P, TILE]) for i in range(2)]
        po = [st.ps(f"po{i}", [P, D]) for i in range(2)]
        names = ("w1_in", "w2_in", "get_ready", "turned", "xgT_ready", "hid_ps", "hid_ready", "out_ps", "ys_ready",
                 "put_ready", "x_in")
        (w1_in, w2_in, get_ready, turned, xgT_ready, hid_ps, hid_ready, out_ps, ys_ready, put_ready,
         x_in) = (st.sem(n) for n in names)
        gathered, added = st.pool_dma_sem("gathered"), st.pool_dma_sem("added")
        W1, W2, b1d, b2d = (a[f"{tag}_{n}"] for n in ("W1", "W2", "b1", "b2"))
        with nc.Block() as block:

            @block.sync
            def _(sp):
                st.set_semaphores(sp)
                with sp.Fori(0, tiles) as t:
                    e = t if tag == "L0" else sp.value_load(G["owner"][0:1, bass.ds(t, 1)], min_val=0, max_val=E - 1)
                    sp.wait_ge(hid_ready, past(t * FC))
                    alone(sp)
                    sp.dma_start(w1[:], W1[bass.ds(e, 1)].rearrange("e (c p) f -> p (e c) f", p=P)).then_inc(w1_in, 16)
                    sp.dma_start(b1[:], b1d[bass.ds(e, 1)].rearrange("e p c -> p (e c)")).then_inc(w1_in, 16)
                    sp.wait_ge(out_ps, past(t * TC))
                    alone(sp)
                    sp.dma_start(w2[:], W2[bass.ds(e, 1)].rearrange("e (c p) d -> p (e c) d", p=P)).then_inc(w2_in, 16)
                    sp.dma_start(b2[:], b2d[bass.ds(e, 1), :]).then_inc(w2_in, 16)
                if tag == "L0":
                    sp.wait_ge(added, 16 * tiles * TC)
                    sp.dma_start(G["x"][:], sums[0:N, :].rearrange("(c p) d -> p c d", p=P)).then_inc(x_in, 16)
                    sp.wait_ge(x_in, past(16))

            @block.gpsimd
            def _(pool):
                def fetch(t):
                    pool.tensor_copy(get[:], G["row"][:, bass.ds(t * TC, TC)]).then_inc(get_ready, 1)
                    pool.wait_ge(get_ready, past(t + 1))
                    alone(pool)
                    for c in range(TC):
                        pool.indirect_dma_start(
                            out=xg[:, c, :], out_offset=None, in_=rows,
                            in_offset=bass.IndirectOffsetOnAxis(ap=get[:, c:c + 1], axis=0)).then_inc(gathered, 16)

                fetch(0)
                with pool.Fori(0, tiles) as t:
                    pool.wait_ge(gathered, (t + 1) * TC * 16)
                    pool.wait_ge(turned, past(t + 1))
                    alone(pool)
                    fetch(t + 1)
                    pool.tensor_copy(put[:], G["row"][:, bass.ds(t * TC, TC)]).then_inc(put_ready, 1)
                    pool.wait_ge(put_ready, past(t + 1))
                    for c in range(TC):
                        pool.wait_ge(ys_ready, past(t * TC + c + 1))
                        if c:
                            pool.wait_ge(added, (t * TC + c) * 16)
                        alone(pool)
                        pool.indirect_dma_start(
                            out=sums, out_offset=bass.IndirectOffsetOnAxis(ap=put[:, c:c + 1], axis=0),
                            in_=ys[:, c, :], in_offset=None, compute_op=ALU.add).then_inc(added, 16)
                    pool.wait_ge(added, (t + 1) * TC * 16)
                    alone(pool)
                pool.wait_ge(gathered, (tiles + 1) * TC * 16)

            @block.tensor
            def _(pe):
                def turn_rows(n):
                    pe.wait_ge(gathered, n * TC * 16)
                    for m in range(DC):
                        for c in range(TC):
                            ins = pe.transpose(pt[m][:, c * P:(c + 1) * P], xg[:, c, m * P:(m + 1) * P], G["ident"][:])
                    ins.then_inc(turned, 1)

                turn_rows(1)
                with pe.Fori(0, tiles) as t:
                    pe.wait_ge(w1_in, past((t + 1) * 32))
                    pe.wait_ge(xgT_ready, past(t + 1))
                    for f in range(FC):
                        pe.wait_ge(hid_ready, past(t * FC + max(f - 1, 0)))
                        for m in range(DC):
                            mm = pe.matmul(ph[f % 2][:], w1[:, m, f * P:(f + 1) * P], xgT[:, m, :],
                                           start=m == 0, stop=m == DC - 1)
                        mm.then_inc(hid_ps, 1)
                    turn_rows(t + 2)
                    pe.wait_ge(hid_ready, past(t * FC + FC))
                    pe.wait_ge(w2_in, past((t + 1) * 32))
                    for c in range(TC):
                        pe.wait_ge(ys_ready, past(t * TC + max(c - 1, 0)))
                        pe.matmul(po[c % 2][:], G["ones"][0:1, :], b2[:], start=True, stop=False)
                        for f in range(FC):
                            mm = pe.matmul(po[c % 2][:], hid[:, f, c * P:(c + 1) * P], w2[:, f, :],
                                           start=False, stop=f == FC - 1)
                        mm.then_inc(out_ps, 1)

            @block.scalar
            def _(act):
                with act.Fori(0, tiles) as t:
                    act.wait_ge(out_ps, past(t * TC))
                    for f in range(FC):
                        act.wait_ge(hid_ps, past(t * FC + f + 1))
                        act.activation(hid[:, f, :], ph[f % 2][:], gelu, bias=b1[:, f:f + 1]).then_inc(hid_ready, 1)

            @block.vector
            def _(dve):
                def save_turned():
                    for m in range(DC):
                        ins = dve.tensor_copy(xgT[:, m, :], pt[m][:])
                    ins.then_inc(xgT_ready, 1)

                dve.wait_ge(turned, past(1))
                save_turned()
                with dve.Fori(0, tiles) as t:
                    dve.wait_ge(turned, past(t + 2))
                    dve.wait_ge(hid_ps, past(t * FC + FC))
                    save_turned()
                    dve.wait_ge(put_ready, past(t + 1))
                    for c in range(TC):
                        dve.wait_ge(out_ps, past(t * TC + c + 1))
                        dve.tensor_scalar(ys[:, c, :], po[c % 2][:], G["roww"][:, bass.ds(t * TC + c, 1)], None,
                                          ALU.mult).then_inc(ys_ready, 1)


def attention(nc, G, a, tag, self_):
    with ExitStack() as ctx:
        st = Stage(nc, ctx, "at" + tag)
        wq, wk, wv, wo = (st.sb(n, [P, DC, D]) for n in ("wq", "wk", "wv", "wo"))
        stats, mv, rstd = st.sb("stats", [P, CB, 6]), st.sb("mv", [P, CB, 2]), st.sb("rstd", [P, CB])
        xn, xnT = st.sb("xn", [P, CB, D]), st.sb("xnT", [P, DC, S])
        src = xnT if self_ else st.sb("src", [P, DC, S])
        parts = {}
        for n in "qk":
            parts[n] = [st.sb(f"{n}{k}", [P, DC, S], BF16) for k in range(3)]
            parts[n + "f"] = st.sb(f"{n}f", [P, DC, S])
        stack = {n: st.sb(f"{n}stack", [KR + 3, H, S], BF16) for n in "qk"}
        vals = st.sb("vals", [P, CB, H, 32])
        tops, neg, rest = (st.sb(n, [P, CB, HG]) for n in ("tops", "neg", "rest"))
        neg3 = st.sb("neg3", [P, CB, 3, HG], BF16)
        negT = st.sb("negT", [3 * HG, S], BF16)
        junk = st.sb("junk", [P, 2, S], BF16)
        prob = [st.sb(f"prob{i}", [P, 2, S]) for i in range(2)]
        outT, rec = st.sb("outT", [P, S]), st.sb("rec", [P, CB, HG])
        att, attT = st.sb("att", [P, CB, D]), st.sb("attT", [P, DC, S])
        pm = [st.ps(f"pm{i}", [P, S]) for i in range(2)]
        pe_ = [st.ps(f"pe{i}", [P, 2, S]) for i in range(2)]
        po, px = st.ps("po", [P, S]), st.ps("px", [P, S])
        pxb = px[:].bitcast(BF16)
        names = ("loaded", "src_in", "stats_ready", "rstd_ready", "xn_ready", "turned", "xnT_ready", "q_ps", "k_ps",
                 "v_ps", "qf_ready", "kf_ready", "v_ready", "q_cut", "k_cut", "stacked", "m_ps", "m_done", "neg_ready",
                 "negT_ps", "negT_ready", "neg_in", "s_ps", "p_ready", "pv_done", "o_saved", "oT_ps", "att_part",
                 "att_turned", "attT_ready", "y_ps", "x_ready", "vchain", "pchain", "cleared")
        s = {n: st.sem(n) for n in names}
        X = G["x"]
        NM, NE = CB * HG, CB * 2
        if self_:
            bq, bk = st.sb("bq", [P, DC]), st.sb("bk", [P, DC])
            bv, bo = st.sb("bv", [1, D]), st.sb("bo", [1, D])
            gain, shift = st.sb("gain", [P, D]), st.sb("shift", [P, D])
            yn = st.sb("yn", [P, CB, D])
            gw, gb = st.sb("gw", [P, DC, E]), st.sb("gb", [1, E])
            small = [st.sb(n, [P, CB]) for n in ("rtop", "rsum", "rrec")]
            wide = [st.sb(n, [P, CB, E]) for n in ("rshift", "rexp")]
            for n in ("logits_ps", "shift_ready", "rexp_ready", "x2_ready", "rows_stored"):
                s[n] = st.sem(n)
        NT = 2 if self_ else 1
        VPER = NG * 7 + (10 if self_ else 2)
        LOADS = 4 + (8 if self_ else 0)

        def rows(b):
            return lambda t: X[:, b * CB + t, :]

        with nc.Block() as block:

            @block.sync
            def _(sp):
                st.set_semaphores(sp)
                for dst, name in ((wq, "Wq"), (wk, "Wk"), (wv, "Wv"), (wo, "Wo")):
                    sp.dma_start(dst[:], a[f"{tag}_{name}"].rearrange("(c p) n -> p c n", p=P)).then_inc(s["loaded"], 16)
                if self_:
                    for dst, name in ((bq, "bq"), (bk, "bk")):
                        sp.dma_start(dst[:], a[f"{tag}_{name}"]).then_inc(s["loaded"], 16)
                    for dst, name in ((bv, "bv"), (bo, "bo"), (gb, "gate_b")):
                        sp.dma_start(dst[:], a[f"{tag}_{name}"]).then_inc(s["loaded"], 16)
                    for dst, name in ((gain, "ln1_g"), (shift, "ln1_b")):
                        sp.dma_start(dst[:], a[f"{tag}_{name}"].broadcast_to([P, D])).then_inc(s["loaded"], 16)
                    sp.dma_start(gw[:], a[f"{tag}_gate_w"].rearrange("(c p) n -> p c n", p=P)).then_inc(s["loaded"], 16)
                with sp.Fori(0, B) as b:
                    if not self_:
                        sp.wait_ge(s["v_ps"], past(b))
                        sp.dma_start(src[:], a["ctxT"].rearrange("(c p) n -> p c n", p=P)[:, :, bass.ds(b * S, S)]
                                     ).then_inc(s["src_in"], 16)
                    sp.wait_ge(s["pv_done"], past(b * NG * NE))
                    alone(sp)
                    for n, terms in (("k", K_TERMS), ("q", Q_TERMS)):
                        sp.wait_ge(s[n + "_cut"], past(b + 1))
                        for k, part in enumerate(terms):
                            for o in range(DC):
                                sp.dma_start(stack[n][16 * k:16 * k + 16, o * HC:(o + 1) * HC, :],
                                             parts[n][part][:, o, :]).then_inc(s["stacked"], 16)
                    for g in range(NG):
                        sp.wait_ge(s["negT_ready"], past(b * NG + g + 1))
                        for k in range(3):
                            sp.dma_start(stack["q"][KR + k:KR + k + 1, g * HG:(g + 1) * HG, :],
                                         negT[k * HG:(k + 1) * HG, :]).then_inc(s["neg_in"], 16)
                    if self_:
                        sp.wait_ge(s["x2_ready"], past(b + 1))
                        sp.dma_start(G["rows1"].rearrange("(c p) d -> p c d", p=P)[:, bass.ds(b * CB, CB), :], xn[:]
                                     ).then_inc(s["rows_stored"], 16)
                if self_:
                    sp.wait_ge(s["rows_stored"], past(16 * B))

            @block.tensor
            def _(pe):
                pe.wait_ge(s["loaded"], past(16 * LOADS))
                pe.wait_ge(s["cleared"], past(3))
                with pe.Fori(0, B) as b:
                    banks = (pm[0], pm[1])
                    pe.wait_ge(s["xn_ready"], past(b + 1))
                    turn(pe, G, lambda m: banks[m], lambda t, m: xn[:, t, m * P:(m + 1) * P]
                         ).then_inc(s["turned"], 1)
                    pe.wait_ge(s["xnT_ready"], past(b * NT + 1))
                    if not self_:
                        pe.wait_ge(s["src_in"], past(b * 16 + 16))
                    for w, x_, bank, done in ((wk, src, pe_[0], "k_ps"), (wq, xnT, pe_[1], "q_ps")):
                        for o in range(DC):
                            for m in range(DC):
                                mm = pe.matmul(bank[:, o, :], w[:, m, o * P:(o + 1) * P], x_[:, m, :],
                                               start=m == 0, stop=m == DC - 1)
                        mm.then_inc(s[done], 1)
                    for t in range(CB):
                        out = banks[t // 2][:, (t % 2) * D:(t % 2 + 1) * D]
                        if self_:
                            pe.matmul(out, G["ones"][0:1, :], bv[:], start=True, stop=False)
                        for m in range(DC):
                            mm = pe.matmul(out, src[:, m, t * P:(t + 1) * P], wv[:, m, :],
                                           start=m == 0 and not self_, stop=m == DC - 1)
                    mm.then_inc(s["v_ps"], 1)
                    pe.wait_ge(s["stacked"], past((b + 1) * 2 * len(Q_TERMS) * DC * 16))
                    pe.wait_ge(s["v_ready"], past(b + 1))

                    def max_step(g, n):
                        i = g * NM + n
                        h, t = g * HG + n % HG, n // HG
                        pe.wait_ge(s["m_done"], past(b * NG * NM + max(i - 1, 0)))
                        pe.matmul(pm[i % 2][:], stack["q"][0:KR, h, t * P:(t + 1) * P], stack["k"][0:KR, h, :],
                                  start=True, stop=True).then_inc(s["m_ps"], 1)

                    def max_rows(g):
                        pe.wait_ge(s["neg_ready"], past(b * NG + g + 1))
                        pe.wait_ge(s["att_part"], past(b * NG + max(g - 1, 0)))
                        for t in range(CB):
                            ins = pe.transpose(pxb[0:3 * HG, t * P:(t + 1) * P],
                                               neg3[:, t, :, :].rearrange("p k h -> p (k h)"), G["identb"][:])
                        ins.then_inc(s["negT_ps"], 1)

                    def score_step(g, n):
                        i = g * NE + n
                        kc, pair = n // 2, n % 2
                        pe.wait_ge(s["p_ready"], past(b * NG * NE + max(i - 1, 0)))
                        for j in range(2):
                            h = g * HG + pair * 2 + j
                            mm = pe.matmul(pe_[i % 2][:, j, :], stack["k"][0:KR + 3, h, kc * P:(kc + 1) * P],
                                           stack["q"][0:KR + 3, h, :], start=True, stop=self_)
                            if not self_:
                                mm = pe.matmul(pe_[i % 2][:, j, :], G["identb"][:], G["bias"][1][:, kc, :],
                                               start=False, stop=True)
                        mm.then_inc(s["s_ps"], 1)

                    def value_step(g, n):
                        i = g * NE + n
                        kc, pair = n // 2, n % 2
                        pe.wait_ge(s["p_ready"], past(b * NG * NE + i + 1))
                        if n == 0:
                            pe.wait_ge(s["o_saved"], past(b * NG + g))
                        for j in range(2):
                            r = (pair * 2 + j) * 32
                            mm = pe.matmul(po[r:r + 32, :], vals[:, kc, g * HG + pair * 2 + j, :],
                                           prob[i % 2][:, j, :], start=kc == 0, stop=kc == CB - 1)
                        mm.then_inc(s["pv_done"], 1)

                    for n in range(NM):
                        max_step(0, n)
                    max_rows(0)
                    for g in range(NG):
                        pe.wait_ge(s["neg_in"], past((b * NG + g + 1) * 48))
                        for n in range(NE):
                            score_step(g, n)
                            if g + 1 < NG:
                                max_step(g + 1, 2 * n)
                                max_step(g + 1, 2 * n + 1)
                            if n:
                                value_step(g, n - 1)
                        value_step(g, NE - 1)
                        if g + 1 < NG:
                            max_rows(g + 1)
                        pe.wait_ge(s["o_saved"], past(b * NG + g + 1))
                        pe.wait_ge(s["negT_ready"], past(b * NG + min(g + 2, NG)))
                        pe.wait_ge(s["att_part"], past(b * NG + g))
                        for t in range(CB):
                            ins = pe.transpose(px[:, t * P:(t + 1) * P], outT[:, t * P:(t + 1) * P], G["ident"][:])
                        ins.then_inc(s["oT_ps"], 1)
                    pe.wait_ge(s["att_part"], past((b + 1) * NG))
                    turn(pe, G, lambda m: banks[m], lambda t, m: att[:, t, m * P:(m + 1) * P]
                         ).then_inc(s["att_turned"], 1)
                    pe.wait_ge(s["attT_ready"], past(b + 1))
                    for t in range(CB):
                        out = pe_[0][:, t // 2, (t % 2) * D:(t % 2 + 1) * D]
                        if self_:
                            pe.matmul(out, G["ones"][0:1, :], bo[:], start=True, stop=False)
                        for m in range(DC):
                            mm = pe.matmul(out, attT[:, m, t * P:(t + 1) * P], wo[:, m, :],
                                           start=m == 0 and not self_, stop=m == DC - 1)
                    mm.then_inc(s["y_ps"], 1)
                    if self_:
                        pe.wait_ge(s["x2_ready"], past(b + 1))
                        turn(pe, G, lambda m: banks[m], lambda t, m: xn[:, t, m * P:(m + 1) * P]
                             ).then_inc(s["turned"], 1)
                        pe.wait_ge(s["xnT_ready"], past(b * NT + 2))
                        for t in range(CB):
                            out = px[:, t * E:(t + 1) * E]
                            pe.matmul(out, G["ones"][0:1, :], gb[:], start=True, stop=False)
                            for m in range(DC):
                                mm = pe.matmul(out, xnT[:, m, t * P:(t + 1) * P], gw[:, m, :],
                                               start=False, stop=m == DC - 1)
                        mm.then_inc(s["logits_ps"], 1)

            @block.scalar
            def _(act):
                with act.Fori(0, B) as b:
                    act.wait_ge(s["turned"], past(b * NT + 1))
                    for m in range(DC):
                        ins = act.copy(xnT[:, m, :], pm[m][:])
                    ins.then_inc(s["xnT_ready"], 1)
                    for n, bank, bias in (("k", pe_[0], bk if self_ else None), ("q", pe_[1], bq if self_ else None)):
                        act.wait_ge(s[n + "_ps"], past(b + 1))
                        act.wait_ge(s[n + "_cut"], past(b))
                        for o in range(DC):
                            if self_:
                                ins = act.activation(parts[n + "f"][:, o, :], bank[:, o, :], ACT.Identity,
                                                     bias=bias[:, o:o + 1])
                            else:
                                ins = act.copy(parts[n + "f"][:, o, :], bank[:, o, :])
                        ins.then_inc(s[n + "f_ready"], 1)
                    act.wait_ge(s["v_ps"], past(b + 1))
                    for k in range(2):
                        ins = act.copy(vals[:, 2 * k:2 * k + 2, :, 0:HD],
                                       pm[k][:].rearrange("p (t h d) -> p t h d", t=2, h=H))
                    ins.then_inc(s["v_ready"], 1)

                    def neg_rows(g):
                        act.wait_ge(s["negT_ps"], past(b * NG + g + 1))
                        act.wait_ge(s["neg_in"], past((b * NG + g) * 48))
                        act.copy(negT[:], pxb[0:3 * HG, 0:S]).then_inc(s["negT_ready"], 1)

                    neg_rows(0)
                    for g in range(NG):
                        for n in range(NE):
                            i = g * NE + n
                            act.wait_ge(s["s_ps"], past(b * NG * NE + i + 1))
                            act.wait_ge(s["pv_done"], past(b * NG * NE + max(i - 1, 0)))
                            act.activation(prob[i % 2][:], pe_[i % 2][:], ACT.Exp, scale=SCALE).then_inc(s["p_ready"], 1)
                        act.wait_ge(s["pv_done"], past(b * NG * NE + (g + 1) * NE))
                        act.wait_ge(s["oT_ps"], past(b * NG + g))
                        act.copy(outT[:], po[:]).then_inc(s["o_saved"], 1)
                        if g + 1 < NG:
                            neg_rows(g + 1)
                    act.wait_ge(s["att_turned"], past(b + 1))
                    act.wait_ge(s["y_ps"], past(b))
                    for m in range(DC):
                        ins = act.copy(attT[:, m, :], pm[m][:])
                    ins.then_inc(s["attT_ready"], 1)
                    if self_:
                        act.wait_ge(s["turned"], past(b * NT + 2))
                        for m in range(DC):
                            ins = act.copy(xnT[:, m, :], pm[m][:])
                        ins.then_inc(s["xnT_ready"], 1)
                        act.wait_ge(s["shift_ready"], past(b + 1))
                        act.activation(wide[1][:], wide[0][:], ACT.Exp).then_inc(s["rexp_ready"], 1)

            @block.gpsimd
            def _(pool):
                pool.memset(vals[:], 0.0).then_inc(s["cleared"], 1)
                pool.wait_ge(s["cleared"], past(1))
                pool.memset(vals[:, :, :, HD:HD + 1], 1.0).then_inc(s["cleared"], 1)
                pool.wait_ge(s["cleared"], past(2))
                pool.memset(stack["k"][KR:KR + 3, :, :], 1.0).then_inc(s["cleared"], 1)
                pool.wait_ge(s["cleared"], past(3))
                with pool.Fori(0, B) as b:
                    PPER = 2 * 3 + NT
                    chain = Chain(pool, s["pchain"], b * PPER)
                    pool.wait_ge(s["stats_ready"], past(b * NT + 1))
                    norm_rstd(pool, G, chain, mv, rstd).then_inc(s["rstd_ready"], 1)
                    for n in "kq":
                        full, (hi, mid, lo) = parts[n + "f"], parts[n]
                        pool.wait_ge(s[n + "f_ready"], past(b + 1))
                        pool.wait_ge(s["stacked"], past(b * 2 * len(Q_TERMS) * DC * 16))
                        alone(pool)
                        chain(pool.tensor_copy(hi[:], full[:]))
                        chain(pool.tensor_tensor(full[:], full[:], hi[:], ALU.subtract))
                        chain(pool.tensor_copy(mid[:], full[:]))
                        pool.tensor_tensor(lo[:], full[:], mid[:], ALU.subtract).then_inc(s[n + "_cut"], 1)
                    if self_:
                        pool.wait_ge(s["stats_ready"], past(b * NT + 2))
                        norm_rstd(pool, G, chain, mv, rstd).then_inc(s["rstd_ready"], 1)
                    assert chain.n == PPER

            @block.vector
            def _(dve):
                if self_:
                    dve.wait_ge(s["loaded"], past(16 * LOADS))
                with dve.Fori(0, B) as b:
                    chain = Chain(dve, s["vchain"], b * VPER)
                    norm_stats(dve, chain, stats, mv, rows(b)).then_inc(s["stats_ready"], 1)
                    dve.wait_ge(s["rstd_ready"], past(b * NT + 1))
                    dve.wait_ge(s["stats_ready"], past(b * NT + 1))
                    dve.wait_ge(s["turned"], past(b * NT))
                    if self_:
                        dve.wait_ge(s["rows_stored"], past(b * 16))
                    norm_apply(dve, lambda t: xn[:, t, :], rows(b), mv, rstd).then_inc(s["xn_ready"], 1)

                    def maxima(g, ns):
                        for n in ns:
                            i, t, j = g * NM + n, n // HG, n % HG
                            dve.wait_ge(s["m_ps"], past(b * NG * NM + i + 1))
                            if not self_:
                                alone(dve)
                            if self_:
                                ins = dve.tensor_reduce(tops[:, t, j:j + 1], pm[i % 2][:], AX.X, ALU.max)
                            else:
                                ins = dve.tensor_tensor_reduce(junk[:, i % 2, :], pm[i % 2][:], G["bias"][0][:, t, :], 1.0,
                                                               -BIG / 2, ALU.add, ALU.max, tops[:, t, j:j + 1])
                            ins.then_inc(s["m_done"], 1)

                    def cut_maxima(g):
                        dve.wait_ge(s["m_done"], past(b * NG * NM + (g + 1) * NM))
                        dve.wait_ge(s["negT_ps"], past(b * NG + g))
                        chain(dve.tensor_scalar(neg[:], tops[:], -1.0, None, ALU.mult))
                        chain(dve.tensor_copy(neg3[:, :, 0, :], neg[:]))
                        chain(dve.tensor_tensor(rest[:], neg[:], neg3[:, :, 0, :], ALU.subtract))
                        chain(dve.tensor_copy(neg3[:, :, 1, :], rest[:]))
                        chain(dve.tensor_tensor(neg3[:, :, 2, :], rest[:], neg3[:, :, 1, :], ALU.subtract))
                        dve.nop().then_inc(s["neg_ready"], 1)

                    def scale_outputs(g):
                        dve.wait_ge(s["oT_ps"], past(b * NG + g + 1))
                        view = px[:].rearrange("p (t h d) -> p t h d", t=CB, h=HG)
                        chain(dve.tensor_scalar(rec[:], view[:, :, :, HD], 1e-9, None, ALU.max))
                        dve.reciprocal(rec[:], rec[:]).then_inc(s["vchain"], 1)
                        chain.n += 1
                        dve.wait_ge(s["vchain"], past(chain.base + chain.n))
                        dve.tensor_tensor(att[:, :, g * HG * HD:(g + 1) * HG * HD].rearrange(
                            "p t (h d) -> p t h d", h=HG), view[:, :, :, 0:HD],
                            rec[:].unsqueeze(3).broadcast_to([P, CB, HG, HD]), ALU.mult).then_inc(s["att_part"], 1)

                    maxima(0, range(NM))
                    cut_maxima(0)
                    for g in range(NG):
                        if g + 1 < NG:
                            maxima(g + 1, range(NM))
                            cut_maxima(g + 1)
                        scale_outputs(g)
                    dve.wait_ge(s["y_ps"], past(b + 1))
                    view = pe_[0][:].rearrange("p a (t d) -> p (a t) d", t=2)
                    if not self_:
                        rr = X[:, bass.ds(b * CB, CB), :]
                        chain(dve.tensor_tensor(rr, rr, view, ALU.add))
                        assert chain.n == VPER
                    else:
                        alone(dve)
                        norm_stats(dve, chain, stats, mv, lambda t: view[:, t, :]).then_inc(s["stats_ready"], 1)
                        dve.wait_ge(s["rstd_ready"], past(b * NT + 2))
                        dve.wait_ge(s["stats_ready"], past(b * NT + 2))
                        chain(norm_apply(dve, lambda t: yn[:, t, :], lambda t: view[:, t, :], mv, rstd))
                        chain(dve.tensor_tensor(yn[:], yn[:], gain[:].unsqueeze(1).broadcast_to([P, CB, D]), ALU.mult))
                        chain(dve.tensor_tensor(yn[:], yn[:], shift[:].unsqueeze(1).broadcast_to([P, CB, D]), ALU.add))
                        rr = X[:, bass.ds(b * CB, CB), :]
                        chain(dve.tensor_tensor(xn[:], xn[:], yn[:], ALU.add))
                        dve.tensor_tensor(rr, rr, xn[:], ALU.add).then_inc(s["x2_ready"], 1)
                        dve.wait_ge(s["logits_ps"], past(b + 1))
                        router_dve(dve, chain, px[:, 0:CB * E].rearrange("p (t e) -> p t e", e=E), small, wide,
                                   s["rexp_ready"], b + 1, s["shift_ready"], G["prob"][:, bass.ds(b * CB, CB), :])
                        dve.wait_ge(s["x2_ready"], past(b + 1))
                        assert chain.n == VPER


def top_experts(nc, G):
    with ExitStack() as ctx:
        st = Stage(nc, ctx, "top")
        tiles = TILES["L1"]
        ahead, tie = st.sb("ahead", [P, NC, E, E]), st.sb("tie", [P, NC, E, E])
        rank, chosen, at, got = (st.sb(n, [P, E, NC]) for n in ("rank", "chosen", "at", "got"))
        front, scan, keep = (st.sb(n, [P, E * NC]) for n in ("front", "scan", "keep"))
        full = st.sb("full", [P, E, N // TILE])
        steps, size, first, last = (st.sb(n, [P, w]) for n, w in
                                    (("steps", N // TILE), ("size", E), ("first", E), ("last", E)))
        cross = st.sb("cross", [P, E, E])
        past_end, owner = st.sb("past_end", [1, tiles, E]), st.sb("owner", [1, tiles])
        pin, pall = st.ps("pin", [P, S]), st.ps("pall", [P, S])
        vchain, flagged, counted = (st.sem(n) for n in ("vchain", "flagged", "counted"))
        mine = G["prob"][:].unsqueeze(3).broadcast_to([P, NC, E, E])
        other = G["prob"][:].unsqueeze(2).broadcast_to([P, NC, E, E])

        def to(t, shape, axis):
            return t.unsqueeze(axis).broadcast_to(shape)

        with nc.Block() as block:

            @block.sync
            def _(sp):
                st.set_semaphores(sp)

            @block.tensor
            def _(pe):
                pe.wait_ge(flagged, past(1))
                in_front_pe(pe, G, pin, pall, chosen[:].rearrange("p e c -> p (e c)")).then_inc(counted, 1)

            @block.vector
            def _(dve):
                chain = Chain(dve, vchain)
                chain(dve.memset(keep[:], 1.0))
                chain(dve.memset(keep[:].rearrange("p (e c) -> p e c", c=NC)[:, :, 0:1], 0.0))
                chain(dve.tensor_tensor(ahead[:], other, mine, ALU.is_gt))
                chain(dve.tensor_tensor(tie[:], other, mine, ALU.is_equal))
                chain(dve.tensor_tensor(tie[:], tie[:], to(G["lower"][:], [P, NC, E, E], 1), ALU.mult))
                chain(dve.tensor_tensor(ahead[:], ahead[:], tie[:], ALU.add))
                chain(dve.tensor_reduce(rank[:].rearrange("p e c -> p c e"), ahead[:], AX.X, ALU.add))
                dve.tensor_scalar(chosen[:], rank[:], float(TOPK), None, ALU.is_lt).then_inc(flagged, 1)
                chain(dve.tensor_scalar(steps[:], G["lane"][:, 0:N // TILE], float(TILE), None, ALU.mult))
                dve.wait_ge(counted, past(1))
                in_front_dve(dve, chain, front, scan, keep, pin, pall)
                sizes = scan[:].rearrange("p (e c) -> p e c", c=NC)[:, :, NC - 1]
                chain(dve.tensor_tensor(full[:], to(sizes, [P, E, N // TILE], 2), to(steps[:], [P, E, N // TILE], 1),
                                        ALU.is_gt))
                chain(dve.tensor_reduce(size[:], full[:], AX.X, ALU.add))
                chain(dve.tensor_tensor(cross[:], G["lower"][:], to(size[:], [P, E, E], 1), ALU.mult))
                chain(dve.tensor_reduce(first[:], cross[:], AX.X, ALU.add))
                chain(dve.tensor_tensor(last[:], first[:], size[:], ALU.add))
                chain(dve.tensor_tensor(past_end[:], to(last[0:1, :], [1, tiles, E], 1),
                                        to(G["lane"][0:1, 0:tiles], [1, tiles, E], 2), ALU.is_le))
                chain(dve.tensor_reduce(owner[:], past_end[:], AX.X, ALU.add))
                chain(dve.tensor_scalar(G["owner"][:], owner[:], float(E - 1), None, ALU.min))
                chain(dve.scalar_tensor_tensor(out=at[:], in0=to(first[:], [P, E, NC], 2), scalar=float(TILE),
                                               in1=front[:].rearrange("p (e c) -> p e c", c=NC),
                                               op0=ALU.mult, op1=ALU.add))
                for k in range(TOPK):
                    for dst, src in ((G["place"], at[:]), (G["weight"], G["prob"][:].rearrange("p c e -> p e c"))):
                        chain(dve.scalar_tensor_tensor(out=got[:], in0=rank[:], scalar=float(k), in1=src,
                                                       op0=ALU.is_equal, op1=ALU.mult))
                        chain(dve.tensor_reduce(dst[:, k * NC:(k + 1) * NC], got[:].rearrange("p e c -> p c e"),
                                                AX.X, ALU.add))


def finish(nc, G, a, out):
    with ExitStack() as ctx:
        st = Stage(nc, ctx, "fin")
        stats, mv, rstd = st.sb("stats", [P, CB, 6]), st.sb("mv", [P, CB, 2]), st.sb("rstd", [P, CB])
        gain, shift, xn = st.sb("gain", [P, D]), st.sb("shift", [P, D]), st.sb("xn", [P, CB, D])
        loaded, stats_ready, rstd_ready, vchain, pchain, ready, stored = (
            st.sem(n) for n in ("loaded", "stats_ready", "rstd_ready", "vchain", "pchain", "ready", "stored"))
        X, Y, y_in = G["x"], st.sb("y", [P, NC, D]), st.sem("y_in")
        VPER = 4
        with nc.Block() as block:

            @block.sync
            def _(sp):
                st.set_semaphores(sp)
                sp.dma_start(gain[:], a["L1_ln2_g"].broadcast_to([P, D])).then_inc(loaded, 16)
                sp.dma_start(shift[:], a["L1_ln2_b"].broadcast_to([P, D])).then_inc(loaded, 16)
                for b in range(B):
                    sp.dma_start(Y[:, b * CB:(b + 1) * CB, :],
                                 G["sum1"][0:N, :].rearrange("(c p) d -> p c d", p=P)[:, b * CB:(b + 1) * CB, :]
                                 ).then_inc(y_in, 16)
                with sp.Fori(0, B) as b:
                    sp.wait_ge(ready, past(b + 1))
                    sp.dma_start(out.rearrange("b (c p) d -> p (b c) d", p=P)[:, bass.ds(b * CB, CB), :],
                                 X[:, bass.ds(b * CB, CB), :]).then_inc(stored, 16)
                sp.wait_ge(stored, past(16 * B))

            @block.gpsimd
            def _(pool):
                with pool.Fori(0, B) as b:
                    chain = Chain(pool, pchain, b)
                    pool.wait_ge(stats_ready, past(b + 1))
                    norm_rstd(pool, G, chain, mv, rstd).then_inc(rstd_ready, 1)

            @block.vector
            def _(dve):
                dve.wait_ge(loaded, past(32))
                dve.wait_ge(y_in, past(16 * B))
                with dve.Fori(0, B) as b:
                    chain = Chain(dve, vchain, b * VPER)
                    norm_stats(dve, chain, stats, mv, lambda t: Y[:, b * CB + t, :]).then_inc(stats_ready, 1)
                    dve.wait_ge(rstd_ready, past(b + 1))
                    dve.wait_ge(stats_ready, past(b + 1))
                    chain(norm_apply(dve, lambda t: xn[:, t, :], lambda t: Y[:, b * CB + t, :], mv, rstd))
                    chain(dve.tensor_tensor(xn[:], xn[:], gain[:].unsqueeze(1).broadcast_to([P, CB, D]), ALU.mult))
                    chain(dve.tensor_tensor(xn[:], xn[:], shift[:].unsqueeze(1).broadcast_to([P, CB, D]), ALU.add))
                    rr = X[:, bass.ds(b * CB, CB), :]
                    dve.tensor_tensor(rr, rr, xn[:], ALU.add).then_inc(ready, 1)
                    dve.wait_ge(ready, past(b + 1))
                    assert chain.n == VPER


def build(nc, a, out):
    with ExitStack() as ctx:
        def sb(name, shape, dt=F32):
            return ctx.enter_context(nc.sbuf_tensor(name, shape, dt))

        def dram(name, shape):
            return nc.dram_tensor(name, shape, F32, kind="Internal").ap()

        G = {
            "x": sb("x", [P, NC, D]),
            "ident": sb("ident", [P, P]), "identb": sb("identb", [P, P], BF16), "before": sb("before", [P, P]),
            "ones": sb("ones", [P, P]), "mhalf": sb("mhalf", [P, CB]), "lower": sb("lower", [P, E, E]),
            "lane": sb("lane", [P, P]), "token1": sb("token1", [P, NC]), "spare1": sb("spare1", [P, 1]),
            "bias": [sb(f"bias{i}", [P, CB, S], BF16) for i in range(2)],
            "ratio": sb("ratio", [P, DC, B]), "prob": sb("prob", [P, NC, E]),
            "place": sb("place", [P, E * NC]), "weight": sb("weight", [P, E * NC]),
            "row": sb("row", [P, COLS], U32), "roww": sb("roww", [P, COLS]),
            "owner": sb("owner", [1, TILES["L1"]], mybir.dt.int32),
            "rows0": dram("rows0", [N + P, D]), "rows1": dram("rows1", [N + P, D]),
            "sum0": dram("sum0", [N + P, D]), "sum1": dram("sum1", [N + P, D]),
        }
        setup(nc, G, a)
        aft_keys(nc, G, a)
        aft_tokens(nc, G, a)
        expert_choice(nc, G)
        lists(nc, G, "L0", E, NC, CAP // P)
        experts(nc, G, a, "L0", ACT.Gelu_apprx_tanh)
        attention(nc, G, a, "L1x", False)
        attention(nc, G, a, "L1", True)
        top_experts(nc, G)
        lists(nc, G, "L1", 1, TOPK * NC, COLS)
        experts(nc, G, a, "L1", ACT.Gelu)
        finish(nc, G, a, out)


def kernel(**inputs):
    import numpy as np
    import concourse.bacc as bacc
    from concourse.bass_utils import run_bass_kernel_spmd

    i = {k: np.asarray(v) for k, v in inputs.items()}
    mask = i["mask_SxS2_bk0"]

    def columns(v, n):
        return v.reshape(-1, n, P).swapaxes(-1, -2)

    by_row = np.arange(D).reshape(DC, HC, HD).swapaxes(1, 2).reshape(D)
    lay = {
        "x": i["x"], "ctxT": i["ctx_1024"].reshape(N, D).T, "mask": mask, "maskT": mask.T,
        "L0_WqT": i["L0_xattn_Wq"].T, "L0_WkT": i["L0_xattn_Wk"].T, "L0_WvT": i["L0_xattn_Wv"].T,
        "L0_WoT": i["L0_xattn_Wo"].T, "L0_Ws": i["L0_ffn_Ws"], "L0_bs": i["L0_ffn_bs"].reshape(1, E),
        "L1_Wq": i["L1_ffn_Wq"], "L1_Wk": i["L1_ffn_Wk"], "L1_Wv": i["L1_ffn_Wv"], "L1_Wo": i["L1_ffn_Wo"],
        "L1_bq": columns(i["L1_ffn_bq"][by_row], DC)[0], "L1_bk": columns(i["L1_ffn_bk"][by_row], DC)[0],
        "L1_gate_w": i["L1_ffn_gate_w"],
    }
    for n in ("Wq", "Wk", "Wv", "Wo"):
        lay["L1x_" + n] = i["L1_xattn_" + n].T
    for t in ("L1x", "L1"):
        for n in ("Wq", "Wk"):
            lay[f"{t}_{n}"] = lay[f"{t}_{n}"][:, by_row]
    for n in ("bv", "bo", "ln1_g", "ln1_b", "ln2_g", "ln2_b", "gate_b"):
        lay["L1_" + n] = i["L1_ffn_" + n].reshape(1, -1)
    for t in ("L0", "L1"):
        for n in ("W1", "W2", "b2"):
            lay[f"{t}_{n}"] = i[f"{t}_ffn_{n}"]
        lay[f"{t}_b1"] = columns(i[f"{t}_ffn_b1"], FC)

    nc = bacc.Bacc("TRN2", target_bir_lowering=False, num_devices=1)
    arrays, a = {}, {}
    for name, v in lay.items():
        v = np.ascontiguousarray(v)
        arrays["in_" + name] = v
        a[name] = nc.dram_tensor("in_" + name, v.shape, mybir.dt.from_np(v.dtype), kind="ExternalInput").ap()
    out = nc.dram_tensor("out", (B, S, D), F32, kind="ExternalOutput").ap()
    build(nc, a, out)
    r = run_bass_kernel_spmd(nc, [arrays], core_ids=[0])
    return r.results[0]["out"]
```

```python
from contextlib import ExitStack

import concourse.bass as bass
from concourse import mybir

F32 = mybir.dt.float32
BF16 = mybir.dt.bfloat16
U32 = mybir.dt.uint32
U8 = mybir.dt.uint8
ALU = mybir.AluOpType
ACT = mybir.ActivationFunctionType
AX = mybir.AxisListType

P = 128
B, S, D = 8, 512, 256
N = B * S
NC = N // P
CB = S // P
DC = D // P
E, F = 8, 1024
FC = F // P
H, HD = 16, 16
HG = 4
NG = H // HG
HC = H // DC
CAP = N // E
TOPK = 2
TILE = 512
TC = TILE // P
TILES = {"L0": E * CAP // TILE, "L1": (N * TOPK + E * (TILE - 1)) // TILE}
COLS = (TILES["L1"] + 1) * TC
SLAB = 16
BITS = 30
EPS = 1e-5
SCALE = HD ** -0.5
BIG = 2.0 ** 30
Q_TERMS = (0, 0, 1, 1, 0, 2)
K_TERMS = (0, 1, 0, 1, 2, 0)
KR = 16 * len(Q_TERMS)


def past(n):
    return n + 1


class Stage:

    def __init__(self, nc, ctx, tag):
        self.nc, self.ctx, self.tag, self.sems = nc, ctx, tag, []

    def sb(self, name, shape, dt=F32):
        return self.ctx.enter_context(self.nc.sbuf_tensor(f"{self.tag}_{name}", shape, dt))

    def ps(self, name, shape, dt=F32):
        return self.ctx.enter_context(self.nc.psum_tensor(f"{self.tag}_{name}", shape, dt))

    def sem(self, name):
        self.sems.append(self.ctx.enter_context(self.nc.semaphore(f"{self.tag}_{name}")))
        return self.sems[-1]

    def pool_dma_sem(self, name):
        return self.ctx.enter_context(self.nc.semaphore(f"{self.tag}_{name}"))

    def set_semaphores(self, sp):
        for s in self.sems:
            sp.sem_inc(s, 1)


def alone(eng):
    eng.nop(nofuse=True)


class Chain:

    def __init__(self, eng, sem, base=0):
        self.eng, self.sem, self.base, self.n = eng, sem, base, 0

    def __call__(self, ins):
        ins.then_inc(self.sem, 1)
        self.n += 1
        self.eng.wait_ge(self.sem, past(self.base + self.n))
        if not isinstance(self.base, int):
            alone(self.eng)


def setup(nc, G, a):
    with ExitStack() as ctx:
        st = Stage(nc, ctx, "setup")
        loaded, cleared, built, mask_in = (st.sem(n) for n in ("loaded", "cleared", "built", "mask_in"))
        vec, zeroed, stored, counted = (st.sem(n) for n in ("vec", "zeroed", "stored", "counted"))
        zero = st.sb("zero", [P, D])
        lane_i, token_i, spare_i = (st.sb(n, [P, w], mybir.dt.int32) for n, w in (("lane", P), ("tok", NC), ("spare", 1)))
        raw = [st.sb(f"mask_raw{i}", [P, CB, S], U8) for i in range(2)]
        with nc.Block() as block:

            @block.sync
            def _(sp):
                st.set_semaphores(sp)
                sp.dma_start(G["x"][:], a["x"].rearrange("b (c p) d -> p (b c) d", p=P)).then_inc(loaded, 16)
                sp.dma_start(raw[0][:], a["mask"].rearrange("(c p) k -> p c k", p=P)).then_inc(mask_in, 16)
                sp.dma_start(raw[1][:], a["maskT"].rearrange("(c p) k -> p c k", p=P)).then_inc(mask_in, 16)
                sp.wait_ge(loaded, past(16))
                sp.wait_ge(zeroed, past(1))
                for dst, first in ((G["sum1"], 0), (G["rows0"], NC), (G["rows1"], NC), (G["sum0"], NC)):
                    sp.dma_start(dst.rearrange("(c p) d -> p c d", p=P)[:, first:, :],
                                 zero[:].unsqueeze(1).broadcast_to([P, NC + 1 - first, D])).then_inc(stored, 16)
                sp.wait_ge(stored, past(64))

            @block.gpsimd
            def _(pool):
                pool.memset(G["ident"][:], 0.0).then_inc(cleared, 1)
                pool.memset(G["identb"][:], 0.0).then_inc(cleared, 1)
                pool.memset(G["before"][:], 1.0).then_inc(cleared, 1)
                pool.memset(G["ones"][:], 1.0).then_inc(built, 1)
                pool.memset(G["mhalf"][:], -0.5).then_inc(built, 1)
                pool.memset(G["lower"][:], 1.0).then_inc(cleared, 1)
                pool.wait_ge(cleared, past(4))
                for t in (G["ident"], G["identb"]):
                    pool.affine_select(out=t[:], in_=t[:], compare_op=ALU.not_equal, fill=1.0, base=0,
                                       pattern=[[-1, P]], channel_multiplier=1).then_inc(built, 1)
                pool.affine_select(out=G["before"][:], in_=G["before"][:], compare_op=ALU.is_gt, fill=0.0,
                                   base=0, pattern=[[1, P]], channel_multiplier=-1).then_inc(built, 1)
                pool.affine_select(out=G["lower"][:], in_=G["lower"][:], compare_op=ALU.is_gt, fill=0.0,
                                   base=0, pattern=[[1, E], [-1, E]], channel_multiplier=0).then_inc(built, 1)
                pool.wait_ge(built, past(6))
                pool.iota(lane_i[:], pattern=[[1, P]], base=0, channel_multiplier=0).then_inc(counted, 1)
                pool.iota(token_i[:], pattern=[[P, NC]], base=1, channel_multiplier=1).then_inc(counted, 1)
                pool.iota(spare_i[:], pattern=[[1, 1]], base=N + 1, channel_multiplier=1).then_inc(counted, 1)

            @block.vector
            def _(dve):
                dve.memset(zero[:], 0.0).then_inc(zeroed, 1)
                dve.wait_ge(counted, past(3))
                for dst, src in ((G["lane"], lane_i), (G["token1"], token_i), (G["spare1"], spare_i)):
                    dve.tensor_copy(dst[:], src[:]).then_inc(vec, 1)
                dve.wait_ge(mask_in, past(32))
                for i in range(2):
                    dve.tensor_scalar(G["bias"][i][:], raw[i][:], BIG, -BIG, ALU.mult, ALU.add).then_inc(vec, 1)
                dve.wait_ge(vec, past(5))


def aft_keys(nc, G, a):
    with ExitStack() as ctx:
        st = Stage(nc, ctx, "aft")
        ctxT = st.sb("ctxT", [P, DC, N])
        wk, wv = st.sb("wk", [P, DC, D]), st.sb("wv", [P, DC, D])
        keys = st.sb("keys", [P, DC, B, S])
        top = st.sb("top", [P, DC, S])
        diff, ex = st.sb("diff", [P, DC, S]), st.sb("ex", [P, DC, S])
        den, num, rden = st.sb("den", [P, DC]), st.sb("num", [P, DC]), st.sb("rden", [P, DC])
        pk = [st.ps(f"pk{i}", [P, S]) for i in range(DC)]
        pv = [st.ps(f"pv{i}", [P, S]) for i in range(DC)]
        loaded, keys_ps, keys_saved, keys_top = (st.sem(n) for n in ("loaded", "keys_ps", "keys_saved", "keys_top"))
        diff_ready, ex_ready, vals_ps, summed, dvec = (
            st.sem(n) for n in ("diff_ready", "ex_ready", "vals_ps", "summed", "dvec"))
        cleared = st.sem("cleared")
        with nc.Block() as block:

            @block.sync
            def _(sp):
                st.set_semaphores(sp)
                sp.dma_start(ctxT[:], a["ctxT"].rearrange("(c p) n -> p c n", p=P)).then_inc(loaded, 16)
                sp.dma_start(wk[:], a["L0_WkT"].rearrange("(c p) n -> p c n", p=P)).then_inc(loaded, 16)
                sp.dma_start(wv[:], a["L0_WvT"].rearrange("(c p) n -> p c n", p=P)).then_inc(loaded, 16)

            @block.tensor
            def _(pe):
                pe.wait_ge(loaded, past(48))
                with pe.Fori(0, B) as b:
                    pe.wait_ge(keys_saved, past(b * DC))
                    for o in range(DC):
                        for m in range(DC):
                            mm = pe.matmul(pk[o][:], wk[:, m, o * P:(o + 1) * P], ctxT[:, m, bass.ds(b * S, S)],
                                           start=m == 0, stop=m == DC - 1)
                        mm.then_inc(keys_ps, 1)
                with pe.Fori(0, B) as b:
                    pe.wait_ge(summed, past(b * DC))
                    for o in range(DC):
                        for m in range(DC):
                            mm = pe.matmul(pv[o][:], wv[:, m, o * P:(o + 1) * P], ctxT[:, m, bass.ds(b * S, S)],
                                           start=m == 0, stop=m == DC - 1)
                        mm.then_inc(vals_ps, 1)

            @block.scalar
            def _(act):
                with act.Fori(0, B) as b:
                    for o in range(DC):
                        act.wait_ge(keys_ps, past(b * DC + o + 1))
                        act.copy(keys[:, o, b, :], pk[o][:]).then_inc(keys_saved, 1)
                with act.Fori(0, B) as b:
                    act.wait_ge(diff_ready, past(b + 1))
                    act.wait_ge(summed, past(b * DC))
                    for o in range(DC):
                        act.activation(ex[:, o, :], diff[:, o, :], ACT.Exp,
                                       accum_out=den[:, o:o + 1]).then_inc(ex_ready, 1)

            @block.vector
            def _(dve):
                dve.memset(top[:], -3.0e38).then_inc(cleared, 1)
                dve.wait_ge(cleared, past(1))
                with dve.Fori(0, B) as b:
                    dve.wait_ge(keys_top, past(b * DC))
                    for o in range(DC):
                        dve.wait_ge(keys_saved, past(b * DC + o + 1))
                        dve.tensor_tensor(top[:, o, :], top[:, o, :], keys[:, o, b, :], ALU.max).then_inc(keys_top, 1)
                dve.wait_ge(keys_top, past(B * DC))
                dve.wait_ge(keys_saved, past(B * DC))
                with dve.Fori(0, B) as b:
                    dve.wait_ge(ex_ready, past(b * DC))
                    dve.tensor_tensor(diff[:], keys[:, :, b, :], top[:], ALU.subtract).then_inc(diff_ready, 1)
                    dve.wait_ge(dvec, past(b * 2))
                    for o in range(DC):
                        dve.wait_ge(ex_ready, past(b * DC + o + 1))
                        dve.wait_ge(vals_ps, past(b * DC + o + 1))
                        dve.tensor_tensor_reduce(ex[:, o, :], ex[:, o, :], pv[o][:], 1.0, 0.0, ALU.mult, ALU.add,
                                                 num[:, o:o + 1]).then_inc(summed, 1)
                    dve.reciprocal(rden[:], den[:]).then_inc(dvec, 1)
                    dve.wait_ge(dvec, past(b * 2 + 1))
                    dve.wait_ge(summed, past(b * DC + DC))
                    dve.tensor_tensor(G["ratio"][:, :, b], num[:], rden[:], ALU.mult).then_inc(dvec, 1)
                dve.wait_ge(dvec, past(2 * B))


def norm_stats(dve, chain, stats, mv, src):
    for t in range(CB):
        ins = dve.bn_stats(stats[:, t, :], src(t))
    chain(ins)
    for t in range(CB):
        ins = dve.bn_aggr(mv[:, t, :], stats[:, t, :])
    return ins


def norm_rstd(pool, G, chain, mv, rstd):
    alone(pool)
    chain(pool.tensor_scalar(rstd[:], mv[:, :, 1], EPS, None, ALU.add))
    return pool.tensor_tensor(rstd[:], rstd[:], G["mhalf"][:, 0:CB], ALU.pow)


def norm_apply(dve, dst, src, mv, rstd):
    for t in range(CB):
        ins = dve.tensor_scalar(dst(t), src(t), mv[:, t, 0:1], rstd[:, t:t + 1], ALU.subtract, ALU.mult)
    return ins


def turn(pe, G, bank, src):
    for m in range(DC):
        for t in range(CB):
            ins = pe.transpose(bank(m)[:, t * P:(t + 1) * P], src(t, m), G["ident"][:])
    return ins


def router_dve(dve, chain, logits, small, wide, exp_ready, ex_wait, psum_ready_inc, out):
    top, tot, rec = small
    shifted, ex = wide
    chain(dve.tensor_reduce(top[:], logits, AX.X, ALU.max))
    dve.tensor_tensor(shifted[:], logits, top[:].unsqueeze(2).broadcast_to([P, CB, E]),
                      ALU.subtract).then_inc(psum_ready_inc, 1)
    dve.wait_ge(exp_ready, past(ex_wait))
    chain(dve.tensor_reduce(tot[:], ex[:], AX.X, ALU.add))
    chain(dve.reciprocal(rec[:], tot[:]))
    chain(dve.tensor_tensor(out, ex[:], rec[:].unsqueeze(2).broadcast_to([P, CB, E]), ALU.mult))


def aft_tokens(nc, G, a):
    with ExitStack() as ctx:
        st = Stage(nc, ctx, "tok")
        wq, wo, ws = st.sb("wq", [P, DC, D]), st.sb("wo", [P, DC, D]), st.sb("ws", [P, DC, E])
        bs = st.sb("bs", [1, E])
        stats, mv, rstd = st.sb("stats", [P, CB, 6]), st.sb("mv", [P, CB, 2]), st.sb("rstd", [P, CB])
        xn, xnT, yT = st.sb("xn", [P, CB, D]), st.sb("xnT", [P, DC, S]), st.sb("yT", [P, DC, S])
        fxT = st.sb("fxT", [P, DC, S])
        small = [st.sb(n, [P, CB]) for n in ("rtop", "rsum", "rrec")]
        wide = [st.sb(n, [P, CB, E]) for n in ("rshift", "rexp")]
        pt = [st.ps(f"pt{i}", [P, S]) for i in range(DC)]
        pq = [st.ps(f"pq{i}", [P, S]) for i in range(DC)]
        po = [st.ps(f"po{i}", [P, 2, D]) for i in range(2)]
        pl = st.ps("pl", [P, S])
        names = ("loaded", "stats_ready", "rstd_ready", "xn_ready", "turned", "xnT_ready", "q_ps", "sig_ready",
                 "yT_ready", "out_ps", "x1_ready", "logits_ps", "shift_ready", "rexp_ready", "vchain", "pchain",
                 "x1_stored", "rows_stored")
        (loaded, stats_ready, rstd_ready, xn_ready, turned, xnT_ready, q_ps, sig_ready, yT_ready, out_ps, x1_ready,
         logits_ps, shift_ready, rexp_ready, vchain, pchain, x1_stored, rows_stored) = (st.sem(n) for n in names)
        X = G["x"]
        VPER, PPER = 6, 2

        with nc.Block() as block:

            @block.sync
            def _(sp):
                st.set_semaphores(sp)
                for dst, src in ((wq, "L0_WqT"), (wo, "L0_WoT"), (ws, "L0_Ws")):
                    sp.dma_start(dst[:], a[src].rearrange("(c p) n -> p c n", p=P)).then_inc(loaded, 16)
                sp.dma_start(bs[:], a["L0_bs"]).then_inc(loaded, 16)
                with sp.Fori(0, B) as b:
                    here = bass.ds(b * CB, CB)
                    sp.wait_ge(x1_ready, past(b + 1))
                    sp.dma_start(G["sum0"].rearrange("(c p) d -> p c d", p=P)[:, here, :], X[:, here, :]
                                 ).then_inc(x1_stored, 16)
                    sp.wait_ge(xn_ready, past(b * 2 + 2))
                    sp.dma_start(G["rows0"].rearrange("(c p) d -> p c d", p=P)[:, here, :], xn[:]
                                 ).then_inc(rows_stored, 16)
                sp.wait_ge(x1_stored, past(16 * B))
                sp.wait_ge(rows_stored, past(16 * B))

            @block.tensor
            def _(pe):
                pe.wait_ge(loaded, past(64))
                with pe.Fori(0, B) as b:
                    pe.wait_ge(xn_ready, past(b * 2 + 1))
                    turn(pe, G, lambda m: pt[m], lambda t, m: xn[:, t, m * P:(m + 1) * P]).then_inc(turned, 1)
                    pe.wait_ge(xnT_ready, past(b * 2 + 1))
                    for o in range(DC):
                        for m in range(DC):
                            mm = pe.matmul(pq[o][:], wq[:, m, o * P:(o + 1) * P], xnT[:, m, :],
                                           start=m == 0, stop=m == DC - 1)
                    mm.then_inc(q_ps, 1)
                    pe.wait_ge(yT_ready, past(b + 1))
                    for t in range(CB):
                        for m in range(DC):
                            mm = pe.matmul(po[t // 2][:, t % 2, :], yT[:, m, t * P:(t + 1) * P], wo[:, m, :],
                                           start=m == 0, stop=m == DC - 1)
                    mm.then_inc(out_ps, 1)
                    pe.wait_ge(xn_ready, past(b * 2 + 2))
                    turn(pe, G, lambda m: pt[m], lambda t, m: xn[:, t, m * P:(m + 1) * P]).then_inc(turned, 1)
                    pe.wait_ge(xnT_ready, past(b * 2 + 2))
                    for t in range(CB):
                        pe.matmul(pl[:, t * E:(t + 1) * E], G["ones"][0:1, :], bs[:], start=True, stop=False)
                        for m in range(DC):
                            mm = pe.matmul(pl[:, t * E:(t + 1) * E], fxT[:, m, t * P:(t + 1) * P], ws[:, m, :],
                                           start=False, stop=m == DC - 1)
                    mm.then_inc(logits_ps, 1)

            @block.scalar
            def _(act):
                with act.Fori(0, B) as b:
                    act.wait_ge(turned, past(b * 2 + 1))
                    for m in range(DC):
                        ins = act.copy(xnT[:, m, :], pt[m][:])
                    ins.then_inc(xnT_ready, 1)
                    act.wait_ge(q_ps, past(b + 1))
                    act.wait_ge(out_ps, past(b))
                    for o in range(DC):
                        ins = act.activation(yT[:, o, :], pq[o][:], ACT.Sigmoid)
                    ins.then_inc(sig_ready, 1)
                    act.wait_ge(turned, past(b * 2 + 2))
                    act.wait_ge(logits_ps, past(b))
                    for m in range(DC):
                        ins = act.copy(fxT[:, m, :], pt[m][:])
                    ins.then_inc(xnT_ready, 1)
                    act.wait_ge(shift_ready, past(b + 1))
                    act.activation(wide[1][:], wide[0][:], ACT.Exp).then_inc(rexp_ready, 1)

            @block.gpsimd
            def _(pool):
                with pool.Fori(0, B) as b:
                    chain = Chain(pool, pchain, b * PPER)
                    for k in range(2):
                        pool.wait_ge(stats_ready, past(b * 2 + k + 1))
                        norm_rstd(pool, G, chain, mv, rstd).then_inc(rstd_ready, 1)
                    assert chain.n == PPER

            @block.vector
            def _(dve):
                with dve.Fori(0, B) as b:
                    chain = Chain(dve, vchain, b * VPER)

                    def rows(t):
                        return X[:, b * CB + t, :]

                    def norm(k):
                        alone(dve)
                        norm_stats(dve, chain, stats, mv, rows).then_inc(stats_ready, 1)
                        dve.wait_ge(rstd_ready, past(b * 2 + k + 1))
                        dve.wait_ge(stats_ready, past(b * 2 + k + 1))
                        dve.wait_ge(turned, past(b * 2 + k))
                        if k == 0:
                            dve.wait_ge(rows_stored, past(b * 16))
                        norm_apply(dve, lambda t: xn[:, t, :], rows, mv, rstd).then_inc(xn_ready, 1)

                    norm(0)
                    dve.wait_ge(sig_ready, past(b + 1))
                    for o in range(DC):
                        ins = dve.tensor_scalar(yT[:, o, :], yT[:, o, :], G["ratio"][:, o, bass.ds(b, 1)], None,
                                                ALU.mult)
                    ins.then_inc(yT_ready, 1)
                    dve.wait_ge(out_ps, past(b + 1))
                    for k in range(2):
                        rr = X[:, bass.ds(b * CB + 2 * k, 2), :]
                        ins = dve.tensor_tensor(rr, rr, po[k][:], ALU.add)
                    ins.then_inc(x1_ready, 1)
                    dve.wait_ge(x1_ready, past(b + 1))
                    norm(1)
                    dve.wait_ge(logits_ps, past(b + 1))
                    router_dve(dve, chain, pl[:, 0:CB * E].rearrange("p (t e) -> p t e", e=E), small, wide,
                               rexp_ready, b + 1, shift_ready, G["prob"][:, bass.ds(b * CB, CB), :])
                    assert chain.n == VPER


def in_front_pe(pe, G, pin, pall, flags):
    pe.matmul(pin[:, 0:E * NC], G["before"][:], flags, start=True, stop=True)
    return pe.matmul(pall[:, 0:E * NC], G["ones"][:], flags, start=True, stop=True)


def in_front_dve(dve, chain, rank, scan, keep, pin, pall):
    chain(dve.tensor_tensor_scan(scan[:], keep[:], pall[:, 0:E * NC], 0.0, ALU.mult, ALU.add))
    chain(dve.tensor_tensor(rank[:], scan[:], pall[:, 0:E * NC], ALU.subtract))
    chain(dve.tensor_tensor(rank[:], rank[:], pin[:, 0:E * NC], ALU.add))


def expert_choice(nc, G):
    with ExitStack() as ctx:
        st = Stage(nc, ctx, "pick")
        low, cand, took = (st.sb(n, [P, E], U32) for n in ("low", "cand", "took"))
        bit = st.sb("bit", [P, 1], U32)
        cmp_, more, equal = (st.sb(n, [P, E, NC]) for n in ("cmp", "more", "equal"))
        cnt, need = st.sb("cnt", [P, E]), st.sb("need", [P, E])
        keep, rank, scan = (st.sb(n, [P, E * NC]) for n in ("keep", "rank", "scan"))
        ptot, pin, pall = st.ps("ptot", [P, S]), st.ps("pin", [P, S]), st.ps("pall", [P, S])
        vchain, counted, totalled = (st.sem(n) for n in ("vchain", "counted", "totalled"))
        prob = G["prob"][:].rearrange("p c e -> p e c")

        def wide(t):
            return t.unsqueeze(2).broadcast_to([P, E, NC])

        VPER, INIT = 6, 4
        with nc.Block() as block:

            @block.sync
            def _(sp):
                st.set_semaphores(sp)

            @block.vector
            def _(dve):
                chain = Chain(dve, vchain)
                chain(dve.memset(low[:], 0))
                chain(dve.memset(bit[:], 1 << (BITS - 1)))
                chain(dve.memset(keep[:], 1.0))
                chain(dve.memset(keep[:].rearrange("p (e c) -> p e c", c=NC)[:, :, 0:1], 0.0))
                assert chain.n == INIT
                with dve.Fori(0, BITS) as i:
                    c = Chain(dve, vchain, i * VPER + INIT)
                    c(dve.tensor_tensor(cand[:], low[:], bit[:].broadcast_to([P, E]), ALU.bitwise_or))
                    c(dve.tensor_tensor(cmp_[:], prob, wide(cand[:].bitcast(F32)), ALU.is_ge))
                    dve.tensor_reduce(cnt[:], cmp_[:], AX.X, ALU.add).then_inc(counted, 1)
                    dve.wait_ge(totalled, past(i + 1))
                    c(dve.scalar_tensor_tensor(out=took[:], in0=ptot[:, 0:E], scalar=float(CAP),
                                               in1=bit[:].broadcast_to([P, E]), op0=ALU.is_ge, op1=ALU.mult))
                    c(dve.tensor_tensor(low[:], low[:], took[:], ALU.bitwise_or))
                    c(dve.tensor_scalar(bit[:], bit[:], 1, None, ALU.logical_shift_right))
                    c(dve.nop())
                    assert c.n == VPER
                chain = Chain(dve, vchain, BITS * VPER + INIT)
                edge = wide(low[:].bitcast(F32))
                chain(dve.tensor_tensor(more[:], prob, edge, ALU.is_gt))
                chain(dve.tensor_tensor(equal[:], prob, edge, ALU.is_equal))
                dve.tensor_reduce(cnt[:], more[:], AX.X, ALU.add).then_inc(counted, 1)
                dve.wait_ge(totalled, past(BITS + 1))
                chain(dve.tensor_scalar(need[:], ptot[:, 0:E], -1.0, float(CAP), ALU.mult, ALU.add))
                in_front_dve(dve, chain, rank, scan, keep, pin, pall)
                rv = rank[:].rearrange("p (e c) -> p e c", c=NC)
                chain(dve.tensor_tensor(rv, rv, wide(need[:]), ALU.is_lt))
                chain(dve.tensor_tensor(rv, rv, equal[:], ALU.mult))
                dve.tensor_tensor(more[:], rv, more[:], ALU.add).then_inc(counted, 1)
                dve.wait_ge(counted, past(BITS + 2))
                dve.wait_ge(totalled, past(BITS + 2))
                in_front_dve(dve, chain, rank, scan, keep, pin, pall)
                chain(dve.scalar_tensor_tensor(out=rv, in0=rv, scalar=1.0, in1=more[:], op0=ALU.add, op1=ALU.mult))
                chain(dve.tensor_scalar(G["place"][:], rank[:], -1.0, None, ALU.add))
                chain(dve.tensor_copy(G["weight"][:].rearrange("p (e c) -> p e c", c=NC), prob))

            @block.tensor
            def _(pe):
                with pe.Fori(0, BITS) as i:
                    pe.wait_ge(counted, past(i + 1))
                    pe.matmul(ptot[:, 0:E], G["ones"][:], cnt[:], start=True, stop=True).then_inc(totalled, 1)
                pe.wait_ge(counted, past(BITS + 1))
                eq = equal[:].rearrange("p e c -> p (e c)")
                in_front_pe(pe, G, pin, pall, eq)
                pe.matmul(ptot[:, 0:E], G["ones"][:], cnt[:], start=True, stop=True).then_inc(totalled, 1)
                pe.wait_ge(counted, past(BITS + 2))
                in_front_pe(pe, G, pin, pall, more[:].rearrange("p e c -> p (e c)")).then_inc(totalled, 1)


def lists(nc, G, tag, sets, per, cols):
    with ExitStack() as ctx:
        st = Stage(nc, ctx, "li" + tag)
        n_all, I32 = sets * per, mybir.dt.int32
        whole, high, low = (st.sb(n, [P, n_all], I32) for n in ("whole", "high", "low"))
        highf, lowf = st.sb("highf", [P, n_all]), st.sb("lowf", [P, n_all])
        hot_low = [st.sb(f"hot_low{i}", [P, SLAB, P]) for i in range(2)]
        hot_high = st.sb("hot_high", [P, SLAB, cols])
        scaled = [st.sb(f"scaled{i}", [P, SLAB, 2, cols]) for i in range(2)]
        spare = st.sb("spare", [P, sets, cols])
        pt = st.ps("pt", [P, S])
        slabs = per // SLAB
        vchain, built, summed = (st.sem(n) for n in ("vchain", "built", "summed"))
        INIT, VPER = 7, 2 * slabs
        lane = G["lane"]
        with nc.Block() as block:

            @block.sync
            def _(sp):
                st.set_semaphores(sp)

            @block.vector
            def _(dve):
                chain = Chain(dve, vchain)
                chain(dve.tensor_copy(whole[:], G["place"][:, 0:n_all]))
                chain(dve.tensor_scalar(high[:], whole[:], 7, None, ALU.logical_shift_right))
                chain(dve.tensor_scalar(low[:], whole[:], P - 1, None, ALU.bitwise_and))
                chain(dve.tensor_copy(highf[:], high[:]))
                chain(dve.tensor_copy(lowf[:], low[:]))
                chain(dve.tensor_scalar(G["row"][:], G["spare1"][:].broadcast_to([P, COLS]), -1.0, None, ALU.add))
                chain(dve.memset(G["roww"][:], 0.0))
                assert chain.n == INIT
                with dve.Fori(0, sets) as r:
                    c = Chain(dve, vchain, r * VPER + INIT)
                    for s in range(slabs):
                        here, buf = bass.ds(r * per + s * SLAB, SLAB), s % 2
                        dve.wait_ge(summed, past(r * slabs + max(s - 1, 0)))

                        def chunks(t, width):
                            return t.unsqueeze(2).broadcast_to([P, SLAB, width])

                        c(dve.tensor_tensor(hot_low[buf][:], lane[:].unsqueeze(1).broadcast_to([P, SLAB, P]),
                                            chunks(lowf[:, here], P), ALU.is_equal))
                        c(dve.tensor_tensor(hot_high[:], lane[:, 0:cols].unsqueeze(1).broadcast_to([P, SLAB, cols]),
                                            chunks(highf[:, here], cols), ALU.is_equal))
                        first = s * SLAB % NC
                        dve.tensor_tensor(scaled[buf][:, :, 0, :], hot_high[:],
                                          chunks(G["token1"][:, first:first + SLAB], cols), ALU.mult
                                          ).then_inc(built, 1)
                        dve.tensor_tensor(scaled[buf][:, :, 1, :], hot_high[:],
                                          chunks(G["weight"][:, here], cols), ALU.mult).then_inc(built, 1)
                        dve.wait_ge(built, past(r * slabs * 2 + s * 2 + 2))
                        alone(dve)
                    assert c.n == VPER
                dve.wait_ge(summed, past(sets * slabs))
                chain = Chain(dve, vchain, sets * VPER + INIT)
                view = pt[:, 0:sets * 2 * cols].rearrange("p (r k c) -> p r k c", k=2, c=cols)
                chain(dve.tensor_scalar(spare[:], view[:, :, 0, :], 0.0, G["spare1"][:, 0:1], ALU.is_equal, ALU.mult))
                chain(dve.scalar_tensor_tensor(
                    out=G["row"][:, 0:sets * cols].rearrange("p (r c) -> p r c", c=cols), in0=view[:, :, 0, :],
                    scalar=-1.0, in1=spare[:], op0=ALU.add, op1=ALU.add))
                chain(dve.tensor_copy(G["roww"][:, 0:sets * cols].rearrange("p (r c) -> p r c", c=cols),
                                      view[:, :, 1, :]))

            @block.tensor
            def _(pe):
                with pe.Fori(0, sets) as r:
                    for s in range(slabs):
                        pe.wait_ge(built, past(r * slabs * 2 + s * 2 + 2))
                        alone(pe)
                        for i in range(SLAB):
                            mm = pe.matmul(pt[:, bass.ds(r * 2 * cols, 2 * cols)], hot_low[s % 2][:, i, :],
                                           scaled[s % 2][:, i, :, :].rearrange("p k c -> p (k c)"),
                                           start=s == 0 and i == 0, stop=s == slabs - 1 and i == SLAB - 1)
                        mm.then_inc(summed, 1)


def experts(nc, G, a, tag, gelu):
    rows, sums, tiles = G["rows" + tag[1]], G["sum" + tag[1]], TILES[tag]
    with ExitStack() as ctx:
        st = Stage(nc, ctx, "ex" + tag)
        w1, w2 = st.sb("w1", [P, DC, F]), st.sb("w2", [P, FC, D])
        b1, b2 = st.sb("b1", [P, FC]), st.sb("b2", [1, D])
        get, put = st.sb("get", [P, TC], U32), st.sb("put", [P, TC], U32)
        xg, xgT = st.sb("xg", [P, TC, D]), st.sb("xgT", [P, DC, TILE])
        hid, ys = st.sb("hid", [P, FC, TILE]), st.sb("ys", [P, TC, D])
        pt = [st.ps(f"pt{i}", [P, TILE]) for i in range(DC)]
        ph = [st.ps(f"ph{i}", [P, TILE]) for i in range(2)]
        po = [st.ps(f"po{i}", [P, D]) for i in range(2)]
        names = ("w1_in", "w2_in", "get_ready", "turned", "xgT_ready", "hid_ps", "hid_ready", "out_ps", "ys_ready",
                 "put_ready", "x_in")
        (w1_in, w2_in, get_ready, turned, xgT_ready, hid_ps, hid_ready, out_ps, ys_ready, put_ready,
         x_in) = (st.sem(n) for n in names)
        gathered, added = st.pool_dma_sem("gathered"), st.pool_dma_sem("added")
        W1, W2, b1d, b2d = (a[f"{tag}_{n}"] for n in ("W1", "W2", "b1", "b2"))
        with nc.Block() as block:

            @block.sync
            def _(sp):
                st.set_semaphores(sp)
                with sp.Fori(0, tiles) as t:
                    e = t if tag == "L0" else sp.value_load(G["owner"][0:1, bass.ds(t, 1)], min_val=0, max_val=E - 1)
                    sp.wait_ge(hid_ready, past(t * FC))
                    alone(sp)
                    sp.dma_start(w1[:], W1[bass.ds(e, 1)].rearrange("e (c p) f -> p (e c) f", p=P)).then_inc(w1_in, 16)
                    sp.dma_start(b1[:], b1d[bass.ds(e, 1)].rearrange("e p c -> p (e c)")).then_inc(w1_in, 16)
                    sp.wait_ge(out_ps, past(t * TC))
                    alone(sp)
                    sp.dma_start(w2[:], W2[bass.ds(e, 1)].rearrange("e (c p) d -> p (e c) d", p=P)).then_inc(w2_in, 16)
                    sp.dma_start(b2[:], b2d[bass.ds(e, 1), :]).then_inc(w2_in, 16)
                if tag == "L0":
                    sp.wait_ge(added, 16 * tiles * TC)
                    sp.dma_start(G["x"][:], sums[0:N, :].rearrange("(c p) d -> p c d", p=P)).then_inc(x_in, 16)
                    sp.wait_ge(x_in, past(16))

            @block.gpsimd
            def _(pool):
                def fetch(t):
                    pool.tensor_copy(get[:], G["row"][:, bass.ds(t * TC, TC)]).then_inc(get_ready, 1)
                    pool.wait_ge(get_ready, past(t + 1))
                    alone(pool)
                    for c in range(TC):
                        pool.indirect_dma_start(
                            out=xg[:, c, :], out_offset=None, in_=rows,
                            in_offset=bass.IndirectOffsetOnAxis(ap=get[:, c:c + 1], axis=0)).then_inc(gathered, 16)

                fetch(0)
                with pool.Fori(0, tiles) as t:
                    pool.wait_ge(gathered, (t + 1) * TC * 16)
                    pool.wait_ge(turned, past(t + 1))
                    alone(pool)
                    fetch(t + 1)
                    pool.tensor_copy(put[:], G["row"][:, bass.ds(t * TC, TC)]).then_inc(put_ready, 1)
                    pool.wait_ge(put_ready, past(t + 1))
                    for c in range(TC):
                        pool.wait_ge(ys_ready, past(t * TC + c + 1))
                        if c:
                            pool.wait_ge(added, (t * TC + c) * 16)
                        alone(pool)
                        pool.indirect_dma_start(
                            out=sums, out_offset=bass.IndirectOffsetOnAxis(ap=put[:, c:c + 1], axis=0),
                            in_=ys[:, c, :], in_offset=None, compute_op=ALU.add).then_inc(added, 16)
                    pool.wait_ge(added, (t + 1) * TC * 16)
                    alone(pool)
                pool.wait_ge(gathered, (tiles + 1) * TC * 16)

            @block.tensor
            def _(pe):
                def turn_rows(n):
                    pe.wait_ge(gathered, n * TC * 16)
                    for m in range(DC):
                        for c in range(TC):
                            ins = pe.transpose(pt[m][:, c * P:(c + 1) * P], xg[:, c, m * P:(m + 1) * P], G["ident"][:])
                    ins.then_inc(turned, 1)

                turn_rows(1)
                with pe.Fori(0, tiles) as t:
                    pe.wait_ge(w1_in, past((t + 1) * 32))
                    pe.wait_ge(xgT_ready, past(t + 1))
                    for f in range(FC):
                        pe.wait_ge(hid_ready, past(t * FC + max(f - 1, 0)))
                        for m in range(DC):
                            mm = pe.matmul(ph[f % 2][:], w1[:, m, f * P:(f + 1) * P], xgT[:, m, :],
                                           start=m == 0, stop=m == DC - 1)
                        mm.then_inc(hid_ps, 1)
                    turn_rows(t + 2)
                    pe.wait_ge(hid_ready, past(t * FC + FC))
                    pe.wait_ge(w2_in, past((t + 1) * 32))
                    for c in range(TC):
                        pe.wait_ge(ys_ready, past(t * TC + max(c - 1, 0)))
                        pe.matmul(po[c % 2][:], G["ones"][0:1, :], b2[:], start=True, stop=False)
                        for f in range(FC):
                            mm = pe.matmul(po[c % 2][:], hid[:, f, c * P:(c + 1) * P], w2[:, f, :],
                                           start=False, stop=f == FC - 1)
                        mm.then_inc(out_ps, 1)

            @block.scalar
            def _(act):
                with act.Fori(0, tiles) as t:
                    act.wait_ge(out_ps, past(t * TC))
                    for f in range(FC):
                        act.wait_ge(hid_ps, past(t * FC + f + 1))
                        act.activation(hid[:, f, :], ph[f % 2][:], gelu, bias=b1[:, f:f + 1]).then_inc(hid_ready, 1)

            @block.vector
            def _(dve):
                def save_turned():
                    for m in range(DC):
                        ins = dve.tensor_copy(xgT[:, m, :], pt[m][:])
                    ins.then_inc(xgT_ready, 1)

                dve.wait_ge(turned, past(1))
                save_turned()
                with dve.Fori(0, tiles) as t:
                    dve.wait_ge(turned, past(t + 2))
                    dve.wait_ge(hid_ps, past(t * FC + FC))
                    save_turned()
                    dve.wait_ge(put_ready, past(t + 1))
                    for c in range(TC):
                        dve.wait_ge(out_ps, past(t * TC + c + 1))
                        dve.tensor_scalar(ys[:, c, :], po[c % 2][:], G["roww"][:, bass.ds(t * TC + c, 1)], None,
                                          ALU.mult).then_inc(ys_ready, 1)


ROUND = CB * HG
LAG = 2


def job_table(self_, first, last):
    jobs = [(0, 3, "d", "neg1"), (1, 3, "d", "neg2"), (2, 3, "d", "neg3"),
            (1, 9, "d", "out0"), (2, 5, "d", "out1"), (3, 5, "d", "out2")]
    if not last:
        jobs += [(0, 8, "a", "turn0+"), (0, 10, "a", "turn1+"), (0, 12, "a", "k0+"), (0, 14, "a", "q0+"),
                 (1, 4, "a", "k1+"), (1, 6, "a", "q1+"), (1, 8, "a", "v0+"), (1, 10, "a", "v1+"),
                 (3, 3, "d", "neg0+")]
    if not first:
        jobs += [(0, 5, "d", "out3-"), (1, 0, "a", "att0-"), (1, 2, "a", "att1-"),
                 (1, 5, "d", "y0-"), (1, 7, "d", "y1-")]
        if self_:
            jobs += [(2, 8, "a", "u0-"), (2, 10, "a", "u1-"), (2, 14, "d", "logits-")]
    return sorted(jobs)


class Jobs:

    BEFORE = {"a": ["turn0+", "turn1+", "k0+", "q0+", "k1+", "q1+", "v0+", "v1+"], "d": ["neg0+"]}
    BEHIND = {"d": ["out3-", "y0-", "y1-"], "a": ["att0-", "att1-"]}

    def __init__(self, self_):
        names = {k: {bank: [n for _, _, b, n in job_table(self_, *k) if b == bank] for bank in "ad"}
                 for k in ((True, False), (False, False), (False, True))}
        self.names, self.self_ = names, self_

    def base(self, bank, b):
        if isinstance(b, int) and b == 0:
            return len(self.BEFORE[bank])
        return (b - 1) * len(self.names[False, False][bank]) + (
            len(self.BEFORE[bank]) + len(self.names[True, False][bank]))

    def index(self, bank, b, first, last, name):
        return self.base(bank, b) + self.names[first, last][bank].index(name)

    def behind(self, bank):
        return self.base(bank, B - 1) + len(self.names[False, True][bank])


def attention(nc, G, a, tag, self_):
    with ExitStack() as ctx:
        st = Stage(nc, ctx, "at" + tag)
        wq, wk, wv, wo = (st.sb(n, [P, DC, D]) for n in ("wq", "wk", "wv", "wo"))
        stats, mv, rstd = st.sb("stats", [P, CB, 6]), st.sb("mv", [P, CB, 2]), st.sb("rstd", [P, CB])
        xn, xnT = st.sb("xn", [P, CB, D]), st.sb("xnT", [P, DC, S])
        src = xnT if self_ else st.sb("src", [P, DC, S])
        full = {n: st.sb(f"{n}f", [P, DC, S]) for n in "qk"}
        parts = {n: [st.sb(f"{n}{k}", [P, DC, S], BF16) for k in range(3)] for n in "qk"}
        stack = {n: [st.sb(f"{n}stack{i}", [KR + 3, H, S], BF16) for i in range(2)] for n in "qk"}
        vals = [st.sb(f"vals{i}", [P, CB, H, 32]) for i in range(2)]
        tops, neg, rest = (st.sb(n, [P, CB, HG]) for n in ("tops", "neg", "rest"))
        neg3 = st.sb("neg3", [P, CB, 3, HG], BF16)
        negT = st.sb("negT", [3 * HG, S], BF16)
        prob = [st.sb(f"prob{i}", [P, S]) for i in range(4)]
        outT, rec = st.sb("outT", [P, S]), st.sb("rec", [P, CB, HG])
        att, attT = st.sb("att", [P, CB, D]), st.sb("attT", [P, DC, S])
        pm = [st.ps(f"pm{i}", [P, S]) for i in range(2)]
        ps = [st.ps(f"ps{i}", [P, S]) for i in range(2)]
        po = [st.ps(f"po{i}", [P, S]) for i in range(2)]
        pj = {bank: st.ps("pj" + bank, [P, S]) for bank in "ad"}
        names = ["loaded", "src_in", "stats_ready", "rstd_ready", "xn_ready", "cut0", "cut1", "stacked0", "stacked1",
                 "m_ps", "m_done", "neg_ready", "neg_in", "s_ps", "p_ready", "pv_done", "o_saved", "job_a", "job_d",
                 "free_a", "free_d", "vchain", "pchain", "cleared"]
        if self_:
            names += ["y_stats", "y_rstd", "u_ready", "rows_stored", "shift_ready", "rexp_ready", "u_kept", "xn_kept"]
            bq, bk = st.sb("bq", [P, DC]), st.sb("bk", [P, DC])
            bv, bo = st.sb("bv", [1, D]), st.sb("bo", [1, D])
            gain, shift = st.sb("gain", [P, D]), st.sb("shift", [P, D])
            gw, gb = st.sb("gw", [P, DC, E]), st.sb("gb", [1, E])
            small = [st.sb(n, [P, CB]) for n in ("rtop", "rsum", "rrec")]
            wide = [st.sb(n, [P, CB, E]) for n in ("rshift", "rexp")]
            ukept = [st.sb(f"ukept{i}", [P, CB, D]) for i in range(2)]
            yn, u2 = st.sb("yn", [P, CB, D]), st.sb("u2", [P, CB, D])
            uT = st.sb("uT", [P, DC, S])
            ymv, yrstd = st.sb("ymv", [P, CB, 2]), st.sb("yrstd", [P, CB])
            bias = {"q": bq, "k": bk}
        else:
            junk = st.sb("junk", [P, 2, S], BF16)
        s = {n: st.sem(n) for n in names}
        X, J = G["x"], Jobs(self_)
        PER = NG * ROUND
        LOADS = 4 + (8 if self_ else 0)
        QK = ("k", "q") * 2

        def first_last(b):
            return (isinstance(b, int) and b == 0, isinstance(b, int) and b == B - 1)

        def run(eng, before, batch, behind):
            before()
            batch(0, 0)
            with eng.Fori(0, (B - 2) // 2) as pair:
                batch(pair * 2 + 1, 1)
                batch(pair * 2 + 2, 0)
            batch(B - 1, 1)
            behind()

        def jobs_at(b, g, step, bank=None):
            return [(k, n) for (jg, js, k, n) in job_table(self_, *first_last(b))
                    if (jg, js) == (g, step) and bank in (None, k)]

        def job_index(bank, b, name):
            return J.index(bank, b, *first_last(b), name)

        with nc.Block() as block:

            @block.sync
            def _(sp):
                st.set_semaphores(sp)
                for dst, name in ((wk, "Wk"), (wq, "Wq"), (wv, "Wv"), (wo, "Wo")):
                    sp.dma_start(dst[:], a[f"{tag}_{name}"].rearrange("(c p) n -> p c n", p=P)).then_inc(s["loaded"], 16)
                if self_:
                    for dst, name in ((bq, "bq"), (bk, "bk")):
                        sp.dma_start(dst[:], a[f"{tag}_{name}"]).then_inc(s["loaded"], 16)
                    for dst, name in ((bv, "bv"), (bo, "bo"), (gb, "gate_b")):
                        sp.dma_start(dst[:], a[f"{tag}_{name}"]).then_inc(s["loaded"], 16)
                    for dst, name in ((gain, "ln1_g"), (shift, "ln1_b")):
                        sp.dma_start(dst[:], a[f"{tag}_{name}"].broadcast_to([P, D])).then_inc(s["loaded"], 16)
                    sp.dma_start(gw[:], a[f"{tag}_gate_w"].rearrange("(c p) n -> p c n", p=P)).then_inc(s["loaded"], 16)

                def load_source(b):
                    if not self_:
                        sp.dma_start(src[:], a["ctxT"].rearrange("(c p) n -> p c n", p=P)[:, :, bass.ds(b * S, S)]
                                     ).then_inc(s["src_in"], 16)

                def fill(b, par, o):
                    for i, (n, terms) in enumerate((("k", K_TERMS), ("q", Q_TERMS))):
                        sp.wait_ge(s[f"cut{o}"], past(b * 2 + i + 1))
                        for k, part in enumerate(terms):
                            sp.dma_start(stack[n][par][16 * k:16 * k + 16, o * HC:(o + 1) * HC, :],
                                         parts[n][part][:, o, :]).then_inc(s[f"stacked{o}"], 16)

                def negatives(b, par, g, index):
                    sp.wait_ge(s["free_d"], past(index + 1))
                    sp.dma_start(stack["q"][par][KR:KR + 3, g * HG:(g + 1) * HG, :], negT[:]).then_inc(s["neg_in"], 16)

                def store_rows(b):
                    sp.wait_ge(s["u_ready"], past(b + 1))
                    sp.dma_start(G["rows1"].rearrange("(c p) d -> p c d", p=P)[:, bass.ds(b * CB, CB), :], u2[:]
                                 ).then_inc(s["rows_stored"], 16)

                def before():
                    load_source(0)
                    fill(0, 0, 0)
                    fill(0, 0, 1)
                    negatives(0, 0, 0, 0)

                def batch(b, par):
                    first, last = first_last(b)
                    if not last and not self_:
                        sp.wait_ge(s["job_a"], past(J.base("a", b)))
                        alone(sp)
                        load_source(b + 1)
                    negatives(b, par, 1, job_index("d", b, "neg1"))
                    if not last:
                        sp.wait_ge(s["s_ps"], past(b * PER))
                        fill(b + 1, 1 - par, 0)
                    negatives(b, par, 2, job_index("d", b, "neg2"))
                    if not last:
                        fill(b + 1, 1 - par, 1)
                    if self_ and not first:
                        store_rows(b - 1)
                    negatives(b, par, 3, job_index("d", b, "neg3"))
                    if not last:
                        negatives(b + 1, 1 - par, 0, job_index("d", b, "neg0+"))

                def behind():
                    if self_:
                        store_rows(B - 1)
                        sp.wait_ge(s["rows_stored"], past(16 * B))

                run(sp, before, batch, behind)

            @block.tensor
            def _(pe):
                def turn_chunk(bank, rows_, m):
                    for t in range(CB):
                        ins = pe.transpose(pj[bank][:, t * P:(t + 1) * P], rows_[:, t, m * P:(m + 1) * P], G["ident"][:])
                    return ins

                def project(w, x_, o):
                    for m in range(DC):
                        mm = pe.matmul(pj["a"][:], w[:, m, o * P:(o + 1) * P], x_[:, m, :],
                                       start=m == 0, stop=m == DC - 1)
                    return mm

                def by_token(bank, xT_, w, row, half):
                    for i in range(2):
                        t, out = half * 2 + i, pj[bank][:, i * D:(i + 1) * D]
                        if row is not None:
                            pe.matmul(out, G["ones"][0:1, :], row[:], start=True, stop=False)
                        for m in range(DC):
                            mm = pe.matmul(out, xT_[:, m, t * P:(t + 1) * P], w[:, m, :],
                                           start=m == 0 and row is None, stop=m == DC - 1)
                    return mm

                def job(b, bank, name, index):
                    kind, i = name[:-1] if name[-1] in "+-" else name, 0
                    kind, i = (kind, 0) if kind == "logits" else (kind[:-1], int(kind[-1]))
                    if not (isinstance(index, int) and index == 0):
                        pe.wait_ge(s["free_" + bank], past(index))
                    if kind == "turn":
                        pe.wait_ge(s["xn_ready"], past(b + 1))
                        ins = turn_chunk("a", xn, i)
                    elif kind in ("k", "q"):
                        if kind == "k" and not self_:
                            pe.wait_ge(s["src_in"], past((b + 1) * 16))
                        ins = project({"k": wk, "q": wq}[kind], {"k": src, "q": xnT}[kind], i)
                    elif kind == "v":
                        ins = by_token("a", src, wv, bv if self_ else None, i)
                    elif kind == "neg":
                        pe.wait_ge(s["neg_ready"], past(b * NG + i + 1))
                        for t in range(CB):
                            ins = pe.transpose(pj["d"][:].bitcast(BF16)[0:3 * HG, t * P:(t + 1) * P],
                                               neg3[:, t, :, :].rearrange("p k h -> p (k h)"), G["identb"][:])
                    elif kind == "out":
                        pe.wait_ge(s["o_saved"], past(b * NG + i + 1))
                        for t in range(CB):
                            ins = pe.transpose(pj["d"][:, t * P:(t + 1) * P], outT[:, t * P:(t + 1) * P], G["ident"][:])
                    elif kind == "att":
                        ins = turn_chunk("a", att, i)
                    elif kind == "y":
                        ins = by_token("d", attT, wo, bo if self_ else None, i)
                    elif kind == "u":
                        pe.wait_ge(s["u_ready"], past(b + 1))
                        ins = turn_chunk("a", u2, i)
                    else:
                        for t in range(CB):
                            out = pj["d"][:, t * E:(t + 1) * E]
                            pe.matmul(out, G["ones"][0:1, :], gb[:], start=True, stop=False)
                            for m in range(DC):
                                ins = pe.matmul(out, uT[:, m, t * P:(t + 1) * P], gw[:, m, :],
                                                start=False, stop=m == DC - 1)
                    ins.then_inc(s["job_" + bank], 1)

                def max_step(b, par, g, n):
                    i = g * ROUND + n
                    h, t = g * HG + n % HG, n // HG
                    if not (isinstance(b, int) and b == 0 and i < 2):
                        pe.wait_ge(s["m_done"], past(b * PER + i - 1))
                    if n == 0 and g % 2 == 0:
                        pe.wait_ge(s[f"stacked{g // 2}"], past((b + 1) * 2 * len(Q_TERMS) * 16))
                    pe.matmul(pm[i % 2][:], stack["q"][par][0:KR, h, t * P:(t + 1) * P],
                              stack["k"][par][0:KR, h, :], start=True, stop=True).then_inc(s["m_ps"], 1)

                def score_step(b, par, g, n):
                    i = g * ROUND + n
                    kc, h = n // HG, g * HG + n % HG
                    if n == 0:
                        pe.wait_ge(s["neg_in"], past((b * NG + g + 1) * 16))
                    if not (isinstance(b, int) and b == 0 and i < 2):
                        pe.wait_ge(s["p_ready"], past(b * PER + i - 1))
                    mm = pe.matmul(ps[i % 2][:], stack["k"][par][0:KR + 3, h, kc * P:(kc + 1) * P],
                                   stack["q"][par][0:KR + 3, h, :], start=True, stop=self_)
                    if not self_:
                        mm = pe.matmul(ps[i % 2][:], G["identb"][:], G["bias"][1][:, kc, :], start=False, stop=True)
                    mm.then_inc(s["s_ps"], 1)

                def value_step(b, par, g, n):
                    i = g * ROUND + n
                    kc, j = n // HG, n % HG
                    pe.wait_ge(s["p_ready"], past(b * PER + i + 1))
                    if n == 0 and not (isinstance(b, int) and b == 0 and g < 2):
                        pe.wait_ge(s["o_saved"], past(b * NG + g - 1))
                    pe.matmul(po[g % 2][j * 32:j * 32 + 32, :], vals[par][:, kc, g * HG + j, :], prob[i % 4][:],
                              start=kc == 0, stop=kc == CB - 1).then_inc(s["pv_done"], 1)

                def before():
                    pe.wait_ge(s["loaded"], past(16 * LOADS))
                    pe.wait_ge(s["cleared"], past(6))
                    for n, name in enumerate(Jobs.BEFORE["a"]):
                        job(0, "a", name, n)
                    for n in range(ROUND):
                        max_step(0, 0, 0, n)
                    job(0, "d", "neg0+", 0)
                    for n in range(ROUND):
                        max_step(0, 0, 1, n)

                def batch(b, par):
                    first, last = first_last(b)
                    pe.wait_ge(s["free_a"], past(J.base("a", b)))
                    for g in range(NG):
                        for n in range(ROUND):
                            for bank, name in jobs_at(b, g, n):
                                if name in ("att0-", "y0-"):
                                    bank_, name_ = {"att0-": ("d", "out3-"), "y0-": ("a", "att1-")}[name]
                                    pe.wait_ge(s["free_" + bank_], past(job_index(bank_, b, name_) + 1))
                                if name == "logits-":
                                    pe.wait_ge(s["free_a"], past(job_index("a", b, "u1-") + 1))
                                job(b + {"+": 1, "-": -1}.get(name[-1], 0), bank, name, job_index(bank, b, name))
                            score_step(b, par, g, n)
                            if n >= LAG:
                                value_step(b, par, g, n - LAG)
                            elif g:
                                value_step(b, par, g - 1, ROUND + n - LAG)
                            elif not first:
                                value_step(b - 1, 1 - par, NG - 1, ROUND + n - LAG)
                            if g < 2:
                                max_step(b, par, g + 2, n)
                            elif not last:
                                max_step(b + 1, 1 - par, g - 2, n)

                def behind():
                    for n in range(ROUND - LAG, ROUND):
                        value_step(B - 1, 1, NG - 1, n)
                    na, nd = J.behind("a"), J.behind("d")
                    job(B - 1, "d", "out3-", nd)
                    pe.wait_ge(s["free_d"], past(nd + 1))
                    job(B - 1, "a", "att0-", na)
                    job(B - 1, "a", "att1-", na + 1)
                    pe.wait_ge(s["free_a"], past(na + 2))
                    job(B - 1, "d", "y0-", nd + 1)
                    job(B - 1, "d", "y1-", nd + 2)
                    if self_:
                        job(B - 1, "a", "u0-", na + 2)
                        job(B - 1, "a", "u1-", na + 3)
                        pe.wait_ge(s["free_a"], past(na + 4))
                        job(B - 1, "d", "logits-", nd + 3)

                run(pe, before, batch, behind)

            @block.scalar
            def _(act):
                def job(b, par, name, index):
                    kind, i = name[:-2], int(name[-2])
                    act.wait_ge(s["job_a"], past(index + 1))
                    if kind == "turn":
                        ins = act.copy(xnT[:, i, :], pj["a"][:])
                    elif kind in ("k", "q"):
                        if not (isinstance(b, int) and b == 0):
                            act.wait_ge(s[f"cut{i}"], past((b - 1) * 2 + (1 if kind == "k" else 2)))
                        if self_:
                            ins = act.activation(full[kind][:, i, :], pj["a"][:], ACT.Identity,
                                                 bias=bias[kind][:, i:i + 1])
                        else:
                            ins = act.copy(full[kind][:, i, :], pj["a"][:])
                    elif kind == "v":
                        ins = act.copy(vals[par][:, 2 * i:2 * i + 2, :, 0:HD],
                                       pj["a"][:].rearrange("p (t h d) -> p t h d", t=2, h=H))
                    elif kind == "att":
                        ins = act.copy(attT[:, i, :], pj["a"][:])
                    else:
                        ins = act.copy(uT[:, i, :], pj["a"][:])
                    ins.then_inc(s["free_a"], 1)

                def save_group(b, g):
                    act.wait_ge(s["pv_done"], past(b * PER + (g + 1) * ROUND))
                    act.copy(outT[:], po[g % 2][:]).then_inc(s["o_saved"], 1)

                def router_exp(b):
                    act.wait_ge(s["shift_ready"], past(b + 1))
                    act.activation(wide[1][:], wide[0][:], ACT.Exp).then_inc(s["rexp_ready"], 1)

                def before():
                    if self_:
                        act.wait_ge(s["loaded"], past(16 * LOADS))
                    act.wait_ge(s["cleared"], past(6))
                    for n, name in enumerate(Jobs.BEFORE["a"]):
                        job(0, 0, name, n)

                def batch(b, par):
                    first, last = first_last(b)
                    for g in range(NG):
                        for n in range(ROUND):
                            i = g * ROUND + n
                            if n == LAG + 1 and (g or not first):
                                pb, pg = (b, g - 1) if g else (b - 1, NG - 1)
                                save_group(pb, pg)
                            for _, name in jobs_at(b, g, n - 1, "a"):
                                job(b + {"+": 1, "-": -1}[name[-1]], 1 - par, name, job_index("a", b, name))
                            if self_ and not first and (g, n) == (3, 2):
                                router_exp(b - 1)
                            act.wait_ge(s["s_ps"], past(b * PER + i + 1))
                            if not (isinstance(b, int) and b == 0 and i < 4):
                                act.wait_ge(s["pv_done"], past(b * PER + i - 3))
                            act.activation(prob[i % 4][:], ps[i % 2][:], ACT.Exp, scale=SCALE).then_inc(s["p_ready"], 1)

                def behind():
                    na = J.behind("a")
                    save_group(B - 1, NG - 1)
                    job(B - 1, 1, "att0-", na)
                    job(B - 1, 1, "att1-", na + 1)
                    if self_:
                        job(B - 1, 1, "u0-", na + 2)
                        job(B - 1, 1, "u1-", na + 3)
                        router_exp(B - 1)

                run(act, before, batch, behind)

            @block.gpsimd
            def _(pool):
                chain = Chain(pool, s["pchain"])

                def cut(b, o):
                    for i, n in enumerate("kq"):
                        x_, (hi, mid, lo) = full[n][:, o, :], (p[:, o, :] for p in parts[n])
                        if isinstance(b, int) and b == 0:
                            pool.wait_ge(s["free_a"], past(Jobs.BEFORE["a"].index(f"{n}{o}+") + 1))
                        else:
                            pool.wait_ge(s["free_a"], past(index_a(b, f"{n}{o}+") + 1))
                            pool.wait_ge(s[f"stacked{o}"], past(b * 2 * len(Q_TERMS) * 16))
                        alone(pool)
                        chain(pool.tensor_copy(hi, x_))
                        chain(pool.tensor_tensor(x_, x_, hi, ALU.subtract))
                        chain(pool.tensor_copy(mid, x_))
                        pool.tensor_tensor(lo, x_, mid, ALU.subtract).then_inc(s[f"cut{o}"], 1)

                def index_a(b, name):
                    first = isinstance(b, int) and b == 1
                    return J.index("a", b - 1, first, False, name)

                def norm(b):
                    pool.wait_ge(s["stats_ready"], past(b + 1))
                    norm_rstd(pool, G, chain, mv, rstd).then_inc(s["rstd_ready"], 1)

                def keep(b, par):
                    pool.wait_ge(s["xn_ready"], past(b + 1))
                    if not (isinstance(b, int) and b < 2):
                        pool.wait_ge(s["u_ready"], past(b - 1))
                    alone(pool)
                    pool.tensor_copy(ukept[par][:], xn[:]).then_inc(s["xn_kept"], 1)

                def norm_y(b):
                    pool.wait_ge(s["y_stats"], past(b + 1))
                    norm_rstd(pool, G, chain, ymv, yrstd).then_inc(s["y_rstd"], 1)

                def before():
                    for i in range(2):
                        pool.memset(vals[i][:], 0.0).then_inc(s["cleared"], 1)
                        pool.wait_ge(s["cleared"], past(3 * i + 1))
                        pool.memset(vals[i][:, :, :, HD:HD + 1], 1.0).then_inc(s["cleared"], 1)
                        pool.wait_ge(s["cleared"], past(3 * i + 2))
                        pool.memset(stack["k"][i][KR:KR + 3, :, :], 1.0).then_inc(s["cleared"], 1)
                        pool.wait_ge(s["cleared"], past(3 * i + 3))
                    norm(0)
                    cut(0, 0)
                    cut(0, 1)
                    if self_:
                        keep(0, 0)

                PPER = 12 + 1 + self_

                def batch(b, par):
                    first, last = first_last(b)
                    if not isinstance(b, int):
                        chain.base, chain.n = (b - 1) * PPER + start[0], 0
                    elif last:
                        chain.base, chain.n = start[0] + (B - 2) * PPER, 0
                    if not last:
                        norm(b + 1)
                        cut(b + 1, 0)
                    if self_ and not first:
                        norm_y(b - 1)
                    if not last:
                        cut(b + 1, 1)
                        if self_:
                            keep(b + 1, 1 - par)
                    if first:
                        start[0] = chain.n
                    elif not last:
                        assert chain.n == PPER

                def behind():
                    if self_:
                        norm_y(B - 1)

                start = [0]
                run(pool, before, batch, behind)

            @block.vector
            def _(dve):
                chain = Chain(dve, s["vchain"])

                def norm_first(b):
                    alone(dve)
                    norm_stats(dve, chain, stats, mv, lambda t: X[:, b * CB + t, :]).then_inc(s["stats_ready"], 1)

                def norm_second(b):
                    dve.wait_ge(s["rstd_ready"], past(b + 1))
                    dve.wait_ge(s["stats_ready"], past(b + 1))
                    if not (isinstance(b, int) and b == 0):
                        dve.wait_ge(s["job_a"], past(J.base("a", b - 1)))
                        if self_:
                            dve.wait_ge(s["xn_kept"], past(b))
                    norm_apply(dve, lambda t: xn[:, t, :], lambda t: X[:, b * CB + t, :], mv, rstd
                               ).then_inc(s["xn_ready"], 1)

                def max_step(b, g, n):
                    i, t, j = g * ROUND + n, n // HG, n % HG
                    dve.wait_ge(s["m_ps"], past(b * PER + i + 1))
                    if self_:
                        ins = dve.tensor_reduce(tops[:, t, j:j + 1], pm[i % 2][:], AX.X, ALU.max)
                    else:
                        alone(dve)
                        ins = dve.tensor_tensor_reduce(junk[:, i % 2, :], pm[i % 2][:], G["bias"][0][:, t, :], 1.0,
                                                       -BIG / 2, ALU.add, ALU.max, tops[:, t, j:j + 1])
                    ins.then_inc(s["m_done"], 1)

                def cut_maxima(b, g, before_):
                    dve.wait_ge(s["m_done"], past(b * PER + (g + 1) * ROUND))
                    if before_ is not None:
                        dve.wait_ge(s["job_d"], past(before_ + 1))
                    chain(dve.tensor_scalar(neg[:], tops[:], -1.0, None, ALU.mult))
                    chain(dve.tensor_copy(neg3[:, :, 0, :], neg[:]))
                    chain(dve.tensor_tensor(rest[:], neg[:], neg3[:, :, 0, :], ALU.subtract))
                    chain(dve.tensor_copy(neg3[:, :, 1, :], rest[:]))
                    dve.tensor_tensor(neg3[:, :, 2, :], rest[:], neg3[:, :, 1, :], ALU.subtract
                                      ).then_inc(s["neg_ready"], 1)

                def job(b, name, index):
                    kind, i = (name[:-1], 0) if name == "logits-" else (name.rstrip("+-")[:-1], int(name.rstrip("+-")[-1]))
                    bank = pj["d"]
                    dve.wait_ge(s["job_d"], past(index + 1))
                    if kind == "neg":
                        if not (isinstance(b, int) and b == 0 and i == 0):
                            dve.wait_ge(s["neg_in"], past((b * NG + i) * 16))
                        ins = dve.tensor_copy(negT[:], bank[:].bitcast(BF16)[0:3 * HG, 0:S])
                    elif kind == "out":
                        view = bank[:].rearrange("p (t h d) -> p t h d", t=CB, h=HG)
                        chain(dve.tensor_scalar(rec[:], view[:, :, :, HD], 1e-9, None, ALU.max))
                        chain(dve.reciprocal(rec[:], rec[:]))
                        ins = dve.tensor_tensor(
                            att[:, :, i * HG * HD:(i + 1) * HG * HD].rearrange("p t (h d) -> p t h d", h=HG),
                            view[:, :, :, 0:HD], rec[:].unsqueeze(3).broadcast_to([P, CB, HG, HD]), ALU.mult)
                    elif kind == "y":
                        view = bank[:].rearrange("p (t d) -> p t d", d=D)
                        if self_:
                            ins = dve.tensor_copy(yn[:, 2 * i:2 * i + 2, :], view)
                        else:
                            rr = X[:, bass.ds(b * CB + 2 * i, 2), :]
                            ins = dve.tensor_tensor(rr, rr, view, ALU.add)
                    else:
                        view = bank[:, 0:CB * E].rearrange("p (t e) -> p t e", e=E)
                        chain(dve.tensor_reduce(small[0][:], view, AX.X, ALU.max))
                        ins = dve.tensor_tensor(wide[0][:], view, small[0][:].unsqueeze(2).broadcast_to([P, CB, E]),
                                                ALU.subtract)
                    ins.then_inc(s["free_d"], 1)
                    if kind == "logits":
                        dve.wait_ge(s["free_d"], past(index + 1))
                        dve.nop().then_inc(s["shift_ready"], 1)

                def y_first(b, index):
                    dve.wait_ge(s["free_d"], past(index + 1))
                    alone(dve)
                    norm_stats(dve, chain, stats, ymv, lambda t: yn[:, t, :]).then_inc(s["y_stats"], 1)

                def y_second(b, par):
                    dve.wait_ge(s["y_rstd"], past(b + 1))
                    dve.wait_ge(s["y_stats"], past(b + 1))
                    chain(norm_apply(dve, lambda t: yn[:, t, :], lambda t: yn[:, t, :], ymv, yrstd))
                    chain(dve.tensor_tensor(yn[:], yn[:], gain[:].unsqueeze(1).broadcast_to([P, CB, D]), ALU.mult))
                    chain(dve.tensor_tensor(yn[:], yn[:], shift[:].unsqueeze(1).broadcast_to([P, CB, D]), ALU.add))
                    rr = X[:, bass.ds(b * CB, CB), :]
                    if not (isinstance(b, int) and b == 0):
                        dve.wait_ge(s["rows_stored"], past(b * 16))
                    dve.wait_ge(s["xn_kept"], past(b + 1))
                    dve.tensor_tensor(u2[:], yn[:], ukept[par][:], ALU.add).then_inc(s["u_ready"], 1)
                    dve.wait_ge(s["u_ready"], past(b + 1))
                    chain(dve.tensor_tensor(rr, rr, u2[:], ALU.add))

                def router(b):
                    dve.wait_ge(s["rexp_ready"], past(b + 1))
                    chain(dve.tensor_reduce(small[1][:], wide[1][:], AX.X, ALU.add))
                    chain(dve.reciprocal(small[2][:], small[1][:]))
                    chain(dve.tensor_tensor(G["prob"][:, bass.ds(b * CB, CB), :], wide[1][:],
                                            small[2][:].unsqueeze(2).broadcast_to([P, CB, E]), ALU.mult))

                def before():
                    if self_:
                        dve.wait_ge(s["loaded"], past(16 * LOADS))
                    norm_first(0)
                    norm_second(0)
                    for n in range(ROUND):
                        max_step(0, 0, n)
                    cut_maxima(0, 0, None)
                    job(0, "neg0+", 0)
                    for n in range(ROUND):
                        max_step(0, 1, n)
                    cut_maxima(0, 1, 0)

                def batch(b, par):
                    first, last = first_last(b)
                    if not isinstance(b, int):
                        chain.base, chain.n = (b - 1) * VPER + start[0], 0
                    elif last:
                        chain.base, chain.n = start[0] + (B - 2) * VPER, 0
                    for g in range(NG):
                        for n in range(ROUND):
                            if not last and (g, n) == (0, 0):
                                norm_first(b + 1)
                            if not last and (g, n) == (0, 6):
                                norm_second(b + 1)
                            for _, name in jobs_at(b, g, n - 1, "d"):
                                if name == "out0" and not first:
                                    dve.wait_ge(s["job_a"], past(job_index("a", b, "att1-") + 1))
                                job(b + {"+": 1, "-": -1}.get(name[-1], 0), name, job_index("d", b, name))
                            if self_ and not first:
                                if (g, n) == (1, 9):
                                    y_first(b - 1, job_index("d", b, "y1-"))
                                if (g, n) == (2, 1):
                                    y_second(b - 1, 1 - par)
                                if (g, n) == (3, 5):
                                    router(b - 1)
                            if g < 2:
                                max_step(b, g + 2, n)
                            elif not last:
                                max_step(b + 1, g - 2, n)
                        if g < 2:
                            cut_maxima(b, g + 2, job_index("d", b, ("neg1", "neg2")[g]))
                        elif not last:
                            cut_maxima(b + 1, g - 2, job_index("d", b, ("neg3", "neg0+")[g - 2]))
                    if first:
                        start[0] = chain.n
                    elif not last:
                        assert chain.n == VPER, chain.n

                def behind():
                    nd = J.behind("d")
                    for i, name in enumerate(("out3-", "y0-", "y1-")):
                        job(B - 1, name, nd + i)
                    if self_:
                        y_first(B - 1, nd + 2)
                        y_second(B - 1, 1)
                        job(B - 1, "logits-", nd + 3)
                        router(B - 1)
                    else:
                        dve.wait_ge(s["free_d"], past(nd + 3))

                start = [0]
                VPER = 4 * NG + 2 * NG + 1 + (9 if self_ else 0)
                run(dve, before, batch, behind)


def top_experts(nc, G):
    with ExitStack() as ctx:
        st = Stage(nc, ctx, "top")
        tiles = TILES["L1"]
        ahead, tie = st.sb("ahead", [P, NC, E, E]), st.sb("tie", [P, NC, E, E])
        rank, chosen, at, got = (st.sb(n, [P, E, NC]) for n in ("rank", "chosen", "at", "got"))
        front, scan, keep = (st.sb(n, [P, E * NC]) for n in ("front", "scan", "keep"))
        full = st.sb("full", [P, E, N // TILE])
        steps, size, first, last = (st.sb(n, [P, w]) for n, w in
                                    (("steps", N // TILE), ("size", E), ("first", E), ("last", E)))
        cross = st.sb("cross", [P, E, E])
        past_end, owner = st.sb("past_end", [1, tiles, E]), st.sb("owner", [1, tiles])
        pin, pall = st.ps("pin", [P, S]), st.ps("pall", [P, S])
        vchain, flagged, counted = (st.sem(n) for n in ("vchain", "flagged", "counted"))
        mine = G["prob"][:].unsqueeze(3).broadcast_to([P, NC, E, E])
        other = G["prob"][:].unsqueeze(2).broadcast_to([P, NC, E, E])

        def to(t, shape, axis):
            return t.unsqueeze(axis).broadcast_to(shape)

        with nc.Block() as block:

            @block.sync
            def _(sp):
                st.set_semaphores(sp)

            @block.tensor
            def _(pe):
                pe.wait_ge(flagged, past(1))
                in_front_pe(pe, G, pin, pall, chosen[:].rearrange("p e c -> p (e c)")).then_inc(counted, 1)

            @block.vector
            def _(dve):
                chain = Chain(dve, vchain)
                chain(dve.memset(keep[:], 1.0))
                chain(dve.memset(keep[:].rearrange("p (e c) -> p e c", c=NC)[:, :, 0:1], 0.0))
                chain(dve.tensor_tensor(ahead[:], other, mine, ALU.is_gt))
                chain(dve.tensor_tensor(tie[:], other, mine, ALU.is_equal))
                chain(dve.tensor_tensor(tie[:], tie[:], to(G["lower"][:], [P, NC, E, E], 1), ALU.mult))
                chain(dve.tensor_tensor(ahead[:], ahead[:], tie[:], ALU.add))
                chain(dve.tensor_reduce(rank[:].rearrange("p e c -> p c e"), ahead[:], AX.X, ALU.add))
                dve.tensor_scalar(chosen[:], rank[:], float(TOPK), None, ALU.is_lt).then_inc(flagged, 1)
                chain(dve.tensor_scalar(steps[:], G["lane"][:, 0:N // TILE], float(TILE), None, ALU.mult))
                dve.wait_ge(counted, past(1))
                in_front_dve(dve, chain, front, scan, keep, pin, pall)
                sizes = scan[:].rearrange("p (e c) -> p e c", c=NC)[:, :, NC - 1]
                chain(dve.tensor_tensor(full[:], to(sizes, [P, E, N // TILE], 2), to(steps[:], [P, E, N // TILE], 1),
                                        ALU.is_gt))
                chain(dve.tensor_reduce(size[:], full[:], AX.X, ALU.add))
                chain(dve.tensor_tensor(cross[:], G["lower"][:], to(size[:], [P, E, E], 1), ALU.mult))
                chain(dve.tensor_reduce(first[:], cross[:], AX.X, ALU.add))
                chain(dve.tensor_tensor(last[:], first[:], size[:], ALU.add))
                chain(dve.tensor_tensor(past_end[:], to(last[0:1, :], [1, tiles, E], 1),
                                        to(G["lane"][0:1, 0:tiles], [1, tiles, E], 2), ALU.is_le))
                chain(dve.tensor_reduce(owner[:], past_end[:], AX.X, ALU.add))
                chain(dve.tensor_scalar(G["owner"][:], owner[:], float(E - 1), None, ALU.min))
                chain(dve.scalar_tensor_tensor(out=at[:], in0=to(first[:], [P, E, NC], 2), scalar=float(TILE),
                                               in1=front[:].rearrange("p (e c) -> p e c", c=NC),
                                               op0=ALU.mult, op1=ALU.add))
                for k in range(TOPK):
                    for dst, src in ((G["place"], at[:]), (G["weight"], G["prob"][:].rearrange("p c e -> p e c"))):
                        chain(dve.scalar_tensor_tensor(out=got[:], in0=rank[:], scalar=float(k), in1=src,
                                                       op0=ALU.is_equal, op1=ALU.mult))
                        chain(dve.tensor_reduce(dst[:, k * NC:(k + 1) * NC], got[:].rearrange("p e c -> p c e"),
                                                AX.X, ALU.add))


def finish(nc, G, a, out):
    with ExitStack() as ctx:
        st = Stage(nc, ctx, "fin")
        stats, mv, rstd = st.sb("stats", [P, CB, 6]), st.sb("mv", [P, CB, 2]), st.sb("rstd", [P, CB])
        gain, shift, xn = st.sb("gain", [P, D]), st.sb("shift", [P, D]), st.sb("xn", [P, CB, D])
        loaded, stats_ready, rstd_ready, vchain, pchain, ready, stored = (
            st.sem(n) for n in ("loaded", "stats_ready", "rstd_ready", "vchain", "pchain", "ready", "stored"))
        X, Y, y_in = G["x"], st.sb("y", [P, NC, D]), st.sem("y_in")
        VPER = 4
        with nc.Block() as block:

            @block.sync
            def _(sp):
                st.set_semaphores(sp)
                sp.dma_start(gain[:], a["L1_ln2_g"].broadcast_to([P, D])).then_inc(loaded, 16)
                sp.dma_start(shift[:], a["L1_ln2_b"].broadcast_to([P, D])).then_inc(loaded, 16)
                for b in range(B):
                    sp.dma_start(Y[:, b * CB:(b + 1) * CB, :],
                                 G["sum1"][0:N, :].rearrange("(c p) d -> p c d", p=P)[:, b * CB:(b + 1) * CB, :]
                                 ).then_inc(y_in, 16)
                with sp.Fori(0, B) as b:
                    sp.wait_ge(ready, past(b + 1))
                    sp.dma_start(out.rearrange("b (c p) d -> p (b c) d", p=P)[:, bass.ds(b * CB, CB), :],
                                 X[:, bass.ds(b * CB, CB), :]).then_inc(stored, 16)
                sp.wait_ge(stored, past(16 * B))

            @block.gpsimd
            def _(pool):
                with pool.Fori(0, B) as b:
                    chain = Chain(pool, pchain, b)
                    pool.wait_ge(stats_ready, past(b + 1))
                    norm_rstd(pool, G, chain, mv, rstd).then_inc(rstd_ready, 1)

            @block.vector
            def _(dve):
                dve.wait_ge(loaded, past(32))
                dve.wait_ge(y_in, past(16 * B))
                with dve.Fori(0, B) as b:
                    chain = Chain(dve, vchain, b * VPER)
                    norm_stats(dve, chain, stats, mv, lambda t: Y[:, b * CB + t, :]).then_inc(stats_ready, 1)
                    dve.wait_ge(rstd_ready, past(b + 1))
                    dve.wait_ge(stats_ready, past(b + 1))
                    chain(norm_apply(dve, lambda t: xn[:, t, :], lambda t: Y[:, b * CB + t, :], mv, rstd))
                    chain(dve.tensor_tensor(xn[:], xn[:], gain[:].unsqueeze(1).broadcast_to([P, CB, D]), ALU.mult))
                    chain(dve.tensor_tensor(xn[:], xn[:], shift[:].unsqueeze(1).broadcast_to([P, CB, D]), ALU.add))
                    rr = X[:, bass.ds(b * CB, CB), :]
                    dve.tensor_tensor(rr, rr, xn[:], ALU.add).then_inc(ready, 1)
                    dve.wait_ge(ready, past(b + 1))
                    assert chain.n == VPER


def build(nc, a, out):
    with ExitStack() as ctx:
        def sb(name, shape, dt=F32):
            return ctx.enter_context(nc.sbuf_tensor(name, shape, dt))

        def dram(name, shape):
            return nc.dram_tensor(name, shape, F32, kind="Internal").ap()

        G = {
            "x": sb("x", [P, NC, D]),
            "ident": sb("ident", [P, P]), "identb": sb("identb", [P, P], BF16), "before": sb("before", [P, P]),
            "ones": sb("ones", [P, P]), "mhalf": sb("mhalf", [P, CB]), "lower": sb("lower", [P, E, E]),
            "lane": sb("lane", [P, P]), "token1": sb("token1", [P, NC]), "spare1": sb("spare1", [P, 1]),
            "bias": [sb(f"bias{i}", [P, CB, S], BF16) for i in range(2)],
            "ratio": sb("ratio", [P, DC, B]), "prob": sb("prob", [P, NC, E]),
            "place": sb("place", [P, E * NC]), "weight": sb("weight", [P, E * NC]),
            "row": sb("row", [P, COLS], U32), "roww": sb("roww", [P, COLS]),
            "owner": sb("owner", [1, TILES["L1"]], mybir.dt.int32),
            "rows0": dram("rows0", [N + P, D]), "rows1": dram("rows1", [N + P, D]),
            "sum0": dram("sum0", [N + P, D]), "sum1": dram("sum1", [N + P, D]),
        }
        setup(nc, G, a)
        aft_keys(nc, G, a)
        aft_tokens(nc, G, a)
        expert_choice(nc, G)
        lists(nc, G, "L0", E, NC, CAP // P)
        experts(nc, G, a, "L0", ACT.Gelu_apprx_tanh)
        attention(nc, G, a, "L1x", False)
        attention(nc, G, a, "L1", True)
        top_experts(nc, G)
        lists(nc, G, "L1", 1, TOPK * NC, COLS)
        experts(nc, G, a, "L1", ACT.Gelu)
        finish(nc, G, a, out)


def kernel(**inputs):
    import numpy as np
    import concourse.bacc as bacc
    from concourse.bass_utils import run_bass_kernel_spmd

    i = {k: np.asarray(v) for k, v in inputs.items()}
    mask = i["mask_SxS2_bk0"]

    def columns(v, n):
        return v.reshape(-1, n, P).swapaxes(-1, -2)

    by_row = np.arange(D).reshape(DC, HC, HD).swapaxes(1, 2).reshape(D)
    lay = {
        "x": i["x"], "ctxT": i["ctx_1024"].reshape(N, D).T, "mask": mask, "maskT": mask.T,
        "L0_WqT": i["L0_xattn_Wq"].T, "L0_WkT": i["L0_xattn_Wk"].T, "L0_WvT": i["L0_xattn_Wv"].T,
        "L0_WoT": i["L0_xattn_Wo"].T, "L0_Ws": i["L0_ffn_Ws"], "L0_bs": i["L0_ffn_bs"].reshape(1, E),
        "L1_Wq": i["L1_ffn_Wq"], "L1_Wk": i["L1_ffn_Wk"], "L1_Wv": i["L1_ffn_Wv"], "L1_Wo": i["L1_ffn_Wo"],
        "L1_bq": columns(i["L1_ffn_bq"][by_row], DC)[0], "L1_bk": columns(i["L1_ffn_bk"][by_row], DC)[0],
        "L1_gate_w": i["L1_ffn_gate_w"],
    }
    for n in ("Wq", "Wk", "Wv", "Wo"):
        lay["L1x_" + n] = i["L1_xattn_" + n].T
    for t in ("L1x", "L1"):
        for n in ("Wq", "Wk"):
            lay[f"{t}_{n}"] = lay[f"{t}_{n}"][:, by_row]
    for n in ("bv", "bo", "ln1_g", "ln1_b", "ln2_g", "ln2_b", "gate_b"):
        lay["L1_" + n] = i["L1_ffn_" + n].reshape(1, -1)
    for t in ("L0", "L1"):
        for n in ("W1", "W2", "b2"):
            lay[f"{t}_{n}"] = i[f"{t}_ffn_{n}"]
        lay[f"{t}_b1"] = columns(i[f"{t}_ffn_b1"], FC)

    nc = bacc.Bacc("TRN2", target_bir_lowering=False, num_devices=1)
    arrays, a = {}, {}
    for name, v in lay.items():
        v = np.ascontiguousarray(v)
        arrays["in_" + name] = v
        a[name] = nc.dram_tensor("in_" + name, v.shape, mybir.dt.from_np(v.dtype), kind="ExternalInput").ap()
    out = nc.dram_tensor("out", (B, S, D), F32, kind="ExternalOutput").ap()
    build(nc, a, out)
    r = run_bass_kernel_spmd(nc, [arrays], core_ids=[0])
    return r.results[0]["out"]
```

```python
from contextlib import ExitStack

import concourse.bass as bass
from concourse import mybir

F32 = mybir.dt.float32
BF16 = mybir.dt.bfloat16
U32 = mybir.dt.uint32
U8 = mybir.dt.uint8
ALU = mybir.AluOpType
ACT = mybir.ActivationFunctionType
AX = mybir.AxisListType

P = 128
B, S, D = 8, 512, 256
N = B * S
NC = N // P
CB = S // P
DC = D // P
E, F = 8, 1024
FC = F // P
H, HD = 16, 16
HG = 4
NG = H // HG
HC = H // DC
CAP = N // E
TOPK = 2
TILES_OF = {"L0": 512, "L1": 256}
TILE = TILES_OF["L1"]
TILES = {"L0": E * CAP // TILES_OF["L0"], "L1": (N * TOPK + E * (TILE - 1)) // TILE}
COLS = (TILES["L1"] + 2) * TILE // P
SLAB = 16
BITS = 30
EPS = 1e-5
SCALE = HD ** -0.5
BIG = 2.0 ** 30
STEPS = 3
Q_TERMS = (0, 0, 1, 1, 0, 2)
K_TERMS = (0, 1, 0, 1, 2, 0)
KR = 16 * len(Q_TERMS)


def past(n):
    return n + 1


class Stage:

    def __init__(self, nc, ctx, tag):
        self.nc, self.ctx, self.tag, self.sems = nc, ctx, tag, []

    def sb(self, name, shape, dt=F32):
        return self.ctx.enter_context(self.nc.sbuf_tensor(f"{self.tag}_{name}", shape, dt))

    def ps(self, name, shape, dt=F32):
        return self.ctx.enter_context(self.nc.psum_tensor(f"{self.tag}_{name}", shape, dt))

    def sem(self, name):
        self.sems.append(self.ctx.enter_context(self.nc.semaphore(f"{self.tag}_{name}")))
        return self.sems[-1]

    def pool_dma_sem(self, name):
        return self.ctx.enter_context(self.nc.semaphore(f"{self.tag}_{name}"))

    def set_semaphores(self, sp):
        for s in self.sems:
            sp.sem_inc(s, 1)


def alone(eng):
    eng.nop(nofuse=True)


class Chain:

    def __init__(self, eng, sem, base=0):
        self.eng, self.sem, self.base, self.n = eng, sem, base, 0

    def __call__(self, ins):
        ins.then_inc(self.sem, 1)
        self.n += 1
        self.eng.wait_ge(self.sem, past(self.base + self.n))
        if not isinstance(self.base, int):
            alone(self.eng)

    def mark(self, ins):
        ins.then_inc(self.sem, 1)
        self.n += 1

    def await_last(self):
        self.eng.wait_ge(self.sem, past(self.base + self.n))
        alone(self.eng)


def aft_keys(nc, G, a):
    with ExitStack() as ctx:
        st = Stage(nc, ctx, "aft")
        ctxT = st.sb("ctxT", [P, DC, N])
        wk, wv = st.sb("wk", [P, DC, D]), st.sb("wv", [P, DC, D])
        keys = st.sb("keys", [P, DC, B, S])
        top = st.sb("top", [P, DC, S])
        diff, ex = st.sb("diff", [P, DC, S]), st.sb("ex", [P, DC, S])
        den, num, rden = st.sb("den", [P, DC]), st.sb("num", [P, DC]), st.sb("rden", [P, DC])
        zero = st.sb("zero", [P, D])
        lane_i, token_i, spare_i = (st.sb(n, [P, w], mybir.dt.int32) for n, w in (("lane", P), ("tok", NC), ("spare", 1)))
        raw = [st.sb(f"mask_raw{i}", [P, CB, S], U8) for i in range(2)]
        bank = [[st.ps(f"bank{i}{o}", [P, S]) for o in range(DC)] for i in range(2)]
        names = ("wv_in", "ctx0_in", "ctx1_in", "x_in", "mask_in", "keys_ps", "keys_saved", "keys_top",
                 "diff_ready", "ex_ready", "vals_ps", "summed", "dvec", "topped", "cleared", "built", "vec", "zeroed",
                 "stored", "counted")
        (wv_in, ctx0_in, ctx1_in, x_in, mask_in, keys_ps, keys_saved, keys_top, diff_ready, ex_ready, vals_ps,
         summed, dvec, topped, cleared, built, vec, zeroed, stored, counted) = (st.sem(n) for n in names)
        ctx_in, HALF = (ctx0_in, ctx1_in), B // 2

        def project(pe, w, b, slot):
            for o in range(DC):
                for m in range(DC):
                    mm = pe.matmul(bank[slot][o][:], w[:, m, o * P:(o + 1) * P], ctxT[:, m, bass.ds(b * S, S)],
                                   start=m == 0, stop=m == DC - 1)
            return mm

        with nc.Block() as block:

            @block.sync
            def _(sp):
                st.set_semaphores(sp)
                sp.dma_start(wk[:], a["L0_WkT"].rearrange("(c p) n -> p c n", p=P)).then_inc(ctx0_in, 16)
                for i in range(2):
                    here = slice(i * HALF * S, (i + 1) * HALF * S)
                    sp.dma_start(ctxT[:, :, here], a["ctxT"].rearrange("(c p) n -> p c n", p=P)[:, :, here]
                                 ).then_inc(ctx_in[i], 16)
                sp.dma_start(wv[:], a["L0_WvT"].rearrange("(c p) n -> p c n", p=P)).then_inc(wv_in, 16)
                sp.dma_start(raw[0][:], a["mask"].rearrange("(c p) k -> p c k", p=P)).then_inc(mask_in, 16)
                sp.dma_start(raw[1][:], a["maskT"].rearrange("(c p) k -> p c k", p=P)).then_inc(mask_in, 16)
                sp.dma_start(G["x"][:], a["x"].rearrange("b (c p) d -> p (b c) d", p=P)).then_inc(x_in, 16)
                sp.wait_ge(zeroed, past(1))
                for dst, first in ((G["sum1"], 0), (G["rows0"], NC), (G["rows1"], NC), (G["sum0"], NC)):
                    sp.dma_start(dst.rearrange("(c p) d -> p c d", p=P)[:, first:, :],
                                 zero[:].unsqueeze(1).broadcast_to([P, NC + 1 - first, D])).then_inc(stored, 16)
                sp.wait_ge(x_in, past(16))
                sp.wait_ge(stored, past(64))

            @block.tensor
            def _(pe):
                for half in range(2):
                    pe.wait_ge(ctx_in[half], past(16 if half else 32))
                    with pe.Fori(half * HALF // 2, (half + 1) * HALF // 2) as pair:
                        for slot in range(2):
                            pe.wait_ge(keys_saved, past((pair * 2 + max(slot - 1, 0)) * DC))
                            alone(pe)
                            project(pe, wk, pair * 2 + slot, slot).then_inc(keys_ps, 1)
                pe.wait_ge(wv_in, past(16))
                pe.wait_ge(keys_saved, past(B * DC))
                with pe.Fori(0, B // 2) as pair:
                    for slot in range(2):
                        pe.wait_ge(summed, past((pair * 2 + max(slot - 1, 0)) * DC))
                        alone(pe)
                        project(pe, wv, pair * 2 + slot, slot).then_inc(vals_ps, 1)

            @block.scalar
            def _(act):
                with act.Fori(0, B // 2) as pair:
                    for slot in range(2):
                        b = pair * 2 + slot
                        act.wait_ge(keys_ps, past(b + 1))
                        for o in range(DC):
                            act.copy(keys[:, o, b, :], bank[slot][o][:]).then_inc(keys_saved, 1)
                with act.Fori(0, B) as b:
                    act.wait_ge(diff_ready, past(b + 1))
                    act.wait_ge(summed, past(b * DC))
                    for o in range(DC):
                        act.activation(ex[:, o, :], diff[:, o, :], ACT.Exp,
                                       accum_out=den[:, o:o + 1]).then_inc(ex_ready, 1)

            @block.gpsimd
            def _(pool):
                pool.memset(G["ident"][:], 0.0).then_inc(cleared, 1)
                pool.memset(G["identb"][:], 0.0).then_inc(cleared, 1)
                pool.memset(G["before"][:], 1.0).then_inc(cleared, 1)
                pool.memset(G["ones"][:], 1.0).then_inc(built, 1)
                pool.memset(G["mhalf"][:], -0.5).then_inc(built, 1)
                pool.memset(G["lower"][:], 1.0).then_inc(cleared, 1)
                pool.wait_ge(cleared, past(4))
                for t in (G["ident"], G["identb"]):
                    pool.affine_select(out=t[:], in_=t[:], compare_op=ALU.not_equal, fill=1.0, base=0,
                                       pattern=[[-1, P]], channel_multiplier=1).then_inc(built, 1)
                pool.affine_select(out=G["before"][:], in_=G["before"][:], compare_op=ALU.is_gt, fill=0.0,
                                   base=0, pattern=[[1, P]], channel_multiplier=-1).then_inc(built, 1)
                pool.affine_select(out=G["lower"][:], in_=G["lower"][:], compare_op=ALU.is_gt, fill=0.0,
                                   base=0, pattern=[[1, E], [-1, E]], channel_multiplier=0).then_inc(built, 1)
                pool.wait_ge(built, past(6))
                pool.iota(lane_i[:], pattern=[[1, P]], base=0, channel_multiplier=0).then_inc(counted, 1)
                pool.iota(token_i[:], pattern=[[P, NC]], base=1, channel_multiplier=1).then_inc(counted, 1)
                pool.iota(spare_i[:], pattern=[[1, 1]], base=N + 1, channel_multiplier=1).then_inc(counted, 1)

            @block.vector
            def _(dve):
                dve.memset(zero[:], 0.0).then_inc(zeroed, 1)
                dve.memset(top[:], -3.0e38).then_inc(topped, 1)
                dve.wait_ge(topped, past(1))
                with dve.Fori(0, B) as b:
                    dve.wait_ge(keys_top, past(b * DC))
                    for o in range(DC):
                        dve.wait_ge(keys_saved, past(b * DC + o + 1))
                        dve.tensor_tensor(top[:, o, :], top[:, o, :], keys[:, o, b, :], ALU.max).then_inc(keys_top, 1)
                dve.wait_ge(keys_top, past(B * DC))
                dve.wait_ge(keys_saved, past(B * DC))
                with dve.Fori(0, B // 2) as pair:
                    for slot in range(2):
                        b = pair * 2 + slot
                        dve.wait_ge(ex_ready, past(b * DC))
                        dve.tensor_tensor(diff[:], keys[:, :, b, :], top[:], ALU.subtract).then_inc(diff_ready, 1)
                        dve.wait_ge(dvec, past(b * 2))
                        for o in range(DC):
                            dve.wait_ge(ex_ready, past(b * DC + o + 1))
                            dve.wait_ge(vals_ps, past(b + 1))
                            dve.tensor_tensor_reduce(ex[:, o, :], ex[:, o, :], bank[slot][o][:], 1.0, 0.0, ALU.mult,
                                                     ALU.add, num[:, o:o + 1]).then_inc(summed, 1)
                        dve.reciprocal(rden[:], den[:]).then_inc(dvec, 1)
                        dve.wait_ge(dvec, past(b * 2 + 1))
                        dve.wait_ge(summed, past(b * DC + DC))
                        dve.tensor_tensor(G["ratio"][:, :, b], num[:], rden[:], ALU.mult).then_inc(dvec, 1)
                dve.wait_ge(dvec, past(2 * B))
                dve.wait_ge(counted, past(3))
                for dst, src in ((G["lane"], lane_i), (G["token1"], token_i), (G["spare1"], spare_i)):
                    dve.tensor_copy(dst[:], src[:]).then_inc(vec, 1)
                dve.wait_ge(mask_in, past(32))
                for i in range(2):
                    dve.tensor_scalar(G["bias"][i][:], raw[i][:], BIG, -BIG, ALU.mult, ALU.add).then_inc(vec, 1)
                dve.wait_ge(vec, past(5))


def norm_stats(dve, chain, stats, mv, src):
    for t in range(CB):
        ins = dve.bn_stats(stats[:, t, :], src(t))
    chain(ins)
    for t in range(CB):
        ins = dve.bn_aggr(mv[:, t, :], stats[:, t, :])
    return ins


def norm_rstd(pool, G, chain, mv, rstd):
    alone(pool)
    chain(pool.tensor_scalar(rstd[:], mv[:, :, 1], EPS, None, ALU.add))
    return pool.tensor_tensor(rstd[:], rstd[:], G["mhalf"][:, 0:CB], ALU.pow)


def norm_apply(dve, dst, src, mv, rstd):
    for t in range(CB):
        ins = dve.tensor_scalar(dst(t), src(t), mv[:, t, 0:1], rstd[:, t:t + 1], ALU.subtract, ALU.mult)
    return ins


def turn(pe, G, bank, src):
    for m in range(DC):
        for t in range(CB):
            ins = pe.transpose(bank(m)[:, t * P:(t + 1) * P], src(t, m), G["ident"][:])
    return ins


def router_dve(dve, chain, logits, small, wide, exp_ready, ex_wait, psum_ready_inc, out):
    top, tot, rec = small
    shifted, ex = wide
    chain(dve.tensor_reduce(top[:], logits, AX.X, ALU.max))
    dve.tensor_tensor(shifted[:], logits, top[:].unsqueeze(2).broadcast_to([P, CB, E]),
                      ALU.subtract).then_inc(psum_ready_inc, 1)
    dve.wait_ge(exp_ready, past(ex_wait))
    chain(dve.tensor_reduce(tot[:], ex[:], AX.X, ALU.add))
    chain(dve.reciprocal(rec[:], tot[:]))
    chain(dve.tensor_tensor(out, ex[:], rec[:].unsqueeze(2).broadcast_to([P, CB, E]), ALU.mult))


def aft_tokens(nc, G, a):
    with ExitStack() as ctx:
        st = Stage(nc, ctx, "tok")
        wq, wo, ws = st.sb("wq", [P, DC, D]), st.sb("wo", [P, DC, D]), st.sb("ws", [P, DC, E])
        bs = st.sb("bs", [1, E])
        stats = [st.sb(f"stats{i}", [P, CB, 6]) for i in range(2)]
        mv, rstd = [st.sb(f"mv{i}", [P, CB, 2]) for i in range(2)], [st.sb(f"rstd{i}", [P, CB]) for i in range(2)]
        xn, xnT, yT = st.sb("xn", [P, CB, D]), st.sb("xnT", [P, DC, S]), st.sb("yT", [P, DC, S])
        fx, fxT = st.sb("fx", [P, CB, D]), st.sb("fxT", [P, DC, S])
        small = [st.sb(n, [P, CB]) for n in ("rtop", "rsum", "rrec")]
        wide = [st.sb(n, [P, CB, E]) for n in ("rshift", "rexp")]
        pt = [st.ps(f"pt{i}", [P, S]) for i in range(DC)]
        pq = [st.ps(f"pq{i}", [P, S]) for i in range(DC)]
        po = [st.ps(f"po{i}", [P, S]) for i in range(2)]
        pl = st.ps("pl", [P, S])
        names = ("loaded", "stats_ready", "rstd_ready", "xn_ready", "turned", "xnT_ready", "q_ps", "sig_ready",
                 "yT_ready", "out_ps", "x1_ready", "fstats_ready", "frstd_ready", "fx_ready", "fturned", "fxT_ready",
                 "logits_ps", "shift_ready", "rexp_ready", "vchain", "pchain", "fvchain", "fpchain", "rchain",
                 "x1_stored", "rows_stored")
        s = {n: st.sem(n) for n in names}
        X = G["x"]

        def run(eng, step):
            step(-1, ("norm",))
            step(0, ("norm", "turn"))
            step(1, ("norm", "turn", "mix"))
            with eng.Fori(2, B - 1) as i:
                step(i, ("norm", "turn", "mix", "route"))
            step(B - 1, ("turn", "mix", "route"))
            step(B, ("mix", "route"))
            step(B + 1, ("route",))

        with nc.Block() as block:

            @block.sync
            def _(sp):
                st.set_semaphores(sp)
                for dst, src in ((wq, "L0_WqT"), (wo, "L0_WoT"), (ws, "L0_Ws")):
                    sp.dma_start(dst[:], a[src].rearrange("(c p) n -> p c n", p=P)).then_inc(s["loaded"], 16)
                sp.dma_start(bs[:], a["L0_bs"]).then_inc(s["loaded"], 16)

                def step(i, parts):
                    if "route" in parts:
                        b = i - 2
                        sp.wait_ge(s["fx_ready"], past(b + 1))
                        sp.dma_start(G["rows0"].rearrange("(c p) d -> p c d", p=P)[:, bass.ds(b * CB, CB), :], fx[:]
                                     ).then_inc(s["rows_stored"], 16)
                    if "mix" in parts:
                        b = i - 1
                        here = bass.ds(b * CB, CB)
                        sp.wait_ge(s["x1_ready"], past(b + 1))
                        sp.dma_start(G["sum0"].rearrange("(c p) d -> p c d", p=P)[:, here, :], X[:, here, :]
                                     ).then_inc(s["x1_stored"], 16)

                run(sp, step)
                sp.wait_ge(s["x1_stored"], past(16 * B))
                sp.wait_ge(s["rows_stored"], past(16 * B))

            @block.tensor
            def _(pe):
                def step(i, parts):
                    if "mix" in parts:
                        b = i - 1
                        pe.wait_ge(s["xnT_ready"], past(b + 1))
                        pe.wait_ge(s["sig_ready"], past(b))
                        for o in range(DC):
                            for m in range(DC):
                                mm = pe.matmul(pq[o][:], wq[:, m, o * P:(o + 1) * P], xnT[:, m, :],
                                               start=m == 0, stop=m == DC - 1)
                        mm.then_inc(s["q_ps"], 1)
                    if "turn" in parts:
                        pe.wait_ge(s["xn_ready"], past(i + 1))
                        pe.wait_ge(s["xnT_ready"], past(i))
                        turn(pe, G, lambda m: pt[m], lambda t, m: xn[:, t, m * P:(m + 1) * P]
                             ).then_inc(s["turned"], 1)
                    if "route" in parts:
                        b = i - 2
                        pe.wait_ge(s["fx_ready"], past(b + 1))
                        turn(pe, G, lambda m: po[m], lambda t, m: fx[:, t, m * P:(m + 1) * P]
                             ).then_inc(s["fturned"], 1)
                    if "mix" in parts:
                        b = i - 1
                        pe.wait_ge(s["yT_ready"], past(b + 1))
                        pe.wait_ge(s["fxT_ready"], past(b))
                        for t in range(CB):
                            for m in range(DC):
                                mm = pe.matmul(po[t // 2][:, t % 2 * D:(t % 2 + 1) * D], yT[:, m, t * P:(t + 1) * P],
                                               wo[:, m, :], start=m == 0, stop=m == DC - 1)
                        mm.then_inc(s["out_ps"], 1)
                    if "route" in parts:
                        b = i - 2
                        pe.wait_ge(s["fxT_ready"], past(b + 1))
                        pe.wait_ge(s["shift_ready"], past(b))
                        for t in range(CB):
                            pe.matmul(pl[:, t * E:(t + 1) * E], G["ones"][0:1, :], bs[:], start=True, stop=False)
                            for m in range(DC):
                                mm = pe.matmul(pl[:, t * E:(t + 1) * E], fxT[:, m, t * P:(t + 1) * P], ws[:, m, :],
                                               start=False, stop=m == DC - 1)
                        mm.then_inc(s["logits_ps"], 1)

                pe.wait_ge(s["loaded"], past(64))
                run(pe, step)

            @block.scalar
            def _(act):
                def step(i, parts):
                    if "mix" in parts:
                        b = i - 1
                        act.wait_ge(s["q_ps"], past(b + 1))
                        act.wait_ge(s["out_ps"], past(b))
                        for o in range(DC):
                            ins = act.activation(yT[:, o, :], pq[o][:], ACT.Sigmoid)
                        ins.then_inc(s["sig_ready"], 1)
                    if "turn" in parts:
                        act.wait_ge(s["turned"], past(i + 1))
                        act.wait_ge(s["q_ps"], past(i))
                        for m in range(DC):
                            ins = act.copy(xnT[:, m, :], pt[m][:])
                        ins.then_inc(s["xnT_ready"], 1)
                    if "route" in parts:
                        b = i - 2
                        act.wait_ge(s["fturned"], past(b + 1))
                        act.wait_ge(s["logits_ps"], past(b))
                        for m in range(DC):
                            ins = act.copy(fxT[:, m, :], po[m][:])
                        ins.then_inc(s["fxT_ready"], 1)
                        act.wait_ge(s["shift_ready"], past(b + 1))
                        act.activation(wide[1][:], wide[0][:], ACT.Exp).then_inc(s["rexp_ready"], 1)

                run(act, step)

            @block.gpsimd
            def _(pool):
                def step(i, parts):
                    if "norm" in parts:
                        b = i + 1
                        pool.wait_ge(s["stats_ready"], past(b + 1))
                        norm_rstd(pool, G, Chain(pool, s["pchain"], b), mv[0], rstd[0]).then_inc(s["rstd_ready"], 1)
                    if "mix" in parts:
                        b = i - 1
                        pool.wait_ge(s["fstats_ready"], past(b + 1))
                        norm_rstd(pool, G, Chain(pool, s["fpchain"], b), mv[1], rstd[1]).then_inc(s["frstd_ready"], 1)

                run(pool, step)

            @block.vector
            def _(dve):
                VROUTE = 4

                def rows(b):
                    return lambda t: X[:, b * CB + t, :]

                def step(i, parts):
                    if "mix" in parts:
                        bm = i - 1
                        dve.wait_ge(s["sig_ready"], past(bm + 1))
                        for o in range(DC):
                            ins = dve.tensor_scalar(yT[:, o, :], yT[:, o, :], G["ratio"][:, o, bass.ds(bm, 1)], None,
                                                    ALU.mult)
                        ins.then_inc(s["yT_ready"], 1)
                    if "norm" in parts:
                        bn = i + 1
                        alone(dve)
                        norm_stats(dve, Chain(dve, s["vchain"], bn), stats[0], mv[0], rows(bn)
                                   ).then_inc(s["stats_ready"], 1)
                        dve.wait_ge(s["rstd_ready"], past(bn + 1))
                        dve.wait_ge(s["stats_ready"], past(bn + 1))
                        dve.wait_ge(s["turned"], past(bn))
                        norm_apply(dve, lambda t: xn[:, t, :], rows(bn), mv[0], rstd[0]).then_inc(s["xn_ready"], 1)
                    if "mix" in parts:
                        dve.wait_ge(s["out_ps"], past(bm + 1))
                        for k in range(2):
                            rr = X[:, bass.ds(bm * CB + 2 * k, 2), :]
                            ins = dve.tensor_tensor(rr, rr, po[k][:].rearrange("p (t d) -> p t d", d=D), ALU.add)
                        ins.then_inc(s["x1_ready"], 1)
                        dve.wait_ge(s["x1_ready"], past(bm + 1))
                        alone(dve)
                        norm_stats(dve, Chain(dve, s["fvchain"], bm), stats[1], mv[1], rows(bm)
                                   ).then_inc(s["fstats_ready"], 1)
                    if "route" in parts:
                        b = i - 2
                        chain = Chain(dve, s["rchain"], b * VROUTE)
                        dve.wait_ge(s["logits_ps"], past(b + 1))
                        router_dve(dve, chain, pl[:, 0:CB * E].rearrange("p (t e) -> p t e", e=E), small, wide,
                                   s["rexp_ready"], b + 1, s["shift_ready"], G["prob"][:, bass.ds(b * CB, CB), :])
                        assert chain.n == VROUTE
                    if "mix" in parts:
                        dve.wait_ge(s["frstd_ready"], past(bm + 1))
                        dve.wait_ge(s["fstats_ready"], past(bm + 1))
                        dve.wait_ge(s["fturned"], past(bm))
                        dve.wait_ge(s["rows_stored"], past(bm * 16))
                        norm_apply(dve, lambda t: fx[:, t, :], rows(bm), mv[1], rstd[1]).then_inc(s["fx_ready"], 1)

                run(dve, step)


def in_front_pe(pe, G, pin, pall, flags):
    pe.matmul(pin[:, 0:E * NC], G["before"][:], flags, start=True, stop=True)
    return pe.matmul(pall[:, 0:E * NC], G["ones"][:], flags, start=True, stop=True)


def in_front_dve(dve, chain, rank, scan, keep, pin, pall):
    chain(dve.tensor_tensor_scan(scan[:], keep[:], pall[:, 0:E * NC], 0.0, ALU.mult, ALU.add))
    chain(dve.tensor_tensor(rank[:], scan[:], pall[:, 0:E * NC], ALU.subtract))
    chain(dve.tensor_tensor(rank[:], rank[:], pin[:, 0:E * NC], ALU.add))


def expert_choice(nc, G):
    with ExitStack() as ctx:
        st = Stage(nc, ctx, "pick")
        low, gained = st.sb("low", [P, E], U32), st.sb("gained", [P, E], U32)
        cand, took = st.sb("cand", [P, STEPS, E], U32), st.sb("took", [P, STEPS, E])
        pair = st.sb("pair", [P, STEPS], U32)
        cmp_ = st.sb("cmp", [P, STEPS, E, NC])
        more, equal = (st.sb(n, [P, E, NC]) for n in ("more", "equal"))
        reach, cnt, need = st.sb("reach", [P, STEPS, E]), st.sb("cnt", [P, E]), st.sb("need", [P, E])
        unit = st.sb("unit", [P, 1], U32)
        keep, rank, scan = (st.sb(n, [P, E * NC]) for n in ("keep", "rank", "scan"))
        ptot, pin, pall = st.ps("ptot", [P, S]), st.ps("pin", [P, S]), st.ps("pall", [P, S])
        vchain, counted, totalled = (st.sem(n) for n in ("vchain", "counted", "totalled"))
        prob = G["prob"][:].rearrange("p c e -> p e c")

        def wide(t):
            return t.unsqueeze(2).broadcast_to([P, E, NC])

        VPER, INIT, ROUNDS = 7, 4 + STEPS, BITS // 2
        with nc.Block() as block:

            @block.sync
            def _(sp):
                st.set_semaphores(sp)

            @block.vector
            def _(dve):
                chain = Chain(dve, vchain)
                chain(dve.memset(low[:], 0))
                chain(dve.memset(unit[:], 1 << (BITS - 2)))
                for k in range(STEPS):
                    chain(dve.memset(pair[:, k:k + 1], (k + 1) << (BITS - 2)))
                chain(dve.memset(keep[:], 1.0))
                chain(dve.memset(keep[:].rearrange("p (e c) -> p e c", c=NC)[:, :, 0:1], 0.0))
                assert chain.n == INIT
                with dve.Fori(0, ROUNDS) as i:
                    c = Chain(dve, vchain, i * VPER + INIT)
                    shape = [P, STEPS, E]
                    c(dve.tensor_tensor(cand[:], low[:].unsqueeze(1).broadcast_to(shape),
                                        pair[:].unsqueeze(2).broadcast_to(shape), ALU.bitwise_or))
                    c(dve.tensor_tensor(cmp_[:], prob.unsqueeze(1).broadcast_to([P, STEPS, E, NC]),
                                        cand[:].bitcast(F32).unsqueeze(3).broadcast_to([P, STEPS, E, NC]), ALU.is_ge))
                    dve.tensor_reduce(reach[:], cmp_[:], AX.X, ALU.add).then_inc(counted, 1)
                    dve.wait_ge(totalled, past(i + 1))
                    c(dve.scalar_tensor_tensor(out=took[:].rearrange("p k e -> p (k e)"), in0=ptot[:, 0:STEPS * E],
                                               scalar=float(CAP), in1=unit[:].broadcast_to([P, STEPS * E]),
                                               op0=ALU.is_ge, op1=ALU.mult))
                    with nc.allow_low_precision(reason="0 to 3 times a power of two, exact in either type"):
                        c(dve.tensor_reduce(gained[:], took[:].rearrange("p k e -> p e k"), AX.X, ALU.add))
                    c(dve.tensor_tensor(low[:], low[:], gained[:], ALU.bitwise_or))
                    c(dve.tensor_scalar(pair[:], pair[:], 2, None, ALU.logical_shift_right))
                    c(dve.tensor_scalar(unit[:], unit[:], 2, None, ALU.logical_shift_right))
                    assert c.n == VPER
                chain = Chain(dve, vchain, ROUNDS * VPER + INIT)
                edge = wide(low[:].bitcast(F32))
                chain(dve.tensor_tensor(more[:], prob, edge, ALU.is_gt))
                chain(dve.tensor_tensor(equal[:], prob, edge, ALU.is_equal))
                dve.tensor_reduce(cnt[:], more[:], AX.X, ALU.add).then_inc(counted, 1)
                dve.wait_ge(totalled, past(ROUNDS + 1))
                chain(dve.tensor_scalar(need[:], ptot[:, 0:E], -1.0, float(CAP), ALU.mult, ALU.add))
                in_front_dve(dve, chain, rank, scan, keep, pin, pall)
                rv = rank[:].rearrange("p (e c) -> p e c", c=NC)
                chain(dve.tensor_tensor(rv, rv, wide(need[:]), ALU.is_lt))
                chain(dve.tensor_tensor(rv, rv, equal[:], ALU.mult))
                dve.tensor_tensor(more[:], rv, more[:], ALU.add).then_inc(counted, 1)
                dve.wait_ge(counted, past(ROUNDS + 2))
                dve.wait_ge(totalled, past(ROUNDS + 2))
                in_front_dve(dve, chain, rank, scan, keep, pin, pall)
                chain(dve.scalar_tensor_tensor(out=rv, in0=rv, scalar=1.0, in1=more[:], op0=ALU.add, op1=ALU.mult))
                chain(dve.tensor_scalar(G["place"][:], rank[:], -1.0, None, ALU.add))
                chain(dve.tensor_copy(G["weight"][:].rearrange("p (e c) -> p e c", c=NC), prob))

            @block.tensor
            def _(pe):
                with pe.Fori(0, ROUNDS) as i:
                    pe.wait_ge(counted, past(i + 1))
                    pe.matmul(ptot[:, 0:STEPS * E], G["ones"][:], reach[:].rearrange("p k e -> p (k e)"),
                              start=True, stop=True).then_inc(totalled, 1)
                pe.wait_ge(counted, past(ROUNDS + 1))
                eq = equal[:].rearrange("p e c -> p (e c)")
                in_front_pe(pe, G, pin, pall, eq)
                pe.matmul(ptot[:, 0:E], G["ones"][:], cnt[:], start=True, stop=True).then_inc(totalled, 1)
                pe.wait_ge(counted, past(ROUNDS + 2))
                in_front_pe(pe, G, pin, pall, more[:].rearrange("p e c -> p (e c)")).then_inc(totalled, 1)


def lists(nc, G, tag, sets, per, cols, cut):
    with ExitStack() as ctx:
        st = Stage(nc, ctx, "li" + tag)
        n_all, I32 = sets * per, mybir.dt.int32
        whole, high, low = (st.sb(n, [P, n_all], I32) for n in ("whole", "high", "low"))
        highf, lowf = st.sb("highf", [P, n_all]), st.sb("lowf", [P, n_all])
        dt = BF16 if cut else F32
        token_parts, weight_parts = (2, 3) if cut else (1, 1)
        parts = token_parts + weight_parts
        hot_low = [st.sb(f"hot_low{i}", [P, SLAB, P], dt) for i in range(2)]
        hot_high = st.sb("hot_high", [P, SLAB, cols], dt)
        scaled = [st.sb(f"scaled{i}", [P, SLAB, parts, cols], dt) for i in range(2)]
        sums, total = st.sb("sums", [P, sets, parts, cols]), st.sb("total", [P, 2, sets, cols])
        if cut:
            place_in = st.sb("place_in", [P, 1])
            chunk_at, within = st.sb("chunk_at", [P, NC], BF16), st.sb("within", [P, NC], BF16)
            rest, wparts = st.sb("rest", [P, n_all]), [st.sb(f"wpart{k}", [P, n_all], BF16) for k in range(3)]
        spare = st.sb("spare", [P, sets, cols])
        pt = st.ps("pt", [P, S])
        slabs = per // SLAB
        vchain, built, summed = (st.sem(n) for n in ("vchain", "built", "summed"))
        INIT, VPER = 7 + (8 if cut else 0), 2 * slabs
        lane = G["lane"]
        with nc.Block() as block:

            @block.sync
            def _(sp):
                st.set_semaphores(sp)

            @block.vector
            def _(dve):
                chain = Chain(dve, vchain)
                chain(dve.tensor_copy(whole[:], G["place"][:, 0:n_all]))
                chain(dve.tensor_scalar(high[:], whole[:], 7, None, ALU.logical_shift_right))
                chain(dve.tensor_scalar(low[:], whole[:], P - 1, None, ALU.bitwise_and))
                chain(dve.tensor_copy(highf[:], high[:]))
                chain(dve.tensor_copy(lowf[:], low[:]))
                chain(dve.tensor_scalar(G["row"][:], G["spare1"][:].broadcast_to([P, COLS]), -1.0, None, ALU.add))
                chain(dve.memset(G["roww"][:], 0.0))
                if cut:
                    chain(dve.tensor_scalar(place_in[:], G["spare1"][:], -float(N), None, ALU.add))
                    chain(dve.tensor_scalar(chunk_at[:], G["token1"][:], place_in[:, 0:1], None, ALU.subtract))
                    chain(dve.tensor_copy(within[:], place_in[:].broadcast_to([P, NC])))
                    weight = G["weight"][:, 0:n_all]
                    chain(dve.tensor_copy(wparts[0][:], weight))
                    chain(dve.tensor_tensor(rest[:], weight, wparts[0][:], ALU.subtract))
                    chain(dve.tensor_copy(wparts[1][:], rest[:]))
                    chain(dve.tensor_tensor(rest[:], rest[:], wparts[1][:], ALU.subtract))
                    chain(dve.tensor_copy(wparts[2][:], rest[:]))
                    scales = [(chunk_at, True), (within, True)] + [(w, False) for w in wparts]
                else:
                    scales = [(G["token1"], True), (G["weight"], False)]
                assert chain.n == INIT
                with dve.Fori(0, sets) as r:
                    c = Chain(dve, vchain, r * VPER + INIT)
                    for s in range(slabs):
                        here, buf = bass.ds(r * per + s * SLAB, SLAB), s % 2
                        dve.wait_ge(summed, past(r * slabs + max(s - 1, 0)))

                        def chunks(t, width):
                            return t.unsqueeze(2).broadcast_to([P, SLAB, width])

                        c(dve.tensor_tensor(hot_low[buf][:], lane[:].unsqueeze(1).broadcast_to([P, SLAB, P]),
                                            chunks(lowf[:, here], P), ALU.is_equal))
                        c(dve.tensor_tensor(hot_high[:], lane[:, 0:cols].unsqueeze(1).broadcast_to([P, SLAB, cols]),
                                            chunks(highf[:, here], cols), ALU.is_equal))
                        first = s * SLAB % NC
                        for n, (scale, by_token) in enumerate(scales):
                            rows_ = slice(first, first + SLAB) if by_token else here
                            dve.tensor_tensor(scaled[buf][:, :, n, :], hot_high[:], chunks(scale[:, rows_], cols),
                                              ALU.mult).then_inc(built, 1)
                        dve.wait_ge(built, past((r * slabs + s + 1) * parts))
                        alone(dve)
                    assert c.n == VPER
                dve.wait_ge(summed, past(sets * slabs))
                chain = Chain(dve, vchain, sets * VPER + INIT)
                chain(dve.tensor_copy(sums[:].rearrange("p r k c -> p (r k c)"), pt[:, 0:sets * parts * cols]))
                chain(dve.tensor_reduce(total[:, 0], sums[:, :, 0:token_parts, :].rearrange("p r k c -> p r c k"),
                                        AX.X, ALU.add))
                chain(dve.tensor_reduce(total[:, 1], sums[:, :, token_parts:, :].rearrange("p r k c -> p r c k"),
                                        AX.X, ALU.add))
                chain(dve.tensor_scalar(spare[:], total[:, 0], 0.0, G["spare1"][:, 0:1], ALU.is_equal, ALU.mult))
                chain(dve.scalar_tensor_tensor(
                    out=G["row"][:, 0:sets * cols].rearrange("p (r c) -> p r c", c=cols), in0=total[:, 0],
                    scalar=-1.0, in1=spare[:], op0=ALU.add, op1=ALU.add))
                chain(dve.tensor_copy(G["roww"][:, 0:sets * cols].rearrange("p (r c) -> p r c", c=cols), total[:, 1]))

            @block.tensor
            def _(pe):
                with pe.Fori(0, sets) as r:
                    for s in range(slabs):
                        pe.wait_ge(built, past((r * slabs + s + 1) * parts))
                        alone(pe)
                        for i in range(SLAB):
                            mm = pe.matmul(pt[:, bass.ds(r * parts * cols, parts * cols)], hot_low[s % 2][:, i, :],
                                           scaled[s % 2][:, i, :, :].rearrange("p k c -> p (k c)"),
                                           start=s == 0 and i == 0, stop=s == slabs - 1 and i == SLAB - 1)
                        mm.then_inc(summed, 1)


def experts(nc, G, a, tag, gelu):
    rows, sums, tiles, size = G["rows" + tag[1]], G["sum" + tag[1]], TILES[tag], TILES_OF[tag]
    TC = size // P
    with ExitStack() as ctx:
        st = Stage(nc, ctx, "ex" + tag)
        w1, w2 = ([st.sb(f"{n}{i}", shape) for i in range(2)] for n, shape in (("w1", [P, DC, F]), ("w2", [P, FC, D])))
        b1, b2 = ([st.sb(f"{n}{i}", shape) for i in range(2)] for n, shape in (("b1", [P, FC]), ("b2", [1, D])))
        put, get = st.sb("put", [P, TC], U32), [st.sb(f"get{i}", [P, TC], U32) for i in range(2)]
        xg, xgT = [st.sb(f"xg{i}", [P, TC, D]) for i in range(2)], st.sb("xgT", [P, DC, size])
        hid, ys = st.sb("hid", [P, FC, size]), st.sb("ys", [P, TC, D])
        pt = [st.ps(f"pt{i}", [P, size]) for i in range(DC)]
        ph = [st.ps(f"ph{i}", [P, size]) for i in range(2)]
        po = [st.ps(f"po{i}", [P, D]) for i in range(2)]
        names = ("w1_in0", "w1_in1", "w2_in0", "w2_in1", "get_ready", "turned", "xgT_ready", "hid_ps", "hid_ready", "out_ps", "ys_ready",
                 "put_ready")
        (w1_in0, w1_in1, w2_in0, w2_in1, get_ready, turned, xgT_ready, hid_ps, hid_ready, out_ps, ys_ready, put_ready) = (st.sem(n) for n in names)
        gathered, added = [st.pool_dma_sem(f"gathered{i}") for i in range(2)], st.pool_dma_sem("added")
        w1_in, w2_in = (w1_in0, w1_in1), (w2_in0, w2_in1)

        def run(eng, tile, begin=0):
            with eng.Fori(begin // 2, tiles // 2) as pair:
                tile(pair * 2, 0, pair)
                tile(pair * 2 + 1, 1, pair)
            if tiles % 2:
                tile(tiles - 1, 0, tiles // 2)

        W1, W2, b1d, b2d = (a[f"{tag}_{n}"] for n in ("W1", "W2", "b1", "b2"))
        with nc.Block() as block:

            @block.sync
            def _(sp):
                st.set_semaphores(sp)

                def load(t, slot, pair):
                    e = t if tag == "L0" else sp.value_load(G["owner"][0:1, bass.ds(t, 1)], min_val=0, max_val=E - 1)
                    if not (isinstance(t, int) and t < 2):
                        sp.wait_ge(hid_ready, past((t - 1) * FC))
                        alone(sp)
                    sp.dma_start(w1[slot][:], W1[bass.ds(e, 1)].rearrange("e (c p) f -> p (e c) f", p=P)
                                 ).then_inc(w1_in[slot], 16)
                    sp.dma_start(b1[slot][:], b1d[bass.ds(e, 1)].rearrange("e p c -> p (e c)")).then_inc(w1_in[slot], 16)
                    if not (isinstance(t, int) and t < 2):
                        sp.wait_ge(out_ps, past((t - 1) * TC))
                        alone(sp)
                    sp.dma_start(w2[slot][:], W2[bass.ds(e, 1)].rearrange("e (c p) d -> p (e c) d", p=P)
                                 ).then_inc(w2_in[slot], 16)
                    sp.dma_start(b2[slot][:], b2d[bass.ds(e, 1), :]).then_inc(w2_in[slot], 16)

                load(0, 0, 0)
                sp.wait_ge(turned, past(1))
                load(1, 1, 0)
                run(sp, load, 2)

            @block.gpsimd
            def _(pool):
                def fetch(t, slot):
                    pool.tensor_copy(get[slot][:], G["row"][:, bass.ds(t * TC, TC)]).then_inc(get_ready, 1)
                    pool.wait_ge(get_ready, past(t + 1))
                    alone(pool)
                    for c in range(TC):
                        pool.indirect_dma_start(
                            out=xg[slot][:, c, :], out_offset=None, in_=rows,
                            in_offset=bass.IndirectOffsetOnAxis(ap=get[slot][:, c:c + 1], axis=0)
                        ).then_inc(gathered[slot], 16)

                def tile(t, slot, pair):
                    pool.wait_ge(gathered[slot], (pair + 1) * TC * 16)
                    pool.wait_ge(turned, past(t + 1))
                    alone(pool)
                    fetch(t + 2, slot)
                    pool.tensor_copy(put[:], G["row"][:, bass.ds(t * TC, TC)]).then_inc(put_ready, 1)
                    pool.wait_ge(put_ready, past(t + 1))
                    for c in range(TC):
                        pool.wait_ge(ys_ready, past(t * TC + c + 1))
                        if c:
                            pool.wait_ge(added, (t * TC + c) * 16)
                        alone(pool)
                        pool.indirect_dma_start(
                            out=sums, out_offset=bass.IndirectOffsetOnAxis(ap=put[:, c:c + 1], axis=0),
                            in_=ys[:, c, :], in_offset=None, compute_op=ALU.add).then_inc(added, 16)
                    pool.wait_ge(added, (t + 1) * TC * 16)
                    alone(pool)

                fetch(0, 0)
                fetch(1, 1)
                run(pool, tile)
                for slot in range(2):
                    pool.wait_ge(gathered[slot], (tiles + 2 + 1 - slot) // 2 * TC * 16)

            @block.tensor
            def _(pe):
                def turn_rows(slot, pair):
                    pe.wait_ge(gathered[slot], (pair + 1) * TC * 16)
                    for m in range(DC):
                        for c in range(TC):
                            ins = pe.transpose(pt[m][:, c * P:(c + 1) * P], xg[slot][:, c, m * P:(m + 1) * P], G["ident"][:])
                    ins.then_inc(turned, 1)

                turn_rows(0, 0)

                def tile(t, slot, pair):
                    pe.wait_ge(w1_in[slot], past((pair + 1) * 32))
                    pe.wait_ge(xgT_ready, past(t + 1))
                    for f in range(FC):
                        pe.wait_ge(hid_ready, past(t * FC + max(f - 1, 0)))
                        for m in range(DC):
                            mm = pe.matmul(ph[f % 2][:], w1[slot][:, m, f * P:(f + 1) * P], xgT[:, m, :],
                                           start=m == 0, stop=m == DC - 1)
                        mm.then_inc(hid_ps, 1)
                    turn_rows(1 - slot, pair + slot)
                    pe.wait_ge(hid_ready, past(t * FC + FC))
                    pe.wait_ge(w2_in[slot], past((pair + 1) * 32))
                    for c in range(TC):
                        pe.wait_ge(ys_ready, past(t * TC + max(c - 1, 0)))
                        pe.matmul(po[c % 2][:], G["ones"][0:1, :], b2[slot][:], start=True, stop=False)
                        for f in range(FC):
                            mm = pe.matmul(po[c % 2][:], hid[:, f, c * P:(c + 1) * P], w2[slot][:, f, :],
                                           start=False, stop=f == FC - 1)
                        mm.then_inc(out_ps, 1)

                run(pe, tile)

            @block.scalar
            def _(act):
                def tile(t, slot, pair):
                    act.wait_ge(out_ps, past(t * TC))
                    for f in range(FC):
                        act.wait_ge(hid_ps, past(t * FC + f + 1))
                        act.activation(hid[:, f, :], ph[f % 2][:], gelu, bias=b1[slot][:, f:f + 1]).then_inc(hid_ready, 1)

                run(act, tile)

            @block.vector
            def _(dve):
                def save_turned():
                    for m in range(DC):
                        ins = dve.tensor_copy(xgT[:, m, :], pt[m][:])
                    ins.then_inc(xgT_ready, 1)

                dve.wait_ge(turned, past(1))
                save_turned()
                with dve.Fori(0, tiles) as t:
                    dve.wait_ge(turned, past(t + 2))
                    dve.wait_ge(hid_ps, past(t * FC + FC))
                    save_turned()
                    dve.wait_ge(put_ready, past(t + 1))
                    for c in range(TC):
                        dve.wait_ge(out_ps, past(t * TC + c + 1))
                        dve.tensor_scalar(ys[:, c, :], po[c % 2][:], G["roww"][:, bass.ds(t * TC + c, 1)], None,
                                          ALU.mult).then_inc(ys_ready, 1)


ROUND = CB * HG
LAG = 2


def job_table(self_, first, last):
    jobs = [(0, 7, "d", "neg1"), (1, 7, "d", "neg2"), (2, 7, "d", "neg3"),
            (1, 4, "d", "out0"), (2, 4, "d", "out1"), (3, 4, "d", "out2")]
    if not last:
        jobs += [(0, 11, "a", "turn0+"), (0, 13, "a", "turn1+"), (1, 0, "a", "k0+"), (1, 2, "a", "q0+"),
                 (1, 4, "a", "k1+"), (1, 6, "a", "q1+"), (1, 8, "a", "v0+"), (1, 10, "a", "v1+"),
                 (3, 7, "d", "neg0+")]
    if not first:
        jobs += [(0, 4, "d", "out3-"), (0, 7, "a", "att0-"), (0, 9, "a", "att1-"),
                 (0, 11, "d", "y0-"), (0, 13, "d", "y1-")]
        if self_:
            jobs += [(2, 13, "a", "u0-"), (3, 0, "a", "u1-"), (3, 9, "d", "logits-")]
    return sorted(jobs)


class Jobs:

    BEFORE = {"a": ["turn0+", "turn1+", "k0+", "q0+", "k1+", "q1+", "v0+", "v1+"], "d": ["neg0+"]}
    BEHIND = {"d": ["out3-", "y0-", "y1-"], "a": ["att0-", "att1-"]}

    def __init__(self, self_):
        names = {k: {bank: [n for _, _, b, n in job_table(self_, *k) if b == bank] for bank in "ad"}
                 for k in ((True, False), (False, False), (False, True))}
        self.names, self.self_ = names, self_

    def base(self, bank, b):
        if isinstance(b, int) and b == 0:
            return len(self.BEFORE[bank])
        return (b - 1) * len(self.names[False, False][bank]) + (
            len(self.BEFORE[bank]) + len(self.names[True, False][bank]))

    def index(self, bank, b, first, last, name):
        return self.base(bank, b) + self.names[first, last][bank].index(name)

    def behind(self, bank):
        return self.base(bank, B - 1) + len(self.names[False, True][bank])


def attention(nc, G, a, tag, self_):
    with ExitStack() as ctx:
        st = Stage(nc, ctx, "at" + tag)
        wq, wk, wv, wo = (st.sb(n, [P, DC, D]) for n in ("wq", "wk", "wv", "wo"))
        stats, mv, rstd = st.sb("stats", [P, CB, 6]), st.sb("mv", [P, CB, 2]), st.sb("rstd", [P, CB])
        xn, xnT = st.sb("xn", [P, CB, D]), st.sb("xnT", [P, DC, S])
        src = xnT if self_ else st.sb("src", [P, DC, S])
        full = {n: st.sb(f"{n}f", [P, DC, S]) for n in "qk"}
        parts = {n: [st.sb(f"{n}{k}", [P, DC, S], BF16) for k in range(3)] for n in "qk"}
        stack = {n: [st.sb(f"{n}stack{i}", [KR + 3, H, S], BF16) for i in range(2)] for n in "qk"}
        vals = [st.sb(f"vals{i}", [P, CB, H, 32]) for i in range(2)]
        tops, rest = [st.sb(f"tops{i}", [P, CB, HG]) for i in range(2)], st.sb("rest", [P, CB, HG])
        neg3 = st.sb("neg3", [P, CB, 3, HG], BF16)
        negT = st.sb("negT", [3 * HG, S], BF16)
        prob = [st.sb(f"prob{i}", [P, S]) for i in range(4)]
        outT, rec = st.sb("outT", [P, S]), st.sb("rec", [P, CB, HG])
        att, attT = st.sb("att", [P, CB, D]), st.sb("attT", [P, DC, S])
        pm = [st.ps(f"pm{i}", [P, S]) for i in range(2)]
        ps = [st.ps(f"ps{i}", [P, S]) for i in range(2)]
        po = [st.ps(f"po{i}", [P, S]) for i in range(2)]
        pj = {bank: st.ps("pj" + bank, [P, S]) for bank in "ad"}
        names = ["loaded", "src_in", "stats_ready", "rstd_ready", "xn_ready", "cut0", "cut1", "stacked0", "stacked1",
                 "m_ps", "m_done", "neg_ready", "neg_in", "s_ps", "p_ready", "pv_done", "o_saved", "job_a", "job_d",
                 "free_a", "free_d", "vchain", "pchain", "cleared"]
        if self_:
            names += ["y_stats", "y_rstd", "yn_ready", "u_ready", "rows_stored", "shift_ready", "rexp_ready", "xn_kept"]
            bq, bk = st.sb("bq", [P, DC]), st.sb("bk", [P, DC])
            bv, bo = st.sb("bv", [1, D]), st.sb("bo", [1, D])
            gain, shift = st.sb("gain", [P, D]), st.sb("shift", [P, D])
            gw, gb = st.sb("gw", [P, DC, E]), st.sb("gb", [1, E])
            small = [st.sb(n, [P, CB]) for n in ("rtop", "rsum", "rrec")]
            wide = [st.sb(n, [P, CB, E]) for n in ("rshift", "rexp")]
            ukept = [st.sb(f"ukept{i}", [P, CB, D]) for i in range(2)]
            yn, u2 = st.sb("yn", [P, CB, D]), st.sb("u2", [P, CB, D])
            uT = st.sb("uT", [P, DC, S])
            ymv, yrstd = st.sb("ymv", [P, CB, 2]), st.sb("yrstd", [P, CB])
            bias = {"q": bq, "k": bk}
        else:
            names += ["x_first", "x_rest"]
            junk = st.sb("junk", [P, 2, S], BF16)
        s = {n: st.sem(n) for n in names}
        X, J = G["x"], Jobs(self_)
        PER = NG * ROUND
        LOADS = 4 + (8 if self_ else 0)
        QK = ("k", "q") * 2

        def first_last(b):
            return (isinstance(b, int) and b == 0, isinstance(b, int) and b == B - 1)

        def run(eng, before, batch, behind):
            before()
            batch(0, 0)
            with eng.Fori(0, (B - 2) // 2) as pair:
                batch(pair * 2 + 1, 1)
                batch(pair * 2 + 2, 0)
            batch(B - 1, 1)
            behind()

        def jobs_at(b, g, step, bank=None):
            return [(k, n) for (jg, js, k, n) in job_table(self_, *first_last(b))
                    if (jg, js) == (g, step) and bank in (None, k)]

        def job_index(bank, b, name):
            return J.index(bank, b, *first_last(b), name)

        with nc.Block() as block:

            @block.sync
            def _(sp):
                st.set_semaphores(sp)

                def load_x(here, name):
                    sp.dma_start(X[:, here, :], G["sum0"][0:N, :].rearrange("(c p) d -> p c d", p=P)[:, here, :]
                                 ).then_inc(s[name], 16)

                if not self_:
                    load_x(slice(0, CB), "x_first")
                for dst, name in ((wk, "Wk"), (wq, "Wq"), (wv, "Wv"), (wo, "Wo")):
                    sp.dma_start(dst[:], a[f"{tag}_{name}"].rearrange("(c p) n -> p c n", p=P)).then_inc(s["loaded"], 16)
                if self_:
                    for dst, name in ((bq, "bq"), (bk, "bk")):
                        sp.dma_start(dst[:], a[f"{tag}_{name}"]).then_inc(s["loaded"], 16)
                    for dst, name in ((bv, "bv"), (bo, "bo"), (gb, "gate_b")):
                        sp.dma_start(dst[:], a[f"{tag}_{name}"]).then_inc(s["loaded"], 16)
                    for dst, name in ((gain, "ln1_g"), (shift, "ln1_b")):
                        sp.dma_start(dst[:], a[f"{tag}_{name}"].broadcast_to([P, D])).then_inc(s["loaded"], 16)
                    sp.dma_start(gw[:], a[f"{tag}_gate_w"].rearrange("(c p) n -> p c n", p=P)).then_inc(s["loaded"], 16)

                def load_source(b):
                    if not self_:
                        sp.dma_start(src[:], a["ctxT"].rearrange("(c p) n -> p c n", p=P)[:, :, bass.ds(b * S, S)]
                                     ).then_inc(s["src_in"], 16)

                def fill(b, par, o):
                    for i, (n, terms) in enumerate((("k", K_TERMS), ("q", Q_TERMS))):
                        sp.wait_ge(s[f"cut{o}"], past(b * 2 + i + 1))
                        for k, part in enumerate(terms):
                            sp.dma_start(stack[n][par][16 * k:16 * k + 16, o * HC:(o + 1) * HC, :],
                                         parts[n][part][:, o, :]).then_inc(s[f"stacked{o}"], 16)

                def negatives(b, par, g, index):
                    sp.wait_ge(s["free_d"], past(index + 1))
                    sp.dma_start(stack["q"][par][KR:KR + 3, g * HG:(g + 1) * HG, :], negT[:]).then_inc(s["neg_in"], 16)

                def store_rows(b):
                    sp.wait_ge(s["u_ready"], past(b + 1))
                    sp.dma_start(G["rows1"].rearrange("(c p) d -> p c d", p=P)[:, bass.ds(b * CB, CB), :], u2[:]
                                 ).then_inc(s["rows_stored"], 16)

                def before():
                    load_source(0)
                    if not self_:
                        load_x(slice(CB, NC), "x_rest")
                    fill(0, 0, 0)
                    fill(0, 0, 1)
                    negatives(0, 0, 0, 0)

                def batch(b, par):
                    first, last = first_last(b)
                    if not last and not self_:
                        sp.wait_ge(s["job_a"], past(J.base("a", b)))
                        alone(sp)
                        load_source(b + 1)
                    negatives(b, par, 1, job_index("d", b, "neg1"))
                    if not last:
                        sp.wait_ge(s["s_ps"], past(b * PER))
                        fill(b + 1, 1 - par, 0)
                    negatives(b, par, 2, job_index("d", b, "neg2"))
                    negatives(b, par, 3, job_index("d", b, "neg3"))
                    if self_ and not first:
                        store_rows(b - 1)
                    if not last:
                        fill(b + 1, 1 - par, 1)
                        negatives(b + 1, 1 - par, 0, job_index("d", b, "neg0+"))

                def behind():
                    if self_:
                        store_rows(B - 1)
                        sp.wait_ge(s["rows_stored"], past(16 * B))

                run(sp, before, batch, behind)

            @block.tensor
            def _(pe):
                def turn_chunk(bank, rows_, m):
                    for t in range(CB):
                        ins = pe.transpose(pj[bank][:, t * P:(t + 1) * P], rows_[:, t, m * P:(m + 1) * P], G["ident"][:])
                    return ins

                def project(w, x_, o):
                    for m in range(DC):
                        mm = pe.matmul(pj["a"][:], w[:, m, o * P:(o + 1) * P], x_[:, m, :],
                                       start=m == 0, stop=m == DC - 1)
                    return mm

                def by_token(bank, xT_, w, row, half):
                    for i in range(2):
                        t, out = half * 2 + i, pj[bank][:, i * D:(i + 1) * D]
                        if row is not None:
                            pe.matmul(out, G["ones"][0:1, :], row[:], start=True, stop=False)
                        for m in range(DC):
                            mm = pe.matmul(out, xT_[:, m, t * P:(t + 1) * P], w[:, m, :],
                                           start=m == 0 and row is None, stop=m == DC - 1)
                    return mm

                def job(b, bank, name, index):
                    kind, i = name[:-1] if name[-1] in "+-" else name, 0
                    kind, i = (kind, 0) if kind == "logits" else (kind[:-1], int(kind[-1]))
                    if not (isinstance(index, int) and index == 0):
                        pe.wait_ge(s["free_" + bank], past(index))
                    if kind == "turn":
                        pe.wait_ge(s["xn_ready"], past(b + 1))
                        ins = turn_chunk("a", xn, i)
                    elif kind in ("k", "q"):
                        if kind == "k" and not self_:
                            pe.wait_ge(s["src_in"], past((b + 1) * 16))
                        ins = project({"k": wk, "q": wq}[kind], {"k": src, "q": xnT}[kind], i)
                    elif kind == "v":
                        ins = by_token("a", src, wv, bv if self_ else None, i)
                    elif kind == "neg":
                        pe.wait_ge(s["neg_ready"], past(b * NG + i + 1))
                        for t in range(CB):
                            ins = pe.transpose(pj["d"][:].bitcast(BF16)[0:3 * HG, t * P:(t + 1) * P],
                                               neg3[:, t, :, :].rearrange("p k h -> p (k h)"), G["identb"][:])
                    elif kind == "out":
                        pe.wait_ge(s["o_saved"], past(b * NG + i + 1))
                        for t in range(CB):
                            ins = pe.transpose(pj["d"][:, t * P:(t + 1) * P], outT[:, t * P:(t + 1) * P], G["ident"][:])
                    elif kind == "att":
                        ins = turn_chunk("a", att, i)
                    elif kind == "y":
                        ins = by_token("d", attT, wo, bo if self_ else None, i)
                    elif kind == "u":
                        pe.wait_ge(s["u_ready"], past(b + 1))
                        ins = turn_chunk("a", u2, i)
                    else:
                        for t in range(CB):
                            out = pj["d"][:, t * E:(t + 1) * E]
                            pe.matmul(out, G["ones"][0:1, :], gb[:], start=True, stop=False)
                            for m in range(DC):
                                ins = pe.matmul(out, uT[:, m, t * P:(t + 1) * P], gw[:, m, :],
                                                start=False, stop=m == DC - 1)
                    ins.then_inc(s["job_" + bank], 1)

                def max_step(b, par, g, n):
                    i = g * ROUND + n
                    h, t = g * HG + n % HG, n // HG
                    if not (isinstance(b, int) and b == 0 and i < 2):
                        pe.wait_ge(s["m_done"], past(b * PER + i - 1))
                    if n == 0 and g % 2 == 0:
                        pe.wait_ge(s[f"stacked{g // 2}"], past((b + 1) * 2 * len(Q_TERMS) * 16))
                    pe.matmul(pm[i % 2][:], stack["q"][par][0:KR, h, t * P:(t + 1) * P],
                              stack["k"][par][0:KR, h, :], start=True, stop=True).then_inc(s["m_ps"], 1)

                def score_step(b, par, g, n):
                    i = g * ROUND + n
                    kc, h = n // HG, g * HG + n % HG
                    if isinstance(b, int) and b == 0 and g < 2 and n == 0:
                        pe.wait_ge(s["cleared"], past(3 * g + 3))
                    if n == 0:
                        pe.wait_ge(s["neg_in"], past((b * NG + g + 1) * 16))
                    if not (isinstance(b, int) and b == 0 and i < 2):
                        pe.wait_ge(s["p_ready"], past(b * PER + i - 1))
                    mm = pe.matmul(ps[i % 2][:], stack["k"][par][0:KR + 3, h, kc * P:(kc + 1) * P],
                                   stack["q"][par][0:KR + 3, h, :], start=True, stop=self_)
                    if not self_:
                        mm = pe.matmul(ps[i % 2][:], G["identb"][:], G["bias"][1][:, kc, :], start=False, stop=True)
                    mm.then_inc(s["s_ps"], 1)

                def value_step(b, par, g, n):
                    i = g * ROUND + n
                    kc, j = n // HG, n % HG
                    pe.wait_ge(s["p_ready"], past(b * PER + i + 1))
                    if n == 0 and not (isinstance(b, int) and b == 0 and g < 2):
                        pe.wait_ge(s["o_saved"], past(b * NG + g - 1))
                    pe.matmul(po[g % 2][j * 32:j * 32 + 32, :], vals[par][:, kc, g * HG + j, :], prob[i % 4][:],
                              start=kc == 0, stop=kc == CB - 1).then_inc(s["pv_done"], 1)

                def before():
                    pe.wait_ge(s["loaded"], past(16 * LOADS))
                    for n, name in enumerate(Jobs.BEFORE["a"]):
                        job(0, "a", name, n)
                    for n in range(ROUND):
                        max_step(0, 0, 0, n)
                    job(0, "d", "neg0+", 0)
                    for n in range(ROUND):
                        max_step(0, 0, 1, n)

                def batch(b, par):
                    first, last = first_last(b)
                    pe.wait_ge(s["free_a"], past(J.base("a", b)))
                    for g in range(NG):
                        for n in range(ROUND):
                            for bank, name in jobs_at(b, g, n):
                                if name in ("att0-", "y0-"):
                                    bank_, name_ = {"att0-": ("d", "out3-"), "y0-": ("a", "att1-")}[name]
                                    pe.wait_ge(s["free_" + bank_], past(job_index(bank_, b, name_) + 1))
                                if name == "logits-":
                                    pe.wait_ge(s["free_a"], past(job_index("a", b, "u1-") + 1))
                                job(b + {"+": 1, "-": -1}.get(name[-1], 0), bank, name, job_index(bank, b, name))
                            score_step(b, par, g, n)
                            if n >= LAG:
                                value_step(b, par, g, n - LAG)
                            elif g:
                                value_step(b, par, g - 1, ROUND + n - LAG)
                            elif not first:
                                value_step(b - 1, 1 - par, NG - 1, ROUND + n - LAG)
                            if g < 2:
                                max_step(b, par, g + 2, n)
                            elif not last:
                                max_step(b + 1, 1 - par, g - 2, n)

                def behind():
                    for n in range(ROUND - LAG, ROUND):
                        value_step(B - 1, 1, NG - 1, n)
                    na, nd = J.behind("a"), J.behind("d")
                    job(B - 1, "d", "out3-", nd)
                    pe.wait_ge(s["free_d"], past(nd + 1))
                    job(B - 1, "a", "att0-", na)
                    job(B - 1, "a", "att1-", na + 1)
                    pe.wait_ge(s["free_a"], past(na + 2))
                    job(B - 1, "d", "y0-", nd + 1)
                    job(B - 1, "d", "y1-", nd + 2)
                    if self_:
                        job(B - 1, "a", "u0-", na + 2)
                        job(B - 1, "a", "u1-", na + 3)
                        pe.wait_ge(s["free_a"], past(na + 4))
                        job(B - 1, "d", "logits-", nd + 3)

                run(pe, before, batch, behind)

            @block.scalar
            def _(act):
                def job(b, par, name, index):
                    kind, i = name[:-2], int(name[-2])
                    act.wait_ge(s["job_a"], past(index + 1))
                    if kind == "turn":
                        ins = act.copy(xnT[:, i, :], pj["a"][:])
                    elif kind in ("k", "q"):
                        if not (isinstance(b, int) and b == 0):
                            act.wait_ge(s[f"cut{i}"], past((b - 1) * 2 + (1 if kind == "k" else 2)))
                        if self_:
                            ins = act.activation(full[kind][:, i, :], pj["a"][:], ACT.Identity,
                                                 bias=bias[kind][:, i:i + 1])
                        else:
                            ins = act.copy(full[kind][:, i, :], pj["a"][:])
                    elif kind == "v":
                        if isinstance(b, int) and b < 2 and i == 0:
                            act.wait_ge(s["cleared"], past(3 * b + 3))
                        ins = act.copy(vals[par][:, 2 * i:2 * i + 2, :, 0:HD],
                                       pj["a"][:].rearrange("p (t h d) -> p t h d", t=2, h=H))
                    elif kind == "att":
                        ins = act.copy(attT[:, i, :], pj["a"][:])
                    else:
                        ins = act.copy(uT[:, i, :], pj["a"][:])
                    ins.then_inc(s["free_a"], 1)

                def save_group(b, g):
                    act.wait_ge(s["pv_done"], past(b * PER + (g + 1) * ROUND))
                    act.copy(outT[:], po[g % 2][:]).then_inc(s["o_saved"], 1)

                def router_exp(b):
                    act.wait_ge(s["shift_ready"], past(b + 1))
                    act.activation(wide[1][:], wide[0][:], ACT.Exp).then_inc(s["rexp_ready"], 1)

                def before():
                    if self_:
                        act.wait_ge(s["loaded"], past(16 * LOADS))
                    for n, name in enumerate(Jobs.BEFORE["a"]):
                        job(0, 0, name, n)

                def batch(b, par):
                    first, last = first_last(b)
                    for g in range(NG):
                        for n in range(ROUND):
                            i = g * ROUND + n
                            if n == LAG + 1 and (g or not first):
                                pb, pg = (b, g - 1) if g else (b - 1, NG - 1)
                                save_group(pb, pg)
                            for _, name in jobs_at(b, g, n - 1, "a"):
                                job(b + {"+": 1, "-": -1}[name[-1]], 1 - par, name, job_index("a", b, name))
                            if self_ and not first and (g, n) == (3, 10):
                                router_exp(b - 1)
                            act.wait_ge(s["s_ps"], past(b * PER + i + 1))
                            if not (isinstance(b, int) and b == 0 and i < 4):
                                act.wait_ge(s["pv_done"], past(b * PER + i - 3))
                            act.activation(prob[i % 4][:], ps[i % 2][:], ACT.Exp, scale=SCALE).then_inc(s["p_ready"], 1)

                def behind():
                    na = J.behind("a")
                    save_group(B - 1, NG - 1)
                    job(B - 1, 1, "att0-", na)
                    job(B - 1, 1, "att1-", na + 1)
                    if self_:
                        job(B - 1, 1, "u0-", na + 2)
                        job(B - 1, 1, "u1-", na + 3)
                        router_exp(B - 1)

                run(act, before, batch, behind)

            @block.gpsimd
            def _(pool):
                chain = Chain(pool, s["pchain"])

                def cut(b, o):
                    for i, n in enumerate("kq"):
                        x_, (hi, mid, lo) = full[n][:, o, :], (p[:, o, :] for p in parts[n])
                        if isinstance(b, int) and b == 0:
                            pool.wait_ge(s["free_a"], past(Jobs.BEFORE["a"].index(f"{n}{o}+") + 1))
                        else:
                            pool.wait_ge(s["free_a"], past(index_a(b, f"{n}{o}+") + 1))
                            pool.wait_ge(s[f"stacked{o}"], past(b * 2 * len(Q_TERMS) * 16))
                        alone(pool)
                        chain(pool.tensor_copy(hi, x_))
                        chain(pool.tensor_tensor(x_, x_, hi, ALU.subtract))
                        chain(pool.tensor_copy(mid, x_))
                        pool.tensor_tensor(lo, x_, mid, ALU.subtract).then_inc(s[f"cut{o}"], 1)

                def index_a(b, name):
                    first = isinstance(b, int) and b == 1
                    return J.index("a", b - 1, first, False, name)

                def norm(b):
                    pool.wait_ge(s["stats_ready"], past(b + 1))
                    norm_rstd(pool, G, chain, mv, rstd).then_inc(s["rstd_ready"], 1)

                def keep(b, par):
                    pool.wait_ge(s["xn_ready"], past(b + 1))
                    if not (isinstance(b, int) and b < 2):
                        pool.wait_ge(s["u_ready"], past(b - 1))
                    alone(pool)
                    pool.tensor_copy(ukept[par][:], xn[:]).then_inc(s["xn_kept"], 1)

                def clear(i):
                    pool.wait_ge(s["cut1" if i else "rstd_ready"], past(i + 1))
                    pool.memset(stack["k"][i][KR:KR + 3, :, :], 1.0).then_inc(s["cleared"], 1)
                    pool.wait_ge(s["cleared"], past(3 * i + 1))
                    pool.memset(vals[i][:], 0.0).then_inc(s["cleared"], 1)
                    pool.wait_ge(s["cleared"], past(3 * i + 2))
                    pool.memset(vals[i][:, :, :, HD:HD + 1], 1.0).then_inc(s["cleared"], 1)
                    pool.wait_ge(s["cleared"], past(3 * i + 3))

                def norm_y(b):
                    pool.wait_ge(s["y_stats"], past(b + 1))
                    norm_rstd(pool, G, chain, ymv, yrstd).then_inc(s["y_rstd"], 1)

                def add_y(b, par):
                    pool.wait_ge(s["yn_ready"], past(b + 1))
                    alone(pool)
                    chain(pool.tensor_tensor(yn[:], yn[:], gain[:].unsqueeze(1).broadcast_to([P, CB, D]), ALU.mult))
                    chain(pool.tensor_tensor(yn[:], yn[:], shift[:].unsqueeze(1).broadcast_to([P, CB, D]), ALU.add))
                    if not (isinstance(b, int) and b == 0):
                        pool.wait_ge(s["rows_stored"], past(b * 16))
                        alone(pool)
                    pool.tensor_tensor(u2[:], yn[:], ukept[par][:], ALU.add).then_inc(s["u_ready"], 1)
                    pool.wait_ge(s["u_ready"], past(b + 1))
                    alone(pool)
                    rr = X[:, bass.ds(b * CB, CB), :]
                    chain(pool.tensor_tensor(rr, rr, u2[:], ALU.add))

                def before():
                    norm(0)
                    clear(0)
                    cut(0, 0)
                    cut(0, 1)
                    clear(1)
                    if self_:
                        keep(0, 0)

                PPER = 12 + 1 + (4 if self_ else 0)

                def batch(b, par):
                    first, last = first_last(b)
                    if not isinstance(b, int):
                        chain.base, chain.n = (b - 1) * PPER + start[0], 0
                    elif last:
                        chain.base, chain.n = start[0] + (B - 2) * PPER, 0
                    if not last:
                        norm(b + 1)
                        cut(b + 1, 0)
                    if self_ and not first:
                        norm_y(b - 1)
                        add_y(b - 1, 1 - par)
                    if not last:
                        cut(b + 1, 1)
                        if self_:
                            keep(b + 1, 1 - par)
                    if first:
                        start[0] = chain.n
                    elif not last:
                        assert chain.n == PPER

                def behind():
                    if self_:
                        norm_y(B - 1)
                        add_y(B - 1, 1)

                start = [0]
                run(pool, before, batch, behind)

            @block.vector
            def _(dve):
                chain = Chain(dve, s["vchain"])

                def norm_chunk(b, t):
                    if not self_ and isinstance(b, int) and t == 0:
                        dve.wait_ge(s["x_rest" if b else "x_first"], past(16))
                    alone(dve)
                    ins = dve.bn_stats(stats[:, t, :], X[:, b * CB + t, :])
                    if t == CB - 1:
                        chain(ins)
                        for t in range(CB):
                            ins = dve.bn_aggr(mv[:, t, :], stats[:, t, :])
                        ins.then_inc(s["stats_ready"], 1)

                def apply_chunk(b, t):
                    if t == 0:
                        dve.wait_ge(s["rstd_ready"], past(b + 1))
                        dve.wait_ge(s["stats_ready"], past(b + 1))
                        if not (isinstance(b, int) and b == 0):
                            dve.wait_ge(s["job_a"], past(J.base("a", b - 1)))
                            if self_:
                                dve.wait_ge(s["xn_kept"], past(b))
                    ins = dve.tensor_scalar(xn[:, t, :], X[:, b * CB + t, :], mv[:, t, 0:1], rstd[:, t:t + 1],
                                            ALU.subtract, ALU.mult)
                    if t == CB - 1:
                        ins.then_inc(s["xn_ready"], 1)

                def max_step(b, g, n):
                    i, t, j = g * ROUND + n, n // HG, n % HG
                    dve.wait_ge(s["m_ps"], past(b * PER + i + 1))
                    if self_:
                        ins = dve.tensor_reduce(tops[g % 2][:, t, j:j + 1], pm[i % 2][:], AX.X, ALU.max)
                    else:
                        alone(dve)
                        ins = dve.tensor_tensor_reduce(junk[:, i % 2, :], pm[i % 2][:], G["bias"][0][:, t, :], 1.0,
                                                       -BIG / 2, ALU.add, ALU.max, tops[g % 2][:, t, j:j + 1])
                    ins.then_inc(s["m_done"], 1)

                def cut_maxima(b, g, jobs_before, k):
                    top = tops[g % 2]
                    if k == 0:
                        dve.wait_ge(s["m_done"], past(b * PER + (g + 1) * ROUND))
                        if jobs_before is not None:
                            dve.wait_ge(s["job_d"], past(jobs_before))
                        alone(dve)
                        chain.mark(dve.tensor_scalar(neg3[:, :, 0, :], top[:], -1.0, None, ALU.mult))
                        return
                    chain.await_last()
                    if k == 1:
                        chain.mark(dve.scalar_tensor_tensor(out=rest[:], in0=top[:], scalar=-1.0,
                                                            in1=neg3[:, :, 0, :], op0=ALU.mult, op1=ALU.subtract))
                    elif k == 2:
                        chain.mark(dve.tensor_copy(neg3[:, :, 1, :], rest[:]))
                    else:
                        dve.tensor_tensor(neg3[:, :, 2, :], rest[:], neg3[:, :, 1, :], ALU.subtract
                                          ).then_inc(s["neg_ready"], 1)

                def job(b, name, index):
                    kind, i = (name[:-1], 0) if name == "logits-" else (name.rstrip("+-")[:-1], int(name.rstrip("+-")[-1]))
                    bank = pj["d"]
                    dve.wait_ge(s["job_d"], past(index + 1))
                    if kind == "neg":
                        if not (isinstance(b, int) and b == 0 and i == 0):
                            dve.wait_ge(s["neg_in"], past((b * NG + i) * 16))
                        ins = dve.tensor_copy(negT[:], bank[:].bitcast(BF16)[0:3 * HG, 0:S])
                    elif kind == "out":
                        view = bank[:].rearrange("p (t h d) -> p t h d", t=CB, h=HG)
                        if self_:
                            chain(dve.reciprocal(rec[:], view[:, :, :, HD]))
                        else:
                            chain(dve.tensor_scalar(rec[:], view[:, :, :, HD], 1e-9, None, ALU.max))
                            chain(dve.reciprocal(rec[:], rec[:]))
                        ins = dve.tensor_tensor(
                            att[:, :, i * HG * HD:(i + 1) * HG * HD].rearrange("p t (h d) -> p t h d", h=HG),
                            view[:, :, :, 0:HD], rec[:].unsqueeze(3).broadcast_to([P, CB, HG, HD]), ALU.mult)
                    elif kind == "y":
                        view = bank[:].rearrange("p (t d) -> p t d", d=D)
                        if self_:
                            ins = dve.tensor_copy(yn[:, 2 * i:2 * i + 2, :], view)
                        else:
                            rr = X[:, bass.ds(b * CB + 2 * i, 2), :]
                            ins = dve.tensor_tensor(rr, rr, view, ALU.add)
                    else:
                        view = bank[:, 0:CB * E].rearrange("p (t e) -> p t e", e=E)
                        chain(dve.tensor_reduce(small[0][:], view, AX.X, ALU.max))
                        ins = dve.tensor_tensor(wide[0][:], view, small[0][:].unsqueeze(2).broadcast_to([P, CB, E]),
                                                ALU.subtract)
                    ins.then_inc(s["free_d"], 1)
                    if kind == "logits":
                        dve.wait_ge(s["free_d"], past(index + 1))
                        dve.nop().then_inc(s["shift_ready"], 1)

                def y_stats(b, index, t):
                    if t == 0:
                        dve.wait_ge(s["free_d"], past(index + 1))
                        alone(dve)
                    ins = dve.bn_stats(stats[:, t, :], yn[:, t, :])
                    if t == CB - 1:
                        chain(ins)
                        for t in range(CB):
                            ins = dve.bn_aggr(ymv[:, t, :], stats[:, t, :])
                        ins.then_inc(s["y_stats"], 1)

                def y_chunk(b, t):
                    if t == 0:
                        dve.wait_ge(s["y_rstd"], past(b + 1))
                        dve.wait_ge(s["y_stats"], past(b + 1))
                        alone(dve)
                    ins = dve.tensor_scalar(yn[:, t, :], yn[:, t, :], ymv[:, t, 0:1], yrstd[:, t:t + 1],
                                            ALU.subtract, ALU.mult)
                    if t == CB - 1:
                        ins.then_inc(s["yn_ready"], 1)

                def router(b):
                    dve.wait_ge(s["rexp_ready"], past(b + 1))
                    chain(dve.tensor_reduce(small[1][:], wide[1][:], AX.X, ALU.add))
                    chain(dve.reciprocal(small[2][:], small[1][:]))
                    chain(dve.tensor_tensor(G["prob"][:, bass.ds(b * CB, CB), :], wide[1][:],
                                            small[2][:].unsqueeze(2).broadcast_to([P, CB, E]), ALU.mult))

                def before():
                    if self_:
                        dve.wait_ge(s["loaded"], past(16 * LOADS))
                    for t in range(CB):
                        norm_chunk(0, t)
                    for t in range(CB):
                        apply_chunk(0, t)
                    for n in range(ROUND):
                        max_step(0, 0, n)
                    for k in range(4):
                        cut_maxima(0, 0, None, k)
                    job(0, "neg0+", 0)
                    for n in range(ROUND):
                        max_step(0, 1, n)
                    for k in range(4):
                        cut_maxima(0, 1, 1, k)

                def batch(b, par):
                    first, last = first_last(b)
                    if not isinstance(b, int):
                        chain.base, chain.n = (b - 1) * VPER + start[0], 0
                    elif last:
                        chain.base, chain.n = start[0] + (B - 2) * VPER, 0
                    for g in range(NG):
                        for n in range(ROUND):
                            if 1 <= n <= 4:
                                if g == 0 and not first:
                                    cut_maxima(b, 1, J.base("d", b), n - 1)
                                elif 0 < g < NG - 1:
                                    cut_maxima(b, g + 1, job_index("d", b, f"neg{g}") + 1, n - 1)
                                elif g and not last:
                                    cut_maxima(b + 1, 0, job_index("d", b, "neg3") + 1, n - 1)
                            if not last and g == 0 and 1 <= n <= CB:
                                norm_chunk(b + 1, n - 1)
                            if not last and g == 0 and 7 <= n < 7 + CB:
                                apply_chunk(b + 1, n - 7)
                            for _, name in jobs_at(b, g, n - 1, "d"):
                                if name == "out0" and not first:
                                    dve.wait_ge(s["job_a"], past(job_index("a", b, "att1-") + 1))
                                job(b + {"+": 1, "-": -1}.get(name[-1], 0), name, job_index("d", b, name))
                            if self_ and not first:
                                if g == 1 and 9 <= n < 9 + CB:
                                    y_stats(b - 1, job_index("d", b, "y1-"), n - 9)
                                if g == 2 and 1 <= n <= CB:
                                    y_chunk(b - 1, n - 1)
                                if (g, n) == (3, 13):
                                    router(b - 1)
                            if g < 2:
                                max_step(b, g + 2, n)
                            elif not last:
                                max_step(b + 1, g - 2, n)
                    if first:
                        start[0] = chain.n
                    elif not last:
                        assert chain.n == VPER, chain.n

                def behind():
                    nd = J.behind("d")
                    for i, name in enumerate(("out3-", "y0-", "y1-")):
                        job(B - 1, name, nd + i)
                    if self_:
                        for t in range(CB):
                            y_stats(B - 1, nd + 2, t)
                        for t in range(CB):
                            y_chunk(B - 1, t)
                        job(B - 1, "logits-", nd + 3)
                        router(B - 1)
                    else:
                        dve.wait_ge(s["free_d"], past(nd + 3))

                start = [0]
                VPER = 3 * NG + (1 if self_ else 2) * NG + 1 + (9 - 4 if self_ else 0)
                run(dve, before, batch, behind)


def top_experts(nc, G):
    with ExitStack() as ctx:
        st = Stage(nc, ctx, "top")
        tiles = TILES["L1"]
        ahead, tie = st.sb("ahead", [P, NC, E, E]), st.sb("tie", [P, NC, E, E])
        rank, chosen, at, got = (st.sb(n, [P, E, NC]) for n in ("rank", "chosen", "at", "got"))
        front, scan, keep = (st.sb(n, [P, E * NC]) for n in ("front", "scan", "keep"))
        full = st.sb("full", [P, E, N // TILE])
        steps, size, first, last = (st.sb(n, [P, w]) for n, w in
                                    (("steps", N // TILE), ("size", E), ("first", E), ("last", E)))
        cross = st.sb("cross", [P, E, E])
        past_end, owner = st.sb("past_end", [1, tiles, E]), st.sb("owner", [1, tiles])
        pin, pall = st.ps("pin", [P, S]), st.ps("pall", [P, S])
        vchain, flagged, counted = (st.sem(n) for n in ("vchain", "flagged", "counted"))
        mine = G["prob"][:].unsqueeze(3).broadcast_to([P, NC, E, E])
        other = G["prob"][:].unsqueeze(2).broadcast_to([P, NC, E, E])

        def to(t, shape, axis):
            return t.unsqueeze(axis).broadcast_to(shape)

        with nc.Block() as block:

            @block.sync
            def _(sp):
                st.set_semaphores(sp)

            @block.tensor
            def _(pe):
                pe.wait_ge(flagged, past(1))
                in_front_pe(pe, G, pin, pall, chosen[:].rearrange("p e c -> p (e c)")).then_inc(counted, 1)

            @block.vector
            def _(dve):
                chain = Chain(dve, vchain)
                chain(dve.memset(keep[:], 1.0))
                chain(dve.memset(keep[:].rearrange("p (e c) -> p e c", c=NC)[:, :, 0:1], 0.0))
                chain(dve.tensor_tensor(ahead[:], other, mine, ALU.is_gt))
                chain(dve.tensor_tensor(tie[:], other, mine, ALU.is_equal))
                chain(dve.tensor_tensor(tie[:], tie[:], to(G["lower"][:], [P, NC, E, E], 1), ALU.mult))
                chain(dve.tensor_tensor(ahead[:], ahead[:], tie[:], ALU.add))
                chain(dve.tensor_reduce(rank[:].rearrange("p e c -> p c e"), ahead[:], AX.X, ALU.add))
                dve.tensor_scalar(chosen[:], rank[:], float(TOPK), None, ALU.is_lt).then_inc(flagged, 1)
                chain(dve.tensor_scalar(steps[:], G["lane"][:, 0:N // TILE], float(TILE), None, ALU.mult))
                dve.wait_ge(counted, past(1))
                in_front_dve(dve, chain, front, scan, keep, pin, pall)
                sizes = scan[:].rearrange("p (e c) -> p e c", c=NC)[:, :, NC - 1]
                chain(dve.tensor_tensor(full[:], to(sizes, [P, E, N // TILE], 2), to(steps[:], [P, E, N // TILE], 1),
                                        ALU.is_gt))
                chain(dve.tensor_reduce(size[:], full[:], AX.X, ALU.add))
                chain(dve.tensor_tensor(cross[:], G["lower"][:], to(size[:], [P, E, E], 1), ALU.mult))
                chain(dve.tensor_reduce(first[:], cross[:], AX.X, ALU.add))
                chain(dve.tensor_tensor(last[:], first[:], size[:], ALU.add))
                chain(dve.tensor_tensor(past_end[:], to(last[0:1, :], [1, tiles, E], 1),
                                        to(G["lane"][0:1, 0:tiles], [1, tiles, E], 2), ALU.is_le))
                chain(dve.tensor_reduce(owner[:], past_end[:], AX.X, ALU.add))
                chain(dve.tensor_scalar(G["owner"][:], owner[:], float(E - 1), None, ALU.min))
                chain(dve.scalar_tensor_tensor(out=at[:], in0=to(first[:], [P, E, NC], 2), scalar=float(TILE),
                                               in1=front[:].rearrange("p (e c) -> p e c", c=NC),
                                               op0=ALU.mult, op1=ALU.add))
                for k in range(TOPK):
                    for dst, src in ((G["place"], at[:]), (G["weight"], G["prob"][:].rearrange("p c e -> p e c"))):
                        chain(dve.scalar_tensor_tensor(out=got[:], in0=rank[:], scalar=float(k), in1=src,
                                                       op0=ALU.is_equal, op1=ALU.mult))
                        chain(dve.tensor_reduce(dst[:, k * NC:(k + 1) * NC], got[:].rearrange("p e c -> p c e"),
                                                AX.X, ALU.add))


def finish(nc, G, a, out):
    with ExitStack() as ctx:
        st = Stage(nc, ctx, "fin")
        stats, mv_b = st.sb("stats", [P, CB, 6]), st.sb("mv_b", [P, CB, 2])
        mv, rstd = st.sb("mv", [P, NC, 2]), st.sb("rstd", [P, NC])
        gain, shift = st.sb("gain", [P, D]), st.sb("shift", [P, D])
        loaded, stats_ready, rstd_ready, shifted, vchain, pchain, ready, stored = (
            st.sem(n) for n in ("loaded", "stats_ready", "rstd_ready", "shifted", "vchain", "pchain", "ready", "stored"))
        X, Y, y_in = G["x"], st.sb("y", [P, NC, D]), [st.sem(f"y_in{i}") for i in range(2)]
        HALF = B // 2

        def batch(t, b):
            return t[:, bass.ds(b * CB, CB), :]

        def wide(t):
            return t[:].unsqueeze(1).broadcast_to([P, CB, D])

        with nc.Block() as block:

            @block.sync
            def _(sp):
                st.set_semaphores(sp)
                sp.dma_start(shift[:], a["L1_ln2_b"].broadcast_to([P, D])).then_inc(loaded, 16)
                sp.dma_start(gain[:], a["L1_ln2_g"].broadcast_to([P, D])).then_inc(loaded, 16)
                for i in range(2):
                    here = slice(i * HALF * CB, (i + 1) * HALF * CB)
                    sp.dma_start(Y[:, here, :], G["sum1"][0:N, :].rearrange("(c p) d -> p c d", p=P)[:, here, :]
                                 ).then_inc(y_in[i], 16)
                with sp.Fori(0, B) as b:
                    sp.wait_ge(ready, past(b + 1))
                    sp.dma_start(batch(out.rearrange("b (c p) d -> p (b c) d", p=P), b), batch(X, b)
                                 ).then_inc(stored, 16)
                sp.wait_ge(stored, past(16 * B))

            @block.gpsimd
            def _(pool):
                pool.wait_ge(loaded, past(32))
                with pool.Fori(0, B) as b:
                    pool.tensor_tensor(batch(X, b), batch(X, b), wide(shift), ALU.add).then_inc(shifted, 1)
                    pool.wait_ge(shifted, past(b + 1))
                    alone(pool)
                pool.wait_ge(stats_ready, past(B))
                Chain(pool, pchain)(pool.tensor_scalar(rstd[:], mv[:, :, 1], EPS, None, ALU.add))
                pool.tensor_tensor(rstd[:], rstd[:], G["mhalf"][:, 0:1].broadcast_to([P, NC]), ALU.pow
                                   ).then_inc(rstd_ready, 1)

            @block.vector
            def _(dve):
                for i in range(2):
                    dve.wait_ge(y_in[i], past(16))
                    with dve.Fori(i * HALF, (i + 1) * HALF) as b:
                        chain = Chain(dve, vchain, b * 2)
                        chain(norm_stats(dve, chain, stats, mv_b, lambda t: Y[:, b * CB + t, :]))
                        dve.tensor_copy(batch(mv, b), mv_b[:]).then_inc(stats_ready, 1)
                dve.wait_ge(loaded, past(32))
                dve.wait_ge(stats_ready, past(B))
                dve.wait_ge(rstd_ready, past(1))
                with dve.Fori(0, B) as b:
                    chain = Chain(dve, vchain, (b + B) * 2)
                    for t in range(CB):
                        c = b * CB + t
                        ins = dve.tensor_scalar(Y[:, c, :], Y[:, c, :], mv[:, bass.ds(c, 1), 0],
                                                rstd[:, bass.ds(c, 1)], ALU.subtract, ALU.mult)
                    chain(ins)
                    chain(dve.tensor_tensor(batch(Y, b), batch(Y, b), wide(gain), ALU.mult))
                    dve.wait_ge(shifted, past(b + 1))
                    dve.tensor_tensor(batch(X, b), batch(X, b), batch(Y, b), ALU.add).then_inc(ready, 1)


def build(nc, a, out):
    with ExitStack() as ctx:
        def sb(name, shape, dt=F32):
            return ctx.enter_context(nc.sbuf_tensor(name, shape, dt))

        def dram(name, shape):
            return nc.dram_tensor(name, shape, F32, kind="Internal").ap()

        G = {
            "x": sb("x", [P, NC, D]),
            "ident": sb("ident", [P, P]), "identb": sb("identb", [P, P], BF16), "before": sb("before", [P, P]),
            "ones": sb("ones", [P, P]), "mhalf": sb("mhalf", [P, CB]), "lower": sb("lower", [P, E, E]),
            "lane": sb("lane", [P, P]), "token1": sb("token1", [P, NC]), "spare1": sb("spare1", [P, 1]),
            "bias": [sb(f"bias{i}", [P, CB, S], BF16) for i in range(2)],
            "ratio": sb("ratio", [P, DC, B]), "prob": sb("prob", [P, NC, E]),
            "place": sb("place", [P, E * NC]), "weight": sb("weight", [P, E * NC]),
            "row": sb("row", [P, COLS], U32), "roww": sb("roww", [P, COLS]),
            "owner": sb("owner", [1, TILES["L1"]], mybir.dt.int32),
            "rows0": dram("rows0", [N + P, D]), "rows1": dram("rows1", [N + P, D]),
            "sum0": dram("sum0", [N + P, D]), "sum1": dram("sum1", [N + P, D]),
        }
        aft_keys(nc, G, a)
        aft_tokens(nc, G, a)
        expert_choice(nc, G)
        lists(nc, G, "L0", E, NC, CAP // P, True)
        experts(nc, G, a, "L0", ACT.Gelu_apprx_tanh)
        attention(nc, G, a, "L1x", False)
        attention(nc, G, a, "L1", True)
        top_experts(nc, G)
        lists(nc, G, "L1", 1, TOPK * NC, COLS, False)
        experts(nc, G, a, "L1", ACT.Gelu)
        finish(nc, G, a, out)


def kernel(**inputs):
    import numpy as np
    import concourse.bacc as bacc
    from concourse.bass_utils import run_bass_kernel_spmd

    i = {k: np.asarray(v) for k, v in inputs.items()}
    mask = i["mask_SxS2_bk0"]

    def columns(v, n):
        return v.reshape(-1, n, P).swapaxes(-1, -2)

    by_row = np.arange(D).reshape(DC, HC, HD).swapaxes(1, 2).reshape(D)
    lay = {
        "x": i["x"], "ctxT": i["ctx_1024"].reshape(N, D).T, "mask": mask, "maskT": mask.T,
        "L0_WqT": i["L0_xattn_Wq"].T, "L0_WkT": i["L0_xattn_Wk"].T, "L0_WvT": i["L0_xattn_Wv"].T,
        "L0_WoT": i["L0_xattn_Wo"].T, "L0_Ws": i["L0_ffn_Ws"], "L0_bs": i["L0_ffn_bs"].reshape(1, E),
        "L1_Wq": i["L1_ffn_Wq"], "L1_Wk": i["L1_ffn_Wk"], "L1_Wv": i["L1_ffn_Wv"], "L1_Wo": i["L1_ffn_Wo"],
        "L1_bq": columns(i["L1_ffn_bq"][by_row], DC)[0], "L1_bk": columns(i["L1_ffn_bk"][by_row], DC)[0],
        "L1_gate_w": i["L1_ffn_gate_w"],
    }
    for n in ("Wq", "Wk", "Wv", "Wo"):
        lay["L1x_" + n] = i["L1_xattn_" + n].T
    for t in ("L1x", "L1"):
        for n in ("Wq", "Wk"):
            lay[f"{t}_{n}"] = lay[f"{t}_{n}"][:, by_row]
    for n in ("bv", "bo", "ln1_g", "ln1_b", "ln2_g", "ln2_b", "gate_b"):
        lay["L1_" + n] = i["L1_ffn_" + n].reshape(1, -1)
    for t in ("L0", "L1"):
        for n in ("W1", "W2", "b2"):
            lay[f"{t}_{n}"] = i[f"{t}_ffn_{n}"]
        lay[f"{t}_b1"] = columns(i[f"{t}_ffn_b1"], FC)

    nc = bacc.Bacc("TRN2", target_bir_lowering=False, num_devices=1)
    arrays, a = {}, {}
    for name, v in lay.items():
        v = np.ascontiguousarray(v)
        arrays["in_" + name] = v
        a[name] = nc.dram_tensor("in_" + name, v.shape, mybir.dt.from_np(v.dtype), kind="ExternalInput").ap()
    out = nc.dram_tensor("out", (B, S, D), F32, kind="ExternalOutput").ap()
    build(nc, a, out)
    r = run_bass_kernel_spmd(nc, [arrays], core_ids=[0])
    return r.results[0]["out"]
```
